# Optimizing a Trainium2 kernel written in Bass

```python
import numpy as np
import jax
import jax.numpy as jnp

def _softmax(x, axis=-1):
    return jax.nn.softmax(x, axis=axis)

def _gelu(x):
    return jax.nn.gelu(x, approximate=True)

def _silu(x):
    return jax.nn.silu(x)

def _sigmoid(x):
    return jax.nn.sigmoid(x)

def _layernorm(x, axis=-1, eps=1e-05):
    m = jnp.mean(x, axis=axis, keepdims=True)
    v = jnp.var(x, axis=axis, keepdims=True)
    return (x - m) / jnp.sqrt(v + eps)

def _scatter_add(tgt, idx, src, axis=0):
    return tgt.at[idx].add(src)

def _segment_sum(src, seg, n):
    return jax.ops.segment_sum(src, seg, n)
kernel_name = 'mk_conv_preact_d4_conv_nchw128_r2_915550'

def setup_inputs(seed: int=0):
    np.random.seed(seed)
    _w = jnp.asarray

    def _rec_inputs():
        import jax
        import jax.numpy as jnp
        _gk = jax.random.key(seed)
        x = -7.109e-05 + 0.9999 * jax.random.normal(jax.random.fold_in(_gk, 1), (4, 64, 128, 128), jnp.float32)
        return x
    x = _rec_inputs()

    def _L0_conv_setup():
        import jax, jax.numpy as jnp
        import numpy as np
        PH, PW = (8, 8)
        HEADS = 8
        EPS = 1e-06
        N_ITER = 1
        SHIFTS = [(dh, dw) for dh in (-1, 0, 1) for dw in (-1, 0, 1)]

        def unfold3(x):
            B, C, H, W = x.shape
            xp = jnp.pad(x, ((0, 0), (0, 0), (1, 1), (1, 1)))
            return jnp.stack([xp[:, :, 1 + dh:1 + dh + H, 1 + dw:1 + dw + W] for dh, dw in SHIFTS], axis=2)

        def fold3(y):
            H, W = (y.shape[-2], y.shape[-1])
            pad = [(0, 0)] * (y.ndim - 2) + [(1, 1), (1, 1)]
            yp = jnp.pad(y, pad)
            out = jnp.zeros(y.shape[:-3] + (H, W), y.dtype)
            for i, (dh, dw) in enumerate(SHIFTS):
                out = out + yp[..., i, 1 - dh:1 - dh + H, 1 - dw:1 - dw + W]
            return out

        def layernorm_cf(x, w, b):
            mu = x.mean(1, keepdims=True)
            var = ((x - mu) ** 2).mean(1, keepdims=True)
            return w[None, :, None, None] * (x - mu) / jnp.sqrt(var + EPS) + b[None, :, None, None]

        def mha_bchw(x, qkv_w, proj_w, proj_b):
            B, C, H, W = x.shape
            hd = C // HEADS
            t = x.reshape(B, C, H * W).transpose(0, 2, 1)
            qkv = (t @ qkv_w.T).reshape(B, H * W, 3, HEADS, hd).transpose(2, 0, 3, 1, 4)
            q, k, v = (qkv[0], qkv[1], qkv[2])
            attn = jax.nn.softmax(jnp.einsum('bhnd,bhmd->bhnm', q, k) * hd ** (-0.5), axis=-1)
            o = jnp.einsum('bhnm,bhmd->bhnd', attn, v).transpose(0, 2, 1, 3).reshape(B, H * W, C)
            o = o @ proj_w.T + proj_b
            return o.transpose(0, 2, 1).reshape(B, C, H, W)
        key = jax.random.key(seed)
        k1, k2, k3 = jax.random.split(key, 3)
        C = 64
        return {'x': jax.random.normal(k1, (8, C, 128, 128), dtype=jnp.float32), 'ln_w': jnp.ones((C,), jnp.float32), 'ln_b': jnp.zeros((C,), jnp.float32), 'qkv_w': jax.random.normal(k2, (3 * C, C), dtype=jnp.float32) * 0.02, 'proj_w': jax.random.normal(k3, (C, C), dtype=jnp.float32) * 0.02, 'proj_b': jnp.zeros((C,), jnp.float32)}
    _L0_conv_all = _L0_conv_setup()
    _L0_conv_in = {k: v for k, v in _L0_conv_all.items() if k in ('ln_w', 'ln_b', 'qkv_w', 'proj_w', 'proj_b')}
    del _L0_conv_all

    def _L1_conv_setup():
        import jax, jax.numpy as jnp
        import numpy as np
        from jax import lax
        NUM_EXPERTS = 4
        GROUPS = 16
        SPATIAL = GROUPS
        STRIDE = 1
        PAD = 1

        def _routing(x, conv_w, conv_b, fc_w, fc_b):
            b, c, h, w = x.shape
            s = SPATIAL
            p = x.reshape(b, c, s, h // s, s, w // s).mean(axis=(3, 5))
            r = jax.nn.relu(jnp.einsum('bcij,oc->boij', p, conv_w[:, :, 0, 0]) + conv_b[None, :, None, None])
            r = r.reshape(b, -1)
            r = jax.nn.relu(r @ fc_w.T + fc_b)
            return jax.nn.sigmoid(r.reshape(b, NUM_EXPERTS, c))
        key = jax.random.key(seed)
        ks = jax.random.split(key, 6)
        b, c, h, w = (32, 64, 32, 32)
        c_in = c // GROUPS
        red = max(c // 16, 16)
        fc_in = red * SPATIAL * SPATIAL
        fc_out = NUM_EXPERTS * c
        return {'x': jax.random.normal(ks[0], (b, c, h, w), jnp.float32), 'w_experts': jax.random.normal(ks[1], (NUM_EXPERTS, c, c_in, 3, 3), jnp.float32) * 0.1, 'conv_w': jax.random.normal(ks[2], (red, c, 1, 1), jnp.float32) * 0.1, 'conv_b': jax.random.normal(ks[3], (red,), jnp.float32) * 0.1, 'fc_w': jax.random.normal(ks[4], (fc_out, fc_in), jnp.float32) * 0.02, 'fc_b': jax.random.normal(ks[5], (fc_out,), jnp.float32) * 0.02}
    _L1_conv_all = _L1_conv_setup()
    _L1_conv_in = {k: v for k, v in _L1_conv_all.items() if k in ('w_experts', 'conv_w', 'conv_b', 'fc_w', 'fc_b')}
    del _L1_conv_all

    def _L2_conv_setup():
        import jax, jax.numpy as jnp
        import numpy as np
        B, D_MODEL, H, W = (4, 64, 64, 64)
        HEAD_DIM = 16
        GROUP = D_MODEL // HEAD_DIM
        D_INNER = D_MODEL
        D_STATE = 1
        DT_RANK = 8
        D_CONV = 3
        EPS = 1e-06

        def _layer_norm(x, g, b):
            m = x.mean(-1, keepdims=True)
            v = ((x - m) ** 2).mean(-1, keepdims=True)
            return (x - m) * jax.lax.rsqrt(v + EPS) * g + b

        def _dwconv(x, w, b):
            out = jax.lax.conv_general_dilated(x, w, (1, 1), 'SAME', feature_group_count=x.shape[1], dimension_numbers=('NCHW', 'OIHW', 'NCHW'))
            return out + b[None, :, None, None]

        def _dcn_sample(img_last, offset):
            b, h, w, c = img_last.shape
            gc = c // GROUP
            img = img_last.reshape(b, h, w, GROUP, gc)
            off = offset.reshape(b, h, w, GROUP, 2)
            px = jnp.arange(w, dtype=offset.dtype)[None, None, :, None] + off[..., 0]
            py = jnp.arange(h, dtype=offset.dtype)[None, :, None, None] + off[..., 1]
            y0 = jnp.floor(py)
            x0 = jnp.floor(px)
            wy = py - y0
            wx = px - x0
            bi = jnp.arange(b)[:, None, None, None]
            gi = jnp.arange(GROUP)[None, None, None, :]

            def tap(yi, xi, wgt):
                valid = (yi >= 0) & (yi < h) & (xi >= 0) & (xi < w)
                yc = jnp.clip(yi, 0, h - 1).astype(jnp.int32)
                xc = jnp.clip(xi, 0, w - 1).astype(jnp.int32)
                v = img[bi, yc, xc, gi]
                return v * (wgt * valid)[..., None]
            out = tap(y0, x0, (1 - wy) * (1 - wx)) + tap(y0, x0 + 1, (1 - wy) * wx) + tap(y0 + 1, x0, wy * (1 - wx)) + tap(y0 + 1, x0 + 1, wy * wx)
            return out.reshape(b, h, w, c)

        def _selective_scan(xs, dts, A, Bs, Cs, Ds, dt_bias):
            delta = jax.nn.softplus(dts + dt_bias[None, :, None])
            dA = jnp.exp(jnp.einsum('bdl,dn->lbdn', delta, A))
            dBx = jnp.einsum('bdl,bnl,bdl->lbdn', delta, Bs, xs)
            C_t = jnp.transpose(Cs, (2, 0, 1))

            def step(hc, inputs):
                dA_t, dBx_t, c = inputs
                hc = dA_t * hc + dBx_t
                return (hc, jnp.einsum('bdn,bn->bd', hc, c))
            h0 = jnp.zeros(dA.shape[1:], xs.dtype)
            _, ys = jax.lax.scan(step, h0, (dA, dBx, C_t))
            y = jnp.transpose(ys, (1, 2, 0))
            return y + Ds[None, :, None] * xs
        key = jax.random.key(seed)
        ks = jax.random.split(key, 10)
        f = jnp.float32
        dt = jnp.exp(jax.random.uniform(ks[7], (D_INNER,), f) * (np.log(0.1) - np.log(0.001)) + np.log(0.001))
        dt = jnp.clip(dt, 0.0001)
        dt_b = dt + jnp.log(-jnp.expm1(-dt))
        s = DT_RANK ** (-0.5)
        return dict(x=jax.random.normal(ks[0], (B, D_MODEL, H, W), f), in_proj_w=jax.random.normal(ks[1], (D_INNER, D_MODEL), f) * D_MODEL ** (-0.5), conv2d_w=jax.random.normal(ks[2], (D_INNER, 1, D_CONV, D_CONV), f) * 0.1, conv2d_b=jnp.zeros((D_INNER,), f), dw_w=jax.random.normal(ks[3], (D_INNER, 1, 3, 3), f) * 0.1, dw_b=jnp.zeros((D_INNER,), f), dw_ln_g=jnp.ones((D_INNER,), f), dw_ln_b=jnp.zeros((D_INNER,), f), off_w=jax.random.normal(ks[4], (GROUP * 2, D_INNER), f) * 0.01, off_b=jnp.zeros((GROUP * 2,), f), x_proj_w=jax.random.normal(ks[5], (DT_RANK + 2 * D_STATE, D_INNER), f) * D_INNER ** (-0.5), dt_w=jax.random.uniform(ks[6], (D_INNER, DT_RANK), f, -s, s), dt_b=dt_b, A_logs=jnp.tile(jnp.log(jnp.arange(1, D_STATE + 1, dtype=f))[None, :], (D_INNER, 1)), Ds=jnp.ones((D_INNER,), f), out_ln_g=jnp.ones((D_INNER,), f), out_ln_b=jnp.zeros((D_INNER,), f), out_proj_w=jax.random.normal(ks[8], (D_MODEL, D_INNER), f) * D_INNER ** (-0.5))
    _L2_conv_all = _L2_conv_setup()
    _L2_conv_in = {k: v for k, v in _L2_conv_all.items() if k in ('in_proj_w', 'conv2d_w', 'conv2d_b', 'dw_w', 'dw_b', 'dw_ln_g', 'dw_ln_b', 'off_w', 'off_b', 'x_proj_w', 'dt_w', 'dt_b', 'A_logs', 'Ds', 'out_ln_g', 'out_ln_b', 'out_proj_w')}
    del _L2_conv_all

    def _L3_conv_setup():
        import jax, jax.numpy as jnp
        import numpy as np
        key = jax.random.key(seed)
        k1, k2, k3, k4 = jax.random.split(key, 4)
        B, I, O, H, W, p = (16, 64, 64, 64, 64, 4)
        x = jax.random.normal(k1, (B, I, H, W), dtype=jnp.float32)
        w3 = jax.random.normal(k2, (O, I, 3, 3), dtype=jnp.float32) * 0.05
        w1 = jax.random.normal(k3, (O, I), dtype=jnp.float32) * 0.05
        b = jax.random.normal(k4, (O, I), dtype=jnp.float32) * 0.05
        return {'x': x, 'w3': w3, 'w1': w1, 'b': b, 'p': p}
    _L3_conv_all = _L3_conv_setup()
    _L3_conv_in = {k: v for k, v in _L3_conv_all.items() if k in ('w3', 'w1', 'b')}
    del _L3_conv_all
    return {'x': x, 'L0_conv_ln_w': _L0_conv_in['ln_w'], 'L0_conv_ln_b': _L0_conv_in['ln_b'], 'L0_conv_qkv_w': _L0_conv_in['qkv_w'], 'L0_conv_proj_w': _L0_conv_in['proj_w'], 'L0_conv_proj_b': _L0_conv_in['proj_b'], 'L1_conv_w_experts': _L1_conv_in['w_experts'], 'L1_conv_conv_w': _L1_conv_in['conv_w'], 'L1_conv_conv_b': _L1_conv_in['conv_b'], 'L1_conv_fc_w': _L1_conv_in['fc_w'], 'L1_conv_fc_b': _L1_conv_in['fc_b'], 'L2_conv_in_proj_w': _L2_conv_in['in_proj_w'], 'L2_conv_conv2d_w': _L2_conv_in['conv2d_w'], 'L2_conv_conv2d_b': _L2_conv_in['conv2d_b'], 'L2_conv_dw_w': _L2_conv_in['dw_w'], 'L2_conv_dw_b': _L2_conv_in['dw_b'], 'L2_conv_dw_ln_g': _L2_conv_in['dw_ln_g'], 'L2_conv_dw_ln_b': _L2_conv_in['dw_ln_b'], 'L2_conv_off_w': _L2_conv_in['off_w'], 'L2_conv_off_b': _L2_conv_in['off_b'], 'L2_conv_x_proj_w': _L2_conv_in['x_proj_w'], 'L2_conv_dt_w': _L2_conv_in['dt_w'], 'L2_conv_dt_b': _L2_conv_in['dt_b'], 'L2_conv_A_logs': _L2_conv_in['A_logs'], 'L2_conv_Ds': _L2_conv_in['Ds'], 'L2_conv_out_ln_g': _L2_conv_in['out_ln_g'], 'L2_conv_out_ln_b': _L2_conv_in['out_ln_b'], 'L2_conv_out_proj_w': _L2_conv_in['out_proj_w'], 'L3_conv_w3': _L3_conv_in['w3'], 'L3_conv_w1': _L3_conv_in['w1'], 'L3_conv_b': _L3_conv_in['b']}

def reference(x, L0_conv_ln_w, L0_conv_ln_b, L0_conv_qkv_w, L0_conv_proj_w, L0_conv_proj_b, L1_conv_w_experts, L1_conv_conv_w, L1_conv_conv_b, L1_conv_fc_w, L1_conv_fc_b, L2_conv_in_proj_w, L2_conv_conv2d_w, L2_conv_conv2d_b, L2_conv_dw_w, L2_conv_dw_b, L2_conv_dw_ln_g, L2_conv_dw_ln_b, L2_conv_off_w, L2_conv_off_b, L2_conv_x_proj_w, L2_conv_dt_w, L2_conv_dt_b, L2_conv_A_logs, L2_conv_Ds, L2_conv_out_ln_g, L2_conv_out_ln_b, L2_conv_out_proj_w, L3_conv_w3, L3_conv_w1, L3_conv_b):
    import jax
    import jax.numpy as jnp

    def _L0_conv_ref(x, ln_w, ln_b, qkv_w, proj_w, proj_b):
        import jax, jax.numpy as jnp
        import numpy as np
        PH, PW = (8, 8)
        HEADS = 8
        EPS = 1e-06
        N_ITER = 1
        SHIFTS = [(dh, dw) for dh in (-1, 0, 1) for dw in (-1, 0, 1)]

        def unfold3(x):
            B, C, H, W = x.shape
            xp = jnp.pad(x, ((0, 0), (0, 0), (1, 1), (1, 1)))
            return jnp.stack([xp[:, :, 1 + dh:1 + dh + H, 1 + dw:1 + dw + W] for dh, dw in SHIFTS], axis=2)

        def fold3(y):
            H, W = (y.shape[-2], y.shape[-1])
            pad = [(0, 0)] * (y.ndim - 2) + [(1, 1), (1, 1)]
            yp = jnp.pad(y, pad)
            out = jnp.zeros(y.shape[:-3] + (H, W), y.dtype)
            for i, (dh, dw) in enumerate(SHIFTS):
                out = out + yp[..., i, 1 - dh:1 - dh + H, 1 - dw:1 - dw + W]
            return out

        def layernorm_cf(x, w, b):
            mu = x.mean(1, keepdims=True)
            var = ((x - mu) ** 2).mean(1, keepdims=True)
            return w[None, :, None, None] * (x - mu) / jnp.sqrt(var + EPS) + b[None, :, None, None]

        def mha_bchw(x, qkv_w, proj_w, proj_b):
            B, C, H, W = x.shape
            hd = C // HEADS
            t = x.reshape(B, C, H * W).transpose(0, 2, 1)
            qkv = (t @ qkv_w.T).reshape(B, H * W, 3, HEADS, hd).transpose(2, 0, 3, 1, 4)
            q, k, v = (qkv[0], qkv[1], qkv[2])
            attn = jax.nn.softmax(jnp.einsum('bhnd,bhmd->bhnm', q, k) * hd ** (-0.5), axis=-1)
            o = jnp.einsum('bhnm,bhmd->bhnd', attn, v).transpose(0, 2, 1, 3).reshape(B, H * W, C)
            o = o @ proj_w.T + proj_b
            return o.transpose(0, 2, 1).reshape(B, C, H, W)
        x = layernorm_cf(x, ln_w, ln_b)
        B, C, H, W = x.shape
        Hs, Ws = (H // PH, W // PW)
        N = Hs * Ws
        scale = C ** (-0.5)
        xb = x.reshape(B, C, Hs, PH, Ws, PW)
        stoken = xb.mean(axis=(3, 5))
        pix = xb.transpose(0, 2, 4, 3, 5, 1).reshape(B, N, PH * PW, C)

        def unfold_tok(sf):
            u = unfold3(sf)
            return u.transpose(0, 3, 4, 1, 2).reshape(B, N, C, 9)
        sf = stoken
        aff = None
        aff_sum = None
        for idx in range(N_ITER):
            st = unfold_tok(sf)
            aff = jax.nn.softmax(jnp.einsum('bnpc,bnck->bnpk', pix, st) * scale, axis=-1)
            aff_sum = fold3(aff.sum(2).transpose(0, 2, 1).reshape(B, 9, Hs, Ws))[:, None]
            if idx < N_ITER - 1:
                sf = jnp.einsum('bnpc,bnpk->bnck', pix, aff).transpose(0, 2, 3, 1).reshape(B, C, 9, Hs, Ws)
                sf = fold3(sf) / (aff_sum + 1e-12)
        aff = jax.lax.stop_gradient(aff)
        aff_sum = jax.lax.stop_gradient(aff_sum)
        sf = jnp.einsum('bnpc,bnpk->bnck', pix, aff).transpose(0, 2, 3, 1).reshape(B, C, 9, Hs, Ws)
        sf = fold3(sf) / (aff_sum + 1e-12)
        sf = mha_bchw(sf, qkv_w, proj_w, proj_b)
        st = unfold_tok(sf)
        out = jnp.einsum('bnck,bnpk->bncp', st, aff)
        out = out.reshape(B, Hs, Ws, C, PH, PW).transpose(0, 3, 1, 4, 2, 5).reshape(B, C, H, W)
        return out

    def _L1_conv_ref(x, w_experts, conv_w, conv_b, fc_w, fc_b):
        import jax, jax.numpy as jnp
        import numpy as np
        from jax import lax
        NUM_EXPERTS = 4
        GROUPS = 16
        SPATIAL = GROUPS
        STRIDE = 1
        PAD = 1

        def _routing(x, conv_w, conv_b, fc_w, fc_b):
            b, c, h, w = x.shape
            s = SPATIAL
            p = x.reshape(b, c, s, h // s, s, w // s).mean(axis=(3, 5))
            r = jax.nn.relu(jnp.einsum('bcij,oc->boij', p, conv_w[:, :, 0, 0]) + conv_b[None, :, None, None])
            r = r.reshape(b, -1)
            r = jax.nn.relu(r @ fc_w.T + fc_b)
            return jax.nn.sigmoid(r.reshape(b, NUM_EXPERTS, c))
        b, c, h, w = x.shape
        rw = _routing(x, conv_w, conv_b, fc_w, fc_b)
        cw = jnp.einsum('beo,eoikl->boikl', rw, w_experts)

        def conv_one(xi, wi):
            return lax.conv_general_dilated(xi[None], wi, (STRIDE, STRIDE), [(PAD, PAD), (PAD, PAD)], feature_group_count=GROUPS, dimension_numbers=('NCHW', 'OIHW', 'NCHW'))[0]
        return jax.vmap(conv_one)(x, cw)

    def _L2_conv_ref(x, in_proj_w, conv2d_w, conv2d_b, dw_w, dw_b, dw_ln_g, dw_ln_b, off_w, off_b, x_proj_w, dt_w, dt_b, A_logs, Ds, out_ln_g, out_ln_b, out_proj_w):
        import jax, jax.numpy as jnp
        import numpy as np
        B, D_MODEL, H, W = (4, 64, 64, 64)
        HEAD_DIM = 16
        GROUP = D_MODEL // HEAD_DIM
        D_INNER = D_MODEL
        D_STATE = 1
        DT_RANK = 8
        D_CONV = 3
        EPS = 1e-06

        def _layer_norm(x, g, b):
            m = x.mean(-1, keepdims=True)
            v = ((x - m) ** 2).mean(-1, keepdims=True)
            return (x - m) * jax.lax.rsqrt(v + EPS) * g + b

        def _dwconv(x, w, b):
            out = jax.lax.conv_general_dilated(x, w, (1, 1), 'SAME', feature_group_count=x.shape[1], dimension_numbers=('NCHW', 'OIHW', 'NCHW'))
            return out + b[None, :, None, None]

        def _dcn_sample(img_last, offset):
            b, h, w, c = img_last.shape
            gc = c // GROUP
            img = img_last.reshape(b, h, w, GROUP, gc)
            off = offset.reshape(b, h, w, GROUP, 2)
            px = jnp.arange(w, dtype=offset.dtype)[None, None, :, None] + off[..., 0]
            py = jnp.arange(h, dtype=offset.dtype)[None, :, None, None] + off[..., 1]
            y0 = jnp.floor(py)
            x0 = jnp.floor(px)
            wy = py - y0
            wx = px - x0
            bi = jnp.arange(b)[:, None, None, None]
            gi = jnp.arange(GROUP)[None, None, None, :]

            def tap(yi, xi, wgt):
                valid = (yi >= 0) & (yi < h) & (xi >= 0) & (xi < w)
                yc = jnp.clip(yi, 0, h - 1).astype(jnp.int32)
                xc = jnp.clip(xi, 0, w - 1).astype(jnp.int32)
                v = img[bi, yc, xc, gi]
                return v * (wgt * valid)[..., None]
            out = tap(y0, x0, (1 - wy) * (1 - wx)) + tap(y0, x0 + 1, (1 - wy) * wx) + tap(y0 + 1, x0, wy * (1 - wx)) + tap(y0 + 1, x0 + 1, wy * wx)
            return out.reshape(b, h, w, c)

        def _selective_scan(xs, dts, A, Bs, Cs, Ds, dt_bias):
            delta = jax.nn.softplus(dts + dt_bias[None, :, None])
            dA = jnp.exp(jnp.einsum('bdl,dn->lbdn', delta, A))
            dBx = jnp.einsum('bdl,bnl,bdl->lbdn', delta, Bs, xs)
            C_t = jnp.transpose(Cs, (2, 0, 1))

            def step(hc, inputs):
                dA_t, dBx_t, c = inputs
                hc = dA_t * hc + dBx_t
                return (hc, jnp.einsum('bdn,bn->bd', hc, c))
            h0 = jnp.zeros(dA.shape[1:], xs.dtype)
            _, ys = jax.lax.scan(step, h0, (dA, dBx, C_t))
            y = jnp.transpose(ys, (1, 2, 0))
            return y + Ds[None, :, None] * xs
        xin = jnp.einsum('bchw,oc->bohw', x, in_proj_w)
        xc = jax.nn.silu(_dwconv(xin, conv2d_w, conv2d_b))
        x1 = _dwconv(xc, dw_w, dw_b)
        x1 = jax.nn.gelu(_layer_norm(jnp.transpose(x1, (0, 2, 3, 1)), dw_ln_g, dw_ln_b), approximate=False)
        offset = x1 @ off_w.T + off_b
        xd = _dcn_sample(jnp.transpose(xc, (0, 2, 3, 1)), offset)
        xd = jnp.transpose(xd, (0, 3, 1, 2))
        Bn, C, Hh, Ww = xd.shape
        L = Hh * Ww
        xs = xd.reshape(Bn, C, L)
        x_dbl = jnp.einsum('rc,bcl->brl', x_proj_w, xs)
        dts, Bs, Cs = jnp.split(x_dbl, [DT_RANK, DT_RANK + D_STATE], axis=1)
        dts = jnp.einsum('dr,brl->bdl', dt_w, dts)
        A = -jnp.exp(A_logs)
        y = _selective_scan(xs, dts, A, Bs, Cs, Ds, dt_b).reshape(Bn, C, Hh, Ww)
        y = jnp.transpose(_layer_norm(jnp.transpose(y, (0, 2, 3, 1)), out_ln_g, out_ln_b), (0, 3, 1, 2))
        return jnp.einsum('bchw,oc->bohw', y, out_proj_w)

    def _L3_conv_ref(x, w3, w1, b, p):
        import jax, jax.numpy as jnp
        import numpy as np
        O, I = (w3.shape[0], w3.shape[1])
        i = jnp.arange(O)[:, None]
        j = jnp.arange(I)[None, :]
        m3 = (j - i) % p == 0
        w3m = w3 * m3[:, :, None, None].astype(w3.dtype)
        out = jax.lax.conv_general_dilated(x, w3m, window_strides=(1, 1), padding=((1, 1), (1, 1)), dimension_numbers=('NCHW', 'OIHW', 'NCHW'))
        w1m = w1 * (~m3).astype(w1.dtype)
        out = out + jnp.einsum('oi,bihw->bohw', w1m, x)
        out = out + b.sum(axis=1)[None, :, None, None]
        return out

    def _gn(v, G=32, eps=1e-05):
        B_, C_, H_, W_ = v.shape
        g = v.reshape(B_, G, C_ // G, H_, W_)
        m = jnp.mean(g, axis=(2, 3, 4), keepdims=True)
        s = jnp.var(g, axis=(2, 3, 4), keepdims=True)
        return ((g - m) / jnp.sqrt(s + eps)).reshape(v.shape)

    def _ln_c(v, eps=1e-06):
        m = jnp.mean(v, axis=1, keepdims=True)
        s = jnp.var(v, axis=1, keepdims=True)
        return (v - m) / jnp.sqrt(s + eps)

    def _ln_t(v, eps=1e-05):
        m = jnp.mean(v, axis=-1, keepdims=True)
        s = jnp.var(v, axis=-1, keepdims=True)
        return (v - m) / jnp.sqrt(s + eps)

    def _to_tokens(v):
        B_, C_, H_, W_ = v.shape
        return v.reshape(B_, C_, H_ * W_).transpose(0, 2, 1)

    def _from_tokens(t, like):
        B_, C_, H_, W_ = like.shape
        return t.transpose(0, 2, 1).reshape(B_, C_, H_, W_)
    x = x + _L0_conv_ref(_gn(x), L0_conv_ln_w, L0_conv_ln_b, L0_conv_qkv_w, L0_conv_proj_w, L0_conv_proj_b)
    x = x + _L1_conv_ref(_gn(x), L1_conv_w_experts, L1_conv_conv_w, L1_conv_conv_b, L1_conv_fc_w, L1_conv_fc_b)
    x = x + _L2_conv_ref(_gn(x), L2_conv_in_proj_w, L2_conv_conv2d_w, L2_conv_conv2d_b, L2_conv_dw_w, L2_conv_dw_b, L2_conv_dw_ln_g, L2_conv_dw_ln_b, L2_conv_off_w, L2_conv_off_b, L2_conv_x_proj_w, L2_conv_dt_w, L2_conv_dt_b, L2_conv_A_logs, L2_conv_Ds, L2_conv_out_ln_g, L2_conv_out_ln_b, L2_conv_out_proj_w)
    x = x + _L3_conv_ref(_gn(x), L3_conv_w3, L3_conv_w1, L3_conv_b, 4)
    return x

_drawn_inputs = setup_inputs


def setup_inputs(seed=0):
    import zlib

    import numpy as np

    out = dict(_drawn_inputs(seed))
    spreads = {'L0_conv_ln_w': (1.0, 0.6),
     'L0_conv_ln_b': (0.0, 0.8),
     'L0_conv_proj_b': (0.0, 0.1),
     'L2_conv_conv2d_b': (0.0, 0.1),
     'L2_conv_dw_b': (0.0, 0.1),
     'L2_conv_dw_ln_g': (1.0, 0.6),
     'L2_conv_dw_ln_b': (0.0, 0.8),
     'L2_conv_off_b': (0.0, 0.1),
     'L2_conv_A_logs': (0.0, 0.8),
     'L2_conv_Ds': (1.0, 0.2),
     'L2_conv_out_ln_g': (1.0, 0.2),
     'L2_conv_out_ln_b': (0.0, 0.1)}
    factors = {'L0_conv_qkv_w': 8.0,
     'L0_conv_proj_w': 8.0,
     'L1_conv_conv_w': 3.655,
     'L1_conv_conv_b': 3.219,
     'L1_conv_fc_b': 31.914,
     'L2_conv_x_proj_w': 8.0,
     'L2_conv_dt_w': 8.0,
     'L2_conv_dt_b': 8.0}
    for name, (base, spread) in spreads.items():
        noise = np.random.default_rng([zlib.crc32(name.encode()), seed]).standard_normal(out[name].shape)
        drawn = base * np.exp(spread * noise) if base else spread * noise
        out[name] = jnp.asarray(drawn.astype(out[name].dtype))
    for name, factor in factors.items():
        out[name] = (out[name] * factor).astype(out[name].dtype)
    return out
```

```python
from contextlib import ExitStack

import concourse.bass as bass
from concourse import mybir

F32 = mybir.dt.float32
I32 = mybir.dt.int32
ALU = mybir.AluOpType
ACT = mybir.ActivationFunctionType
AX = mybir.AxisListType

BATCH, C, H, W = 4, 64, 128, 128
P = 2 * C
PAIRS = BATCH // 2
PIX = H * W
ROWS = 4
CH = ROWS * W
NT = H // ROWS
NS = H // 8
TW = NS + 2
TOK = NS * NS
HEADS, HD = 8, 8
NH = 2 * HEADS
GROUP = 4
SG = 2 * GROUP
EXPERTS, RED, FC = 4, 16, 256
DT_RANK = 8
PW = W + 2
BASE = 5
XBASE = 1
PROWS = H + BASE + 1
GN_EPS, LN_EPS = 1e-5, 1e-6
MAXR = 128
TAPS = [(dy, dx) for dy in (-1, 0, 1) for dx in (-1, 0, 1)]

VEC = {}
_at = 0
for _name, _n in (("ln_w", 1), ("ln_b", 1), ("proj_b", 1), ("conv2d_b", 1), ("dw_b", 1), ("dw_ln_g", 1),
                  ("dw_ln_b", 1), ("dt_b", 1), ("A_logs", 1), ("Ds", 1), ("out_ln_g", 1), ("out_ln_b", 1),
                  ("fc_b", EXPERTS), ("conv2d_w", 9), ("dw_w", 9), ("experts", EXPERTS * 36), ("l3_b", C)):
    VEC[_name] = (_at, _n)
    _at += _n
NVEC = _at
MAT = {}
_at = 0
for _name, _n in (("q", C), ("k", C), ("v", C), ("proj", C), ("in_proj", C), ("off", 2 * GROUP), ("out_proj", C),
                  ("conv", RED), ("x_proj", DT_RANK + 2), ("w1", C), ("w3", 9 * C)):
    MAT[_name] = (_at, _n)
    _at += _n
NMAT = _at
CST = {}
_at = 0
for _name, _n in (("ident", P), ("center", P), ("mean", P), ("pair", P), ("one", P), ("zero", P), ("group4", P),
                  ("mask3", P), ("same", P), ("headcol", NH), ("headrow", 2 * P - HD), ("shift", 3), ("col", 1), ("row", H)):
    CST[_name] = (_at, _n)
    _at += _n
NCST = _at

NREG = 11000
CREDIT = 2


def after(t):
    return t + 1 + CREDIT


def reuse(t):
    return t - 1 + CREDIT


def program(nc, x, vec, mat, dts, rows, fc, sel, cst, out):
    ctx = ExitStack()
    with ctx:
        def sb(name, shape, dt=F32):
            return ctx.enter_context(nc.sbuf_tensor(name, shape, dt))

        def sem(name):
            return ctx.enter_context(nc.semaphore(name))

        X = sb("X", [P, H, W])
        PAD = sb("PAD", [P, PROWS, PW])
        VECS = sb("VECS", [P, NVEC])
        DTS = sb("DTS", [DT_RANK, 3 * C])
        ROWV = sb("ROWV", [P, 2 * RED + 4 * 16])
        CSTS = sb("CSTS", [P, NCST])
        WQ, WK, WV, WPROJ, WIN, WOUT, WZ, WB, WC = (sb(n, [P, P]) for n in
            ("WQ", "WK", "WV", "WPROJ", "WIN", "WOUT", "WZ", "WB", "WC"))
        WOUT2, GNE = sb("WOUT2", [P, P]), sb("GNE", [P, 2])
        WOFF = sb("WOFF", [P, 2, 2, GROUP])
        WCONV = sb("WCONV", [P, 2, RED])
        WDW1 = sb("WDW1", [P, 9, P])
        WDW2 = sb("WDW2", [P, 9, P])
        WL3 = sb("WL3", [P, 9, P])
        WL1 = sb("WL1", [P, 9, P])
        STATS = sb("STATS", [P, NT, 6])
        SM = sb("SM", [P, 64])
        OUTB = sb("OUTB", [P, 1])
        RI = sb("RI", [P, 1], I32)
        REG = sb("REG", [P, NREG])
        MATS = REG[:, 0:NMAT]
        PLAIN, NOT3 = (REG[:, NMAT + j * P:NMAT + (j + 1) * P] for j in range(2))

        def cs(name):
            a, n = CST[name]
            return CSTS[:, a:a + n]

        def vc(name, j=0, n=1):
            a = VEC[name][0] + j
            return VECS[:, a:a + n]

        def mt(name, lo=0, hi=P):
            a, n = MAT[name]
            return MATS[lo:hi, a:a + n]

        ident = cs("ident")
        PSUM = ctx.enter_context(nc.psum_tensor("PSUM", [P, 8, 512], F32))

        class Region:
            def __init__(self):
                self.at = 0

            def take(self, *shape):
                n = 1
                for d in shape:
                    n *= d
                a = REG[:, self.at:self.at + n]
                self.at += n
                assert self.at <= NREG, self.at
                if len(shape) == 2:
                    a = a.rearrange("p (a b) -> p a b", a=shape[0])
                if len(shape) == 3:
                    a = a.rearrange("p (a b c) -> p a b c", a=shape[0], b=shape[1])
                if len(shape) == 4:
                    a = a.rearrange("p (a b c d) -> p a b c d", a=shape[0], b=shape[1], c=shape[2])
                return a

        r = Region()
        n_xn, n_sq, n_rs, n_y = (r.take(2, CH) for _ in range(4))
        r = Region()
        AFF = r.take(NS, NS, 9)
        EXPD = r.take(2, 8, 2 * C)
        SFAS = r.take(2, TW * TW)
        STB = r.take(TW, 2, TW)
        both = r.at
        STG = r.take(2, 1024)
        PIXT = r.take(2, 1024)
        LG = r.take(2, NS, 9)
        SMX = r.take(2, 3, NS)
        r.at = both
        SFC, QB, KB, OB = (r.take(TOK) for _ in range(4))
        VB = r.take(2, P)
        QM = r.take(2, TOK)
        PB = r.take(2, 2, TOK)
        PTB = r.take(2, 2, TOK)
        VM = r.take(2, 2, P)
        MHS = r.take(2, 6)
        r.at = both
        SOP = r.take(TW, TW)
        SFB = r.take(NS, 2 * C)
        STT = r.take(NS, P)
        ATB = SFB.rearrange("p a b -> p (a b)").rearrange("p (k n) -> p k n", k=2)
        WST = r.take(2, P)
        r = Region()
        FCT = r.take(RED, 2, FC)
        POOLED = r.take(TOK)
        RB = r.take(2, 2 * RED)
        FS = r.take(FC)
        RW = r.take(EXPERTS)
        CW = r.take(36)
        WE = r.take(9, P)
        r = Region()
        OFF = r.take(H, 16)
        SEL = r.take(9, P)
        l2at = r.at
        i_xn = r.take(2, CH)
        r.at = l2at
        d_xb, d_sq, d_rs, d_y = (r.take(2, CH) for _ in range(4))
        r.at = l2at
        MXR = r.take(P)
        r.at = l2at
        HT = r.take(3, 64)
        W9 = r.take(ROWS, 9, SG)
        WT = r.take(CH)
        PRD = r.take(2, CH)
        FAR = r.take(3, ROWS * SG)
        CUR = r.take(4)
        XS, AB, RL, DA, UU, HH, HC, YY, SQ2, RS2, TT = (r.take(CH) for _ in range(11))
        r = Region()
        OBUF = r.take(2, CH)

        load = sem("load")
        const_ready = sem("const_ready")
        settled = sem("settled")
        const_pe = sem("const_pe")
        const_act = sem("const_act")
        const_dve = sem("const_dve")
        const_pool = sem("const_pool")
        x_in = [sem(f"x_in{j}") for j in range(4)]
        stats_done = sem("stats_done")
        gn_dve, gn_pe, gn_act = sem("gn_dve"), sem("gn_pe"), sem("gn_act")
        names = {}

        def steps(*ns):
            for n in ns:
                names[n] = sem(n)
            return [names[n] for n in ns]

        ln0_xn, ln0_cen, ln0_sq, ln0_var, ln0_ln, ln0_rs, ln0_y, ln0_yb = steps(
            "ln0_xn", "ln0_cen", "ln0_sq", "ln0_var", "ln0_ln", "ln0_rs", "ln0_y", "ln0_yb")
        (sp_stage, sp_lgt, sp_tr, sp_pixt, sp_log, sp_mx, sp_sub, sp_exp, sp_sum, sp_rec, sp_aff, sp_e, sp_fold,
         sp_acc) = steps("sp_stage", "sp_lgt", "sp_tr", "sp_pixt", "sp_log", "sp_mx", "sp_sub", "sp_exp", "sp_sum",
                         "sp_rec", "sp_aff", "sp_e", "sp_fold", "sp_acc")
        tok_dve, tok_zero = sem("tok_dve"), sem("tok_zero")
        sf_dve = sem("sf_dve")
        mha_pe, mha_act = sem("mha_pe"), sem("mha_act")
        mh_qm, mh_s, mh_mx, mh_nmx, mh_exp, mh_rec, mh_pn, mh_pt, mh_ptc, mh_vm, mh_pv = steps(
            "mh_qm", "mh_s", "mh_mx", "mh_nmx", "mh_exp", "mh_rec", "mh_pn", "mh_pt", "mh_ptc", "mh_vm", "mh_pv")
        so_dve, so_pe, so_act, so_zero = sem("so_dve"), sem("so_pe"), sem("so_act"), sem("so_zero")
        o_e, o_tr, o_at, o_mm, o_x = steps("o_e", "o_tr", "o_at", "o_mm", "o_x")
        fc_in = sem("fc_in")
        l1_xn, l1_mm, l1_x = steps("l1_xn", "l1_mm", "l1_x")
        l1_pool = sem("l1_pool")
        rt_pe, rt_dve, rt_act = sem("rt_pe"), sem("rt_dve"), sem("rt_act")
        in_xn, in_mm, in_cp = steps("in_xn", "in_mm", "in_cp")
        d1_mm, d1_act = steps("d1_mm", "d1_act")
        border = sem("border")
        d2_mm, d2_xb, d2_cen, d2_sq, d2_var, d2_ln, d2_rs, d2_y, d2_g, d2_off, d2_o = steps(
            "d2_mm", "d2_xb", "d2_cen", "d2_sq", "d2_var", "d2_ln", "d2_rs", "d2_y", "d2_g", "d2_off", "d2_o")
        far_step, far_w, far_tr, far_wt, far_b = (sem(n) for n in ("far_step", "far_w", "far_tr", "far_wt", "far_b"))
        rad_dve, rad_pe = sem("rad_dve"), sem("rad_pe")
        df_tr, df_wt, sel_in = sem("df_tr"), sem("df_wt"), sem("sel_in")
        df_ht, df_w9, df_w, df_p, df_a = sem("df_ht"), sem("df_w9"), sem("df_w"), sem("df_p"), sem("df_a")
        (xs_ready, sc_zbc, sc_abs, sc_exp, sc_ln, sc_delta, sc_u, sc_da, sc_bx, sc_h, sc_hc, sc_y, sc_cen, sc_sq, sc_var,
         sc_lv, sc_rs, sc_t, sc_x) = (sem(n) for n in (
            "xs_ready", "sc_zbc", "sc_abs", "sc_exp", "sc_ln", "sc_delta", "sc_u", "sc_da", "sc_bx", "sc_h", "sc_hc",
            "sc_y", "sc_cen", "sc_sq", "sc_var", "sc_lv", "sc_rs", "sc_t", "sc_x"))
        l3_xn, l3_mm, l3_o = steps("l3_xn", "l3_mm", "l3_o")
        out_dma = [sem(f"out_dma{k}") for k in range(2)]

        def settle(eng):
            eng.sem_inc(settled, 1)

        far_dve_step, far_dve_turn = nc.vector.alloc_register("far_dve_step"), nc.vector.alloc_register("far_dve_turn")
        far_pe_turn = nc.tensor.alloc_register("far_pe_turn")

        def credit(eng, *sems, by=CREDIT):
            for s in sems:
                eng.sem_inc(s, by)

        block = ctx.enter_context(nc.Block())

        def xch(t):
            return X[:, bass.ds(t * ROWS, ROWS), :]

        def pch(t, base=BASE, dy=0, dx=0):
            return PAD[:, bass.ds(t * ROWS + (base + dy), ROWS), 1 + dx:1 + dx + W]

        def img(a):
            return a.rearrange("p (r w) -> p r w", r=ROWS)

        NM, RSTD = SM[:, 4:5], SM[:, 5:6]

        NLOAD = 13

        @block.sync
        def _(sp):
            for lo in (0, C):
                sp.dma_start(VECS[lo:lo + C, :], vec).then_inc(load, 16)
                sp.dma_start(MATS[lo:lo + C, :], mat).then_inc(load, 16)
            sp.dma_start(DTS[:, :], dts).then_inc(load, 16)
            sp.dma_start(ROWV[:, :], rows).then_inc(load, 16)
            sp.dma_start(CSTS[:, :], cst).then_inc(load, 16)
            for k in range(2):
                sp.sem_inc(out_dma[k], 16)
            with sp.Fori(0, PAIRS) as pair:
                sp.wait_ge(l3_o, pair * NT + CREDIT)
                for j in range(4):
                    sp.dma_start(X[:, j * H // 4:(j + 1) * H // 4, :],
                                 x[bass.ds(pair * P, P), j * H // 4:(j + 1) * H // 4, :]).then_inc(x_in[j], 16)
                sp.wait_ge(o_x, pair * NS + NS + CREDIT)
                sp.dma_start(FCT, fc).then_inc(fc_in, 16)
                sp.wait_ge(l1_x, (pair + 1) * NT + CREDIT)
                sp.dma_start(SEL[0:9 * SG], sel).then_inc(sel_in, 16)
                with sp.Fori(0, NT // 2) as i:
                    for k in range(2):
                        t = pair * NT + i * 2 + k
                        sp.wait_ge(l3_o, after(t))
                        sp.dma_start(out[bass.ds(pair * P, P), bass.ds((i * 2 + k) * ROWS, ROWS), :],
                                     img(OBUF[:, k, :])).then_inc(out_dma[k], 16)
            for k in range(2):
                sp.wait_ge(out_dma[k], 16 * (PAIRS * NT // 2 + 1))

        def expand(dve, k, st):
            a = AFF[:, bass.ds(st, 1), :, :].rearrange("p o (j s) (r c) -> p (o j) s r c", s=2, r=3)
            for b in range(2):
                for s in range(2):
                    first = EXPD[b * 64:b * 64 + 64, k, 0, s * C + b:s * C + b + 1]
                    v = bass.AP(first.tensor, first.offset, [list(first.ap[0]), [2 * C + 2, 8], [TW, 3], [1, 3]])
                    ins = dve.tensor_scalar(v, a[b * 64:b * 64 + 64, :, s, :, :], 1.0, None, ALU.mult)
            return ins

        def far_dve(dve, t, reach):
            oy, ox, fy = (FAR[:, j, :].rearrange("p (y g) -> p y g", y=ROWS) for j in range(3))

            def link(ins):
                ins.then_inc(far_step, 1)
                dve.reg_add(far_dve_step, far_dve_step, 1)
                dve.wait_ge(far_step, dve.snap(far_dve_step, min_val=1))

            def hat(a):
                link(dve.scalar_tensor_tensor(out=a, in0=a, scalar=-1.0, in1=a, op0=ALU.mult, op1=ALU.min))
                link(dve.tensor_scalar(a, a, 1.0, 0.0, ALU.add, ALU.max))

            def one_row(ys, e):
                ys = nc.s_assert_within(ys, 0, H - 1, skip_runtime_bounds_check_because="both branches were taken")
                link(dve.tensor_scalar(fy, oy, CUR[:, 0:1], None, ALU.subtract))
                hat(fy)
                dve.tensor_tensor(fy, fy, ox, ALU.mult).then_inc(far_w, 1)
                dve.reg_add(far_dve_turn, far_dve_turn, 1)
                turn = dve.snap(far_dve_turn, min_val=1)
                dve.wait_ge(far_tr, turn)
                dve.tensor_scalar(WT[0:ROWS * SG, 0:W], PSUM[0:ROWS * SG, 5, 0:W], 1.0, None, ALU.mult).then_inc(far_wt, 1)
                dve.wait_ge(far_b, turn)
                src = PAD[:, :, :].rearrange("p r w -> p (r w)")[:, bass.ds(ys * PW + (e - reach) + (XBASE * PW + 1), W)]
                link(dve.tensor_tensor(img(PRD[:, 0, :]), img(PSUM[:, 0, :]),
                                       src.unsqueeze(1).broadcast_to([P, ROWS, W]), ALU.mult))
                link(dve.tensor_tensor(XS, XS, PRD[:, 0, :], ALU.add))
                settle(dve)

            off = OFF[:, bass.ds(t * ROWS, ROWS), :].rearrange("p y (a g) -> p y a g", a=2)
            row = CST["row"][0]
            link(dve.memset(XS, 0.0))
            link(dve.tensor_tensor(oy, off[:, :, 1, :],
                                   CSTS[:, bass.ds(t * ROWS + row, ROWS)].unsqueeze(2).broadcast_to([P, ROWS, SG]), ALU.add))
            link(dve.tensor_scalar(CUR[:, 1:2], SM[:, 19:20], 1.0, None, ALU.mult))
            settle(dve)
            with dve.Fori(0, reach * 2 + 1) as e:
                link(dve.tensor_tensor(CUR[:, 2:3], cs("col"), CUR[:, 1:2], ALU.add))
                link(dve.tensor_scalar(CUR[:, 3:4], CUR[:, 2:3], 0.0, None, ALU.is_ge))
                link(dve.tensor_scalar(CUR[:, 2:3], CUR[:, 2:3], W - 1.0, None, ALU.is_le))
                link(dve.tensor_tensor(CUR[:, 2:3], CUR[:, 2:3], CUR[:, 3:4], ALU.mult))
                link(dve.tensor_scalar(ox, off[:, :, 0, :], CUR[:, 1:2], None, ALU.subtract))
                hat(ox)
                link(dve.tensor_scalar(ox, ox, CUR[:, 2:3], None, ALU.mult))
                link(dve.tensor_tensor(CUR[:, 0:1], CSTS[:, bass.ds(t * ROWS + row, 1)], SM[:, 19:20], ALU.add))
                settle(dve)
                with dve.Fori(0, reach * 2 + ROWS) as d:
                    ys = dve.snap(t * ROWS + d - reach)
                    with dve.If(ys >= 0):
                        with dve.If(ys < H):
                            one_row(ys, e)
                    link(dve.tensor_scalar(CUR[:, 0:1], CUR[:, 0:1], 1.0, None, ALU.add))
                link(dve.tensor_scalar(CUR[:, 1:2], CUR[:, 1:2], 1.0, None, ALU.add))

        def far_pe(pe, t, reach):
            with pe.Fori(0, reach * 2 + 1) as _:
                with pe.Fori(0, reach * 2 + ROWS) as d:
                    ys = pe.snap(t * ROWS + d - reach)
                    with pe.If(ys >= 0):
                        with pe.If(ys < H):
                            pe.reg_add(far_pe_turn, far_pe_turn, 1)
                            turn = pe.snap(far_pe_turn, min_val=1)
                            pe.wait_ge(far_w, turn)
                            pe.transpose(PSUM[0:ROWS * SG, 5, 0:P], FAR[:, 2, :], ident).then_inc(far_tr, 1)
                            pe.wait_ge(far_wt, turn)
                            for y in range(ROWS):
                                ins = pe.matmul(PSUM[:, 0, y * W:(y + 1) * W], SEL[0:ROWS * SG, y, :],
                                                WT[0:ROWS * SG, 0:W], start=True, stop=True)
                            ins.then_inc(far_b, 1)

        def deform_and_scan_dve(dve, pair, stats):
            settle(dve)
            reach = dve.value_load(RI[0:1, 0:1], min_val=0, max_val=MAXR)
            offs = OFF.rearrange("p y n -> p (y n)")
            ht = HT.rearrange("p d (y a g) -> p d y a g", y=ROWS, a=2)
            with dve.Fori(0, NT) as t:
                T = pair * NT + t
                dve.wait_ge(df_w9, T + 1)
                dve.tensor_tensor(HT, offs[:, bass.ds(t * 64, 64)].unsqueeze(1).broadcast_to([P, 3, 64]),
                                  cs("shift").unsqueeze(2).broadcast_to([P, 3, 64]), ALU.subtract).then_inc(df_ht, 1)
                dve.wait_ge(df_ht, T * 3 + 2)
                dve.scalar_tensor_tensor(out=HT, in0=HT, scalar=-1.0, in1=HT, op0=ALU.mult, op1=ALU.min).then_inc(df_ht, 1)
                dve.wait_ge(df_ht, T * 3 + 3)
                dve.tensor_scalar(HT, HT, 1.0, 0.0, ALU.add, ALU.max).then_inc(df_ht, 1)
                dve.wait_ge(df_ht, T * 3 + 4)
                dve.wait_ge(df_tr, T + 1)
                for j in range(3):
                    ins = dve.tensor_tensor(
                        W9[:, :, 3 * j:3 * j + 3, :].rearrange("p y d g -> p d y g"),
                        ht[:, j, :, 1, :].unsqueeze(1).broadcast_to([P, 3, ROWS, SG]), ht[:, :, :, 0, :], ALU.mult)
                ins.then_inc(df_w9, 1)
                dve.wait_ge(sc_cen, T + 1)
                for j, (dy, dx) in enumerate(TAPS):
                    dve.wait_ge(df_w, T * 9 + (j + 2))
                    if j > 2:
                        dve.wait_ge(df_a, T * 8 + (j - 1))
                    elif j > 0:
                        dve.wait_ge(df_a, T * 8 + 1)
                    o = XS if j == 0 else PRD[:, j % 2, :]
                    dve.tensor_tensor(img(o), img(PSUM[:, j % 2, :]), pch(t, XBASE, dy, dx),
                                      ALU.mult).then_inc(df_p, 1)
                dve.wait_ge(df_a, T * 8 + 9)
                settle(dve)
                with dve.If(reach > 0):
                    far_dve(dve, t, reach)
                dve.sem_inc(xs_ready, 1)
                dve.wait_ge(sc_u, T + 2)
                dve.wait_ge(sc_zbc, T + 2)
                dve.tensor_tensor(UU, UU, PSUM[:, 3, :], ALU.mult).then_inc(sc_bx, 1)
                dve.wait_ge(sc_bx, T + 2)
                dve.wait_ge(sc_da, T + 2)
                dve.tensor_tensor_scan(HH, DA, UU, SM[:, 12:13], ALU.mult, ALU.add).then_inc(sc_h, 1)
                dve.wait_ge(sc_h, T + 2)
                dve.tensor_copy(SM[:, 12:13], HH[:, CH - 1:CH])
                dve.tensor_tensor(HC, HH, PSUM[:, 4, :], ALU.mult).then_inc(sc_hc, 1)
                dve.wait_ge(sc_hc, T + 2)
                dve.scalar_tensor_tensor(out=YY, in0=XS, scalar=vc("Ds"), in1=HC,
                                         op0=ALU.mult, op1=ALU.add).then_inc(sc_y, 1)
                dve.wait_ge(sc_rs, T + 2)
                dve.tensor_tensor(TT, PSUM[:, 6, :], RS2, ALU.mult).then_inc(sc_t, 1)
                dve.wait_ge(sc_t, T + 2)
                dve.scalar_tensor_tensor(out=xch(t), in0=img(TT), scalar=OUTB[:, :], in1=xch(t),
                                         op0=ALU.add, op1=ALU.add).then_inc(sc_x, 1)
                dve.wait_ge(sc_x, T + 2)
                stats(t, t)

        @block.vector
        def _(dve):
            credit(dve, ln0_y, sp_log, sp_mx, sp_sub, sp_sum, sp_rec, sp_aff, sp_e, sp_acc, mh_qm, mh_mx, mh_nmx,
                   mh_rec, mh_pn, mh_vm, o_e, o_x, l1_x, in_cp, d2_y, d2_o, l3_o)
            credit(dve, df_ht, df_w9, df_p, xs_ready, sc_bx, sc_h, sc_hc, sc_y, sc_t, sc_x, by=1)
            dve.reg_mov(far_dve_step, 0)
            dve.reg_mov(far_dve_turn, 0)
            dve.wait_ge(load, 16 * 7)
            for w in (WQ, WK, WV, WPROJ, WIN, WOUT, WZ, WB, WC):
                dve.memset(w[:, :], 0.0)
            dve.memset(WOFF[:, :, :, :], 0.0)
            dve.memset(WCONV[:, :, :], 0.0)
            dve.memset(PLAIN[:, :], 0.0)
            dve.memset(SM[:, :], 0.0)
            dve.memset(GNE[:, 0:1], GN_EPS)
            dve.memset(GNE[:, 1:2], LN_EPS)
            dve.memset(WL3[:, :, :], 0.0).then_inc(const_dve, 1)
            dve.tensor_scalar(NOT3[:, :], cs("mask3"), -1.0, 1.0, ALU.mult, ALU.add).then_inc(const_dve, 1)
            dve.wait_ge(const_dve, 2)
            for s in range(2):
                p, q = s * C, s * C + C
                for w, name in ((WQ, "q"), (WK, "k"), (WV, "v"), (WPROJ, "proj"), (WIN, "in_proj"), (PLAIN, "out_proj")):
                    dve.tensor_copy(w[p:q, p:q], mt(name, p, q))
                dve.tensor_copy(WOFF[p:q, :, s, :], mt("off", p, q).rearrange("p (g a) -> p a g", a=2))
                dve.tensor_copy(WCONV[p:q, s, :], mt("conv", p, q))
                xp = MAT["x_proj"][0]
                for w, col in ((WB, DT_RANK), (WC, DT_RANK + 1)):
                    dve.tensor_copy(w[p:q, p:q], MATS[p:q, xp + col:xp + col + 1].broadcast_to([C, C]))
                dve.tensor_scalar(WOUT[p:q, p:q], mt("out_proj", p, q), vc("out_ln_g")[p:q], None, ALU.mult)
                dve.tensor_tensor(WL3[p:q, :, p:q], mt("w3", p, q).rearrange("p (t o) -> p t o", t=9),
                                  cs("mask3")[p:q, p:q].unsqueeze(1).broadcast_to([C, 9, C]), ALU.mult)
                dve.tensor_tensor(NOT3[p:q, p:q], mt("w1", p, q), NOT3[p:q, p:q], ALU.mult).then_inc(const_dve, 1)
            dve.wait_ge(const_dve, 4)
            for s in range(2):
                p, q = s * C, s * C + C
                dve.tensor_tensor(WL3[p:q, 4, p:q], WL3[p:q, 4, p:q], NOT3[p:q, p:q], ALU.add)
            for w, name in ((WDW1, "conv2d_w"), (WDW2, "dw_w")):
                for j in range(9):
                    dve.tensor_scalar(w[:, j, :], ident, vc(name, j), None, ALU.mult)
            dve.tensor_reduce(SM[:, 8:9], vc("l3_b", 0, C), AX.X, ALU.add).then_inc(const_dve, 1)
            dve.wait_ge(const_pe, 1)
            for s in range(2):
                p, q = s * C, s * C + C
                dve.tensor_copy(WZ[p:q, p:q], PSUM[p:q, 0, 0:C])
            dve.tensor_copy(OUTB[:, :], PSUM[:, 1, 0:1])
            dve.tensor_copy(WOUT2[:, :], PSUM[:, 2, 0:P])
            dve.wait_ge(const_act, 1)
            dve.tensor_scalar(SM[:, 9:10], SM[:, 10:11], -1.0, None, ALU.mult).then_inc(const_ready, 1)

            def group_norm(n):
                dve.wait_ge(stats_done, (n + 1) * NT)
                settle(dve)
                dve.bn_aggr(SM[:, 0:2], STATS[:, :, :]).then_inc(gn_dve, 1)
                dve.wait_ge(gn_pe, n * 2 + 1)
                dve.wait_ge(gn_dve, n * 5 + 1)
                dve.tensor_tensor(SM[:, 2:3], SM[:, 0:1], PSUM[:, 7, 0:1], ALU.subtract).then_inc(gn_dve, 1)
                dve.wait_ge(gn_dve, n * 5 + 2)
                dve.scalar_tensor_tensor(out=SM[:, 3:4], in0=SM[:, 2:3], scalar=SM[:, 2:3], in1=SM[:, 1:2],
                                         op0=ALU.mult, op1=ALU.add).then_inc(gn_dve, 1)
                dve.wait_ge(gn_act, n + 1)
                dve.reciprocal(SM[:, 5:6], SM[:, 6:7]).then_inc(gn_dve, 1)
                dve.wait_ge(gn_dve, n * 5 + 4)
                dve.scalar_tensor_tensor(out=SM[:, 4:5], in0=PSUM[:, 7, 0:1], scalar=-1.0, in1=SM[:, 5:6],
                                         op0=ALU.mult, op1=ALU.mult).then_inc(gn_dve, 1)

            def stats(t, s):
                dve.bn_stats(STATS[:, bass.ds(s, 1), :], xch(t)).then_inc(stats_done, 1)

            with dve.Fori(0, PAIRS) as pair:
                for j in range(4):
                    dve.wait_ge(x_in[j], pair * 16 + 16)
                    settle(dve)
                    with dve.Fori(j * NT // 4, (j + 1) * NT // 4) as t:
                        dve.bn_stats(STATS[:, bass.ds(t, 1), :], xch(t)).then_inc(stats_done, 1)
                group_norm(pair * 4)
                with dve.Fori(0, NT // 2) as i:
                    for k in range(2):
                        T = pair * NT + i * 2 + k
                        dve.wait_ge(ln0_rs, after(T))
                        dve.wait_ge(ln0_yb, reuse(T))
                        dve.scalar_tensor_tensor(out=n_y[:, k, :], in0=PSUM[:, k, :], scalar=vc("ln_w"),
                                                 in1=n_rs[:, k, :], op0=ALU.mult, op1=ALU.mult).then_inc(ln0_y, 1)
                dve.wait_ge(ln0_yb, (pair + 1) * NT + CREDIT)
                dve.memset(STB, 0.0)
                dve.memset(SFAS, 0.0)
                dve.memset(EXPD, 0.0).then_inc(tok_zero, 1)
                dve.wait_ge(tok_zero, pair + 1)
                settle(dve)
                for s in range(2):
                    with dve.Fori(0, NS) as i:
                        p, q = s * C, s * C + C
                        dve.tensor_reduce(
                            STB[p:q, bass.ds(i + 1, 1), s, 1:1 + NS],
                            PAD[p:q, bass.ds(i * 8 + BASE, 8), 1:1 + W].rearrange("p r (b q) -> p b r q", q=8),
                            AX.XY, ALU.add).then_inc(tok_dve, 1)
                with dve.Fori(0, NS // 2) as i:
                    S = [pair * NS + i * 2 + k for k in range(2)]
                    st = [i * 2 + k for k in range(2)]
                    for k in range(2):
                        dve.wait_ge(sp_lgt, after(S[k]))
                        v = PSUM[:, k, 0:8 * 24].rearrange("p (a r c) -> p a r c", r=3, c=4)
                        o = LG[:, k, :, :].rearrange("p a (r c) -> p a r c", r=3)
                        dve.tensor_copy(o[0:64], v[0:64, :, :, 0:3])
                        dve.tensor_copy(o[64:128], v[64:128, :, :, 1:4]).then_inc(sp_log, 1)
                    for k in range(2):
                        dve.wait_ge(sp_log, after(S[k]))
                        dve.tensor_reduce(SMX[:, k, 0, :], LG[:, k, :, :], AX.X, ALU.max).then_inc(sp_mx, 1)
                    for k in range(2):
                        dve.wait_ge(sp_mx, after(S[k]))
                        dve.tensor_tensor(LG[:, k, :, :], LG[:, k, :, :],
                                          SMX[:, k, 0, :].unsqueeze(2).broadcast_to([P, NS, 9]),
                                          ALU.subtract).then_inc(sp_sub, 1)
                    for k in range(2):
                        dve.wait_ge(sp_exp, after(S[k]))
                        dve.tensor_reduce(SMX[:, k, 1, :], LG[:, k, :, :], AX.X, ALU.add).then_inc(sp_sum, 1)
                    for k in range(2):
                        dve.wait_ge(sp_sum, after(S[k]))
                        dve.reciprocal(SMX[:, k, 2, :], SMX[:, k, 1, :]).then_inc(sp_rec, 1)
                    for k in range(2):
                        dve.wait_ge(sp_rec, after(S[k]))
                        dve.tensor_tensor(AFF[:, bass.ds(st[k], 1), :, :].rearrange("p o a b -> p (o a) b"),
                                          LG[:, k, :, :],
                                          SMX[:, k, 2, :].unsqueeze(2).broadcast_to([P, NS, 9]),
                                          ALU.mult).then_inc(sp_aff, 1)
                    for k in range(2):
                        dve.wait_ge(sp_aff, after(S[k]))
                        dve.wait_ge(sp_fold, reuse(S[k]))
                        expand(dve, k, st[k]).then_inc(sp_e, 1)
                    for k in range(2):
                        dve.wait_ge(sp_fold, after(S[k]))
                        dve.wait_ge(sp_acc, after(S[k] - 1))
                        for s in range(2):
                            p, q = s * C, s * C + C
                            v = SFAS[p:q, :, bass.ds(st[k] * TW, 3 * TW)]
                            ins = dve.tensor_tensor(
                                v, PSUM[p:q, 6 + k, 0:2 * P].rearrange("p (a b) -> p a b", a=2)[:, :, s * C:s * C + 3 * TW],
                                v, ALU.add)
                        ins.then_inc(sp_acc, 1)
                dve.wait_ge(sp_acc, (pair + 1) * NS + CREDIT)
                inner = SFAS.rearrange("p a (i j) -> p a i j", i=TW)[:, :, 1:1 + NS, 1:1 + NS]
                dve.tensor_scalar(inner[:, 1], inner[:, 1], 1e-12, None, ALU.add).then_inc(sf_dve, 1)
                dve.wait_ge(sf_dve, pair * 3 + 1)
                dve.reciprocal(inner[:, 1], inner[:, 1]).then_inc(sf_dve, 1)
                dve.wait_ge(sf_dve, pair * 3 + 2)
                dve.wait_ge(sp_fold, (pair + 1) * NS + CREDIT)
                dve.tensor_tensor(SFC.rearrange("p (i j) -> p i j", i=NS), inner[:, 0], inner[:, 1],
                                  ALU.mult).then_inc(sf_dve, 1)
                dve.wait_ge(mha_act, pair * 2 + 1)
                settle(dve)
                with dve.Fori(0, NH // 2) as i:
                    h = [i * 2 + k for k in range(2)]
                    N = [pair * NH + h[k] for k in range(2)]
                    for k in range(2):
                        dve.wait_ge(mh_s, reuse(N[k]))
                        a = CST["headcol"][0]
                        dve.tensor_scalar(QM[:, k, :], QB, CSTS[:, bass.ds(h[k] + a, 1)], None,
                                          ALU.mult).then_inc(mh_qm, 1)
                    for k in range(2):
                        dve.wait_ge(mh_pv, reuse(N[k]))
                        a = CST["headrow"][0] + P - HD
                        dve.tensor_tensor(VM[:, k, :, :], VB,
                                          CSTS[:, bass.ds(h[k] * -HD + a, P)].unsqueeze(1).broadcast_to([P, 2, P]),
                                          ALU.mult).then_inc(mh_vm, 1)
                    for k in range(2):
                        dve.wait_ge(mh_s, after(N[k]))
                        dve.tensor_reduce(MHS[:, k, 0:2], PSUM[:, k, :].rearrange("p (a b) -> p a b", a=2),
                                          AX.X, ALU.max).then_inc(mh_mx, 1)
                    for k in range(2):
                        dve.wait_ge(mh_mx, after(N[k]))
                        dve.tensor_scalar(MHS[:, k, 2:4], MHS[:, k, 0:2], -HD ** -0.5, None,
                                          ALU.mult).then_inc(mh_nmx, 1)
                    for k in range(2):
                        dve.wait_ge(mh_exp, after(N[k]))
                        dve.reciprocal(MHS[:, k, 0:2], MHS[:, k, 4:6]).then_inc(mh_rec, 1)
                    for k in range(2):
                        dve.wait_ge(mh_rec, after(N[k]))
                        dve.tensor_tensor(PB[:, k, :, :], PB[:, k, :, :],
                                          MHS[:, k, 0:2].unsqueeze(2).broadcast_to([P, 2, TOK]),
                                          ALU.mult).then_inc(mh_pn, 1)
                dve.wait_ge(mha_pe, pair * 3 + 3)
                dve.memset(SOP, 0.0)
                dve.memset(SFB, 0.0).then_inc(so_dve, 1)
                dve.wait_ge(so_dve, pair * 4 + 1)
                dve.tensor_scalar(SOP[:, 1:1 + NS, 1:1 + NS], PSUM[:, 6, 0:TOK].rearrange("p (i j) -> p i j", i=NS),
                                  vc("proj_b"), None, ALU.add).then_inc(so_dve, 1)
                dve.wait_ge(so_dve, pair * 4 + 2)
                for s in range(2):
                    p, q = s * C, s * C + C
                    for j in range(3):
                        ins = dve.tensor_copy(SFB[p:q, :, s * C + j * TW:s * C + (j + 1) * TW], SOP[p:q, j:j + NS, :])
                ins.then_inc(so_dve, 1)
                dve.wait_ge(so_pe, pair + 1)
                for j in range(4):
                    ins = dve.tensor_copy(STT[:, 4 * j:4 * j + 4, :],
                                          PSUM[:, j, :].rearrange("p (a b) -> p a b", a=4))
                ins.then_inc(so_dve, 1)
                with dve.Fori(0, NS // 2) as i:
                    S = [pair * NS + i * 2 + k for k in range(2)]
                    st = [i * 2 + k for k in range(2)]
                    for k in range(2):
                        dve.wait_ge(o_tr, reuse(S[k]))
                        expand(dve, k, st[k]).then_inc(o_e, 1)
                    for k in range(2):
                        dve.wait_ge(o_mm, after(S[k]))
                        for j in range(2):
                            v = X[:, bass.ds(st[k] * 8, 8), j * 64:(j + 1) * 64].rearrange("p r (b q) -> p b r q", q=8)
                            ins = dve.tensor_tensor(v, PSUM[:, 4 + 2 * k + j, :].rearrange("p (b r q) -> p b r q", b=8, r=8),
                                                    v, ALU.add)
                        ins.then_inc(o_x, 1)
                    for k in range(2):
                        dve.wait_ge(o_x, after(S[k]))
                        for j in range(2):
                            stats(st[k] * 2 + j, st[k] * 2 + j)
                group_norm(pair * 4 + 1)
                dve.wait_ge(o_at, (pair + 1) * NS + CREDIT)
                settle(dve)
                with dve.Fori(0, NS) as i:
                    dve.wait_ge(l1_xn, after(pair * NT + i * 2 + 1))
                    dve.tensor_reduce(POOLED[:, bass.ds(i * NS, NS)],
                                      PAD[:, bass.ds(i * 8 + BASE, 8), 1:1 + W].rearrange("p r (b q) -> p b r q", q=8),
                                      AX.XY, ALU.add).then_inc(l1_pool, 1)
                q0 = pair * 10
                dve.wait_ge(rt_pe, pair * 4 + 1)
                dve.scalar_tensor_tensor(out=RB, in0=PSUM[:, 0, 0:64].rearrange("p (a b) -> p a b", a=2), scalar=1.0 / 64,
                                         in1=ROWV[:, 0:2 * RED].unsqueeze(1).broadcast_to([P, 2, 2 * RED]),
                                         op0=ALU.mult, op1=ALU.add).then_inc(rt_dve, 1)
                dve.wait_ge(rt_dve, q0 + 1)
                dve.tensor_scalar(RB, RB, 0.0, None, ALU.max).then_inc(rt_dve, 1)
                dve.wait_ge(rt_pe, pair * 4 + 2)
                dve.tensor_copy(FS[0:2, :], PSUM[0:2, 1, 0:FC]).then_inc(rt_dve, 1)
                dve.wait_ge(rt_pe, pair * 4 + 3)
                dve.tensor_tensor(RW, PSUM[:, 2, 0:EXPERTS], vc("fc_b", 0, EXPERTS), ALU.add).then_inc(rt_dve, 1)
                dve.wait_ge(rt_dve, q0 + 4)
                dve.tensor_scalar(RW, RW, 0.0, None, ALU.max).then_inc(rt_dve, 1)
                dve.wait_ge(rt_act, pair + 1)
                dve.tensor_scalar(CW, vc("experts", 0, 36), RW[:, 0:1], None, ALU.mult).then_inc(rt_dve, 1)
                for e in range(1, EXPERTS):
                    dve.wait_ge(rt_dve, q0 + 5 + e)
                    dve.scalar_tensor_tensor(out=CW, in0=vc("experts", 36 * e, 36), scalar=RW[:, e:e + 1], in1=CW,
                                             op0=ALU.mult, op1=ALU.add).then_inc(rt_dve, 1)
                dve.wait_ge(rt_dve, q0 + 9)
                for j in range(9):
                    ins = dve.tensor_tensor(
                        WE[:, j, :].rearrange("p (g i) -> p g i", i=4),
                        CW.rearrange("p (i t) -> p t i", t=9)[:, j, :].unsqueeze(1).broadcast_to([P, 32, 4]),
                        cs("group4").rearrange("p (g i) -> p g i", i=4), ALU.mult)
                ins.then_inc(rt_dve, 1)
                dve.wait_ge(rt_pe, pair * 4 + 4)
                dve.tensor_copy(WL1[:, 0:4, :], PSUM[:, 3, :].rearrange("p (a b) -> p a b", a=4))
                dve.tensor_copy(WL1[:, 4:8, :], PSUM[:, 4, :].rearrange("p (a b) -> p a b", a=4))
                dve.tensor_copy(WL1[:, 8, :], PSUM[:, 5, 0:P]).then_inc(l1_pool, 1)
                with dve.Fori(0, NT // 2) as i:
                    for k in range(2):
                        t = i * 2 + k
                        T = pair * NT + t
                        dve.wait_ge(l1_mm, after(T))
                        dve.tensor_tensor(xch(t), img(PSUM[:, k, :]), xch(t), ALU.add).then_inc(l1_x, 1)
                    for k in range(2):
                        t = i * 2 + k
                        dve.wait_ge(l1_x, after(pair * NT + t))
                        stats(t, t)
                group_norm(pair * 4 + 2)
                with dve.Fori(0, NT // 2) as i:
                    for k in range(2):
                        t = i * 2 + k
                        dve.wait_ge(in_mm, after(pair * NT + t))
                        dve.tensor_scalar(pch(t), img(PSUM[:, k, :]), 1.0, None, ALU.mult).then_inc(in_cp, 1)
                with dve.Fori(0, NT // 2) as i:
                    for k in range(2):
                        t = i * 2 + k
                        T = pair * NT + t
                        dve.wait_ge(d2_rs, after(T))
                        dve.wait_ge(d2_off, reuse(T))
                        dve.scalar_tensor_tensor(out=d_y[:, k, :], in0=PSUM[:, 2 + k, :], scalar=vc("dw_ln_g"),
                                                 in1=d_rs[:, k, :], op0=ALU.mult, op1=ALU.mult).then_inc(d2_y, 1)
                    for k in range(2):
                        t = i * 2 + k
                        dve.wait_ge(d2_off, after(pair * NT + t))
                        dve.tensor_tensor(OFF[:, bass.ds(t * ROWS, ROWS), :],
                                          PSUM[:, 6 + k, 0:64].rearrange("p (a b) -> p a b", a=ROWS),
                                          ROWV[:, 2 * RED:].rearrange("p (a b) -> p a b", a=ROWS),
                                          ALU.add).then_inc(d2_o, 1)
                dve.wait_ge(d2_o, (pair + 1) * NT + CREDIT)
                dve.tensor_reduce(SM[:, 16:17], OFF, AX.XY, ALU.max, apply_absolute_value=True).then_inc(rad_dve, 1)
                dve.wait_ge(rad_pe, pair * 2 + 1)
                dve.tensor_reduce(SM[0:1, 17:18], PSUM[0:1, 0, 0:P], AX.X, ALU.max).then_inc(rad_dve, 1)
                dve.wait_ge(rad_pe, pair * 2 + 2)
                dve.tensor_scalar(SM[:, 18:19], PSUM[:, 0, P:P + 1], 1.0, None, ALU.is_gt)
                dve.tensor_scalar(SM[:, 19:20], PSUM[:, 0, P:P + 1], MAXR - 1.0, 1.0, ALU.min, ALU.add).then_inc(rad_dve, 1)
                dve.wait_ge(rad_dve, pair * 5 + 3)
                dve.tensor_tensor(RI[:, :], SM[:, 18:19], SM[:, 19:20], ALU.mult).then_inc(rad_dve, 1)
                dve.wait_ge(rad_dve, pair * 5 + 4)
                dve.tensor_scalar(SM[:, 19:20], RI[:, :], -1.0, None, ALU.mult)
                dve.memset(SM[:, 12:13], 0.0).then_inc(rad_dve, 1)
                dve.wait_ge(rad_dve, pair * 5 + 5)
                deform_and_scan_dve(dve, pair, stats)
                group_norm(pair * 4 + 3)
                with dve.Fori(0, NT // 2) as i:
                    for k in range(2):
                        t = i * 2 + k
                        T = pair * NT + t
                        dve.wait_ge(l3_mm, after(T))
                        dve.wait_ge(out_dma[k], (pair * (NT // 2) + i + 1) * 16)
                        dve.scalar_tensor_tensor(out=img(OBUF[:, k, :]), in0=img(PSUM[:, k, :]), scalar=SM[:, 8:9],
                                                 in1=xch(t), op0=ALU.add, op1=ALU.add).then_inc(l3_o, 1)

        @block.gpsimd
        def _(pool):
            credit(pool, ln0_yb)
            credit(pool, df_a, sc_delta, sc_u, by=1)
            pool.memset(PAD[:, :, :], 0.0).then_inc(border, 1)
            with pool.Fori(0, PAIRS) as pair:
                with pool.Fori(0, NT // 2) as i:
                    for k in range(2):
                        t = i * 2 + k
                        pool.wait_ge(ln0_y, after(pair * NT + t))
                        if k == 0:
                            pool.wait_ge(border, pair * 2 + 1)
                        pool.tensor_tensor(pch(t), img(n_y[:, k, :]),
                                           vc("ln_b").unsqueeze(2).broadcast_to([P, ROWS, W]), ALU.add).then_inc(ln0_yb, 1)
                pool.wait_ge(d1_act, (pair + 1) * NT + CREDIT)
                settle(pool)
                pool.memset(PAD[:, XBASE + H:XBASE + H + 1, :], 0.0).then_inc(border, 1)
                with pool.Fori(0, NT) as t:
                    T = pair * NT + t
                    for j in range(1, 9):
                        pool.wait_ge(df_p, T * 9 + (j + 2))
                        pool.wait_ge(df_a, T * 8 + j)
                        pool.tensor_tensor(XS, XS, PRD[:, j % 2, :], ALU.add).then_inc(df_a, 1)
                    pool.wait_ge(sc_ln, T + 2)
                    pool.tensor_tensor(RL, RL, AB, ALU.add).then_inc(sc_delta, 1)
                    pool.wait_ge(sc_delta, T + 2)
                    pool.wait_ge(sc_h, T + 1)
                    pool.tensor_tensor(UU, RL, XS, ALU.mult).then_inc(sc_u, 1)
                pool.wait_ge(sc_x, (pair + 1) * NT + 1)
                settle(pool)
                pool.memset(PAD[:, BASE - 1:BASE, :], 0.0).then_inc(border, 1)

        @block.scalar
        def _(act):
            credit(act, ln0_xn, ln0_sq, ln0_ln, ln0_rs, sp_stage, sp_pixt, sp_exp, mh_exp, mh_ptc, o_at, l1_xn, in_xn,
                   d1_act, d2_xb, d2_sq, d2_ln, d2_rs, d2_g, l3_xn)
            credit(act, df_wt, sc_abs, sc_exp, sc_ln, sc_da, sc_sq, sc_lv, sc_rs, by=1)
            act.wait_ge(load, 16 * 7)
            act.wait_ge(const_dve, 5)
            act.activation(SM[:, 10:11], vc("A_logs"), ACT.Exp).then_inc(const_act, 1)

            def group_norm(n):
                act.wait_ge(gn_pe, n * 2 + 2)
                act.activation(SM[:, 6:7], PSUM[:, 7, 1:2], ACT.Sqrt, bias=GNE[:, 0:1]).then_inc(gn_act, 1)
                act.wait_ge(gn_dve, n * 5 + 5)

            def normed(t, o, s):
                act.activation(o, xch(t), ACT.Identity, bias=NM, scale=RSTD).then_inc(s, 1)

            with act.Fori(0, PAIRS) as pair:
                group_norm(pair * 4)
                with act.Fori(0, NT // 2) as i:
                    T = [pair * NT + i * 2 + k for k in range(2)]
                    for k in range(2):
                        act.wait_ge(ln0_cen, reuse(T[k]))
                        normed(i * 2 + k, img(n_xn[:, k, :]), ln0_xn)
                    for k in range(2):
                        act.wait_ge(ln0_cen, after(T[k]))
                        act.wait_ge(ln0_var, reuse(T[k]))
                        act.activation(n_sq[:, k, :], PSUM[:, k, :], ACT.Square).then_inc(ln0_sq, 1)
                    for k in range(2):
                        act.wait_ge(ln0_var, after(T[k]))
                        act.wait_ge(ln0_y, reuse(T[k]))
                        act.activation(n_rs[:, k, :], PSUM[:, 2 + k, :], ACT.Ln, bias=GNE[:, 1:2]).then_inc(ln0_ln, 1)
                    for k in range(2):
                        act.wait_ge(ln0_ln, after(T[k]))
                        act.activation(n_rs[:, k, :], n_rs[:, k, :], ACT.Exp, scale=-0.5).then_inc(ln0_rs, 1)
                act.wait_ge(ln0_yb, (pair + 1) * NT + CREDIT)
                settle(act)
                with act.Fori(0, NS // 2) as i:
                    S = [pair * NS + i * 2 + k for k in range(2)]
                    st = [i * 2 + k for k in range(2)]
                    for k in range(2):
                        act.wait_ge(sp_tr, reuse(S[k]))
                        act.activation(STG[:, k, :].rearrange("p (b r q) -> p b r q", b=NS, r=8),
                                       PAD[:, bass.ds(st[k] * 8 + BASE, 8), 1:1 + W].rearrange("p r (b q) -> p b r q", q=8),
                                       ACT.Identity).then_inc(sp_stage, 1)
                    for k in range(2):
                        act.wait_ge(sp_tr, after(S[k]))
                        act.wait_ge(sp_fold, reuse(S[k]))
                        act.activation(PIXT[:, k, :].rearrange("p (a b) -> p a b", a=2),
                                       PSUM[:, 2 + 2 * k:4 + 2 * k, :], ACT.Copy).then_inc(sp_pixt, 1)
                    for k in range(2):
                        act.wait_ge(sp_sub, after(S[k]))
                        act.activation(LG[:, k, :, :], LG[:, k, :, :], ACT.Exp, scale=C ** -0.5 / 64).then_inc(sp_exp, 1)
                act.wait_ge(mha_pe, pair * 3 + 1)
                act.activation(QB, PSUM[:, 0, 0:TOK], ACT.Copy)
                act.activation(KB, PSUM[:, 0, TOK:2 * TOK], ACT.Copy)
                act.activation(VB, PSUM[:, 1, 0:2 * P].rearrange("p (a b) -> p a b", a=2), ACT.Copy).then_inc(mha_act, 1)
                with act.Fori(0, NH // 2) as i:
                    N = [pair * NH + i * 2 + k for k in range(2)]
                    for k in range(2):
                        act.wait_ge(mh_nmx, after(N[k]))
                        act.wait_ge(mh_pt, reuse(N[k]))
                        for h in range(2):
                            ins = act.activation(PB[:, k, h, :], PSUM[:, 2 + k, h * TOK:(h + 1) * TOK], ACT.Exp,
                                                 bias=MHS[:, k, 2 + h:3 + h], scale=HD ** -0.5,
                                                 accum_out=MHS[:, k, 4 + h:5 + h])
                        ins.then_inc(mh_exp, 1)
                    for k in range(2):
                        act.wait_ge(mh_pt, after(N[k]))
                        act.wait_ge(mh_pv, reuse(N[k]))
                        act.activation(PTB[:, k, :, :], PSUM[:, 4 + k, :].rearrange("p (a b) -> p a b", a=2),
                                       ACT.Copy).then_inc(mh_ptc, 1)
                act.wait_ge(mha_pe, pair * 3 + 2)
                act.activation(OB, PSUM[:, 7, 0:TOK], ACT.Copy).then_inc(mha_act, 1)
                act.wait_ge(so_dve, pair * 4 + 4)
                settle(act)
                with act.Fori(0, NS // 2) as i:
                    S = [pair * NS + i * 2 + k for k in range(2)]
                    for k in range(2):
                        act.wait_ge(o_tr, after(S[k]))
                        act.wait_ge(o_mm, reuse(S[k]))
                        act.activation(WST[:, k, :].unsqueeze(1), STT[:, bass.ds(i * 2 + k, 1), :], ACT.Identity)
                        act.activation(ATB[:, k, :].rearrange("p (a b) -> p a b", a=2),
                                       PSUM[:, 2 * k:2 * k + 2, :], ACT.Copy).then_inc(o_at, 1)
                group_norm(pair * 4 + 1)
                with act.Fori(0, NT) as t:
                    normed(t, pch(t), l1_xn)
                act.wait_ge(rt_dve, pair * 10 + 5)
                act.activation(RW, RW, ACT.Sigmoid).then_inc(rt_act, 1)
                group_norm(pair * 4 + 2)
                with act.Fori(0, NT // 2) as i:
                    for k in range(2):
                        t = i * 2 + k
                        act.wait_ge(in_mm, reuse(pair * NT + t))
                        normed(t, img(i_xn[:, k, :]), in_xn)
                with act.Fori(0, NT // 2) as i:
                    for k in range(2):
                        t = i * 2 + k
                        act.wait_ge(d1_mm, after(pair * NT + t))
                        act.activation(pch(t, XBASE), img(PSUM[:, k, :]), ACT.Silu, bias=vc("conv2d_b")).then_inc(d1_act, 1)
                with act.Fori(0, NT // 2) as i:
                    T = [pair * NT + i * 2 + k for k in range(2)]
                    for k in range(2):
                        act.wait_ge(d2_mm, after(T[k]))
                        act.wait_ge(d2_cen, reuse(T[k]))
                        act.activation(d_xb[:, k, :], PSUM[:, k, :], ACT.Identity, bias=vc("dw_b")).then_inc(d2_xb, 1)
                    for k in range(2):
                        act.wait_ge(d2_cen, after(T[k]))
                        act.wait_ge(d2_var, reuse(T[k]))
                        act.activation(d_sq[:, k, :], PSUM[:, 2 + k, :], ACT.Square).then_inc(d2_sq, 1)
                    for k in range(2):
                        act.wait_ge(d2_var, after(T[k]))
                        act.wait_ge(d2_y, reuse(T[k]))
                        act.activation(d_rs[:, k, :], PSUM[:, 4 + k, :], ACT.Ln, bias=GNE[:, 1:2]).then_inc(d2_ln, 1)
                    for k in range(2):
                        act.wait_ge(d2_ln, after(T[k]))
                        act.activation(d_rs[:, k, :], d_rs[:, k, :], ACT.Exp, scale=-0.5).then_inc(d2_rs, 1)
                    for k in range(2):
                        act.wait_ge(d2_y, after(T[k]))
                        act.activation(d_y[:, k, :], d_y[:, k, :], ACT.Gelu, bias=vc("dw_ln_b")).then_inc(d2_g, 1)
                with act.Fori(0, NT) as t:
                    T = pair * NT + t
                    act.wait_ge(df_tr, T + 2)
                    act.wait_ge(df_w, T * 9 + 1)
                    act.activation(WT[0:9 * SG, :], PSUM[0:9 * SG, 5, :], ACT.Copy).then_inc(df_wt, 1)
                    act.wait_ge(sc_zbc, T + 2)
                    act.wait_ge(sc_u, T + 1)
                    act.activation(AB, PSUM[:, 2, :], ACT.Abs, bias=vc("dt_b")).then_inc(sc_abs, 1)
                    act.activation(RL, PSUM[:, 2, :], ACT.Relu, bias=vc("dt_b"))
                    act.wait_ge(sc_abs, T + 2)
                    act.activation(AB, AB, ACT.Exp, scale=-1.0).then_inc(sc_exp, 1)
                    act.wait_ge(sc_exp, T + 2)
                    act.activation(AB, AB, ACT.Ln, bias=1.0).then_inc(sc_ln, 1)
                    act.wait_ge(sc_delta, T + 2)
                    act.wait_ge(sc_h, T + 1)
                    act.activation(DA, RL, ACT.Exp, scale=SM[:, 9:10]).then_inc(sc_da, 1)
                    act.wait_ge(sc_cen, T + 2)
                    act.activation(SQ2, PSUM[:, 5, :], ACT.Square).then_inc(sc_sq, 1)
                    act.wait_ge(sc_var, T + 2)
                    act.wait_ge(sc_t, T + 1)
                    act.activation(RS2, PSUM[:, 7, :], ACT.Ln, bias=GNE[:, 1:2]).then_inc(sc_lv, 1)
                    act.wait_ge(sc_lv, T + 2)
                    act.activation(RS2, RS2, ACT.Exp, scale=-0.5).then_inc(sc_rs, 1)
                group_norm(pair * 4 + 3)
                act.wait_ge(border, pair * 2 + 3)
                settle(act)
                with act.Fori(0, NT) as t:
                    normed(t, pch(t), l3_xn)

        @block.tensor
        def _(pe):
            credit(pe, ln0_cen, ln0_var, sp_lgt, sp_tr, sp_fold, mh_s, mh_pt, mh_pv, o_tr, o_mm, l1_mm, in_mm, d1_mm,
                   d2_mm, d2_cen, d2_var, d2_off, l3_mm)
            credit(pe, df_tr, df_w, sc_zbc, sc_cen, sc_var, by=1)
            pe.reg_mov(far_pe_turn, 0)
            pe.wait_ge(load, 16 * 7)
            pe.wait_ge(const_dve, 5)
            pe.matmul(PSUM[:, 0, 0:C], DTS[:, 0:2 * C], DTS[:, 2 * C:3 * C], start=True, stop=True)
            pe.matmul(PSUM[:, 1, 0:1], PLAIN[:, :], vc("out_ln_b"), start=True, stop=True)
            pe.matmul(PSUM[:, 2, 0:P], cs("center"), WOUT[:, :], start=True, stop=True).then_inc(const_pe, 1)
            pe.wait_ge(const_ready, 1)

            def group_norm(n):
                pe.wait_ge(gn_dve, n * 5 + 1)
                pe.matmul(PSUM[:, 7, 0:1], cs("pair"), SM[:, 0:1], start=True, stop=True).then_inc(gn_pe, 1)
                pe.wait_ge(gn_dve, n * 5 + 3)
                pe.matmul(PSUM[:, 7, 1:2], cs("pair"), SM[:, 3:4], start=True, stop=True).then_inc(gn_pe, 1)

            def conv(k, w, t, base=BASE):
                for j, (dy, dx) in enumerate(TAPS):
                    ins = pe.matmul(img(PSUM[:, k, :]), w[:, j, :], pch(t, base, dy, dx), start=(j == 0), stop=(j == 8))
                return ins

            with pe.Fori(0, PAIRS) as pair:
                group_norm(pair * 4)
                with pe.Fori(0, NT // 2) as i:
                    T = [pair * NT + i * 2 + k for k in range(2)]
                    for k in range(2):
                        pe.wait_ge(ln0_xn, after(T[k]))
                        pe.wait_ge(ln0_y, reuse(T[k]))
                        pe.matmul(PSUM[:, k, :], cs("center"), n_xn[:, k, :], start=True, stop=True).then_inc(ln0_cen, 1)
                    for k in range(2):
                        pe.wait_ge(ln0_sq, after(T[k]))
                        pe.wait_ge(ln0_ln, reuse(T[k]))
                        pe.matmul(PSUM[:, 2 + k, :], cs("mean"), n_sq[:, k, :], start=True, stop=True).then_inc(ln0_var, 1)
                pe.wait_ge(tok_dve, (pair + 1) * 2 * NS)
                settle(pe)
                with pe.Fori(0, NS // 2) as i:
                    S = [pair * NS + i * 2 + k for k in range(2)]
                    for k in range(2):
                        pe.wait_ge(sp_stage, after(S[k]))
                        pe.wait_ge(sp_log, reuse(S[k]))
                        for j in range(8):
                            rhs = STB[:, bass.ds(i * 2 + k, 3), :, 2 * j:2 * j + 4].rearrange("p r s c -> p s r c")
                            ins = pe.matmul(PSUM[:, k, j * 24:(j + 1) * 24].rearrange("p (s r c) -> p s r c", s=2, r=3),
                                            STG[:, k, j * P:(j + 1) * P], rhs, start=True, stop=True)
                        ins.then_inc(sp_lgt, 1)
                        pe.wait_ge(sp_pixt, reuse(S[k]))
                        for j in range(8):
                            ins = pe.transpose(PSUM[:, 2 + 2 * k + j // 4, (j % 4) * P:(j % 4 + 1) * P],
                                               STG[:, k, j * P:(j + 1) * P], ident)
                        ins.then_inc(sp_tr, 1)
                    for k in range(2):
                        pe.wait_ge(sp_e, after(S[k]))
                        pe.wait_ge(sp_pixt, after(S[k]))
                        pe.wait_ge(sp_acc, reuse(S[k]))
                        for j in range(8):
                            pe.matmul(PSUM[:, 6 + k, 0:P], PIXT[:, k, j * P:(j + 1) * P], EXPD[:, k, j, :],
                                      start=(j == 0), stop=(j == 7))
                        for j in range(8):
                            ins = pe.matmul(PSUM[:, 6 + k, P:2 * P], cs("one"), EXPD[:, k, j, :],
                                            start=(j == 0), stop=(j == 7))
                        ins.then_inc(sp_fold, 1)
                pe.wait_ge(sf_dve, pair * 3 + 3)
                pe.matmul(PSUM[:, 0, 0:TOK], WQ[:, :], SFC, start=True, stop=True)
                pe.matmul(PSUM[:, 0, TOK:2 * TOK], WK[:, :], SFC, start=True, stop=True)
                for h in range(2):
                    ins = pe.matmul(PSUM[:, 1, h * P:(h + 1) * P], SFC[:, h * P:(h + 1) * P], WV[:, :],
                                    start=True, stop=True)
                ins.then_inc(mha_pe, 1)
                pe.wait_ge(mha_act, pair * 2 + 1)
                pe.matmul(PSUM[:, 7, 0:TOK], cs("zero"), SFC, start=True, stop=False, skip_group_check=True)
                with pe.Fori(0, NH // 2) as i:
                    N = [pair * NH + i * 2 + k for k in range(2)]
                    for k in range(2):
                        pe.wait_ge(mh_qm, after(N[k]))
                        pe.wait_ge(mh_exp, reuse(N[k]))
                        for h in range(2):
                            ins = pe.matmul(PSUM[:, 2 + k, h * TOK:(h + 1) * TOK], QM[:, k, h * P:(h + 1) * P], KB,
                                            start=True, stop=True)
                        ins.then_inc(mh_s, 1)
                    for k in range(2):
                        pe.wait_ge(mh_pn, after(N[k]))
                        pe.wait_ge(mh_ptc, reuse(N[k]))
                        for kh in range(2):
                            for qh in range(2):
                                ins = pe.transpose(PSUM[:, 4 + k, (kh * 2 + qh) * P:(kh * 2 + qh + 1) * P],
                                                   PB[:, k, qh, kh * P:(kh + 1) * P], ident)
                        ins.then_inc(mh_pt, 1)
                    for k in range(2):
                        pe.wait_ge(mh_ptc, after(N[k]))
                        pe.wait_ge(mh_vm, after(N[k]))
                        for kh in range(2):
                            ins = pe.matmul(PSUM[:, 7, 0:TOK], VM[:, k, kh, :], PTB[:, k, kh, :],
                                            start=False, stop=False, skip_group_check=True)
                        ins.then_inc(mh_pv, 1)
                pe.matmul(PSUM[:, 7, 0:TOK], cs("zero"), KB, start=False, stop=True,
                          skip_group_check=True).then_inc(mha_pe, 1)
                pe.wait_ge(mha_act, pair * 2 + 2)
                pe.matmul(PSUM[:, 6, 0:TOK], WPROJ[:, :], OB, start=True, stop=True).then_inc(mha_pe, 1)
                pe.wait_ge(so_dve, pair * 4 + 3)
                for j in range(NS):
                    ins = pe.transpose(PSUM[:, j // 4, (j % 4) * P:(j % 4 + 1) * P], SFB[:, j, :], ident)
                ins.then_inc(so_pe, 1)
                with pe.Fori(0, NS // 2) as i:
                    S = [pair * NS + i * 2 + k for k in range(2)]
                    for k in range(2):
                        pe.wait_ge(o_e, after(S[k]))
                        pe.wait_ge(o_at, reuse(S[k]))
                        for j in range(8):
                            ins = pe.transpose(PSUM[:, 2 * k + j // 4, (j % 4) * P:(j % 4 + 1) * P], EXPD[:, k, j, :], ident)
                        ins.then_inc(o_tr, 1)
                    for k in range(2):
                        pe.wait_ge(o_at, after(S[k]))
                        pe.wait_ge(o_x, reuse(S[k]))
                        for j in range(2):
                            ins = pe.matmul(PSUM[:, 4 + 2 * k + j, :], WST[:, k, :], ATB[:, k, j * CH:(j + 1) * CH],
                                            start=True, stop=True)
                        ins.then_inc(o_mm, 1)
                group_norm(pair * 4 + 1)
                pe.wait_ge(l1_pool, pair * (NS + 1) + NS)
                for h in range(2):
                    ins = pe.matmul(PSUM[:, 0, h * 32:(h + 1) * 32], POOLED[:, h * P:(h + 1) * P],
                                    WCONV[:, :, :].rearrange("p a b -> p (a b)"), start=True, stop=True)
                ins.then_inc(rt_pe, 1)
                pe.wait_ge(rt_dve, pair * 10 + 2)
                pe.wait_ge(fc_in, pair * 16 + 16)
                for o in range(RED):
                    for h in range(2):
                        ins = pe.matmul(PSUM[0:2, 1, 0:FC], RB[:, h, :].rearrange("p (s o) -> p o s", s=2)[:, o, :],
                                        FCT[:, o, h, :], start=(o + h == 0), stop=(o == RED - 1 and h == 1))
                ins.then_inc(rt_pe, 1)
                pe.wait_ge(rt_dve, pair * 10 + 3)
                for s in range(2):
                    for e in range(EXPERTS):
                        ins = pe.matmul(PSUM[s * C:(s + 1) * C, 2, e:e + 1], FS[0:2, e * C:(e + 1) * C],
                                        ident[0:2, s:s + 1], start=True, stop=True)
                ins.then_inc(rt_pe, 1)
                pe.wait_ge(rt_dve, pair * 10 + 10)
                for j in range(9):
                    ins = pe.transpose(PSUM[:, 3 + j // 4, (j % 4) * P:(j % 4 + 1) * P], WE[:, j, :], ident)
                ins.then_inc(rt_pe, 1)
                pe.wait_ge(l1_pool, (pair + 1) * (NS + 1))
                settle(pe)
                with pe.Fori(0, NT // 2) as i:
                    for k in range(2):
                        t = i * 2 + k
                        pe.wait_ge(l1_x, reuse(pair * NT + t))
                        conv(k, WL1, t).then_inc(l1_mm, 1)
                group_norm(pair * 4 + 2)
                with pe.Fori(0, NT // 2) as i:
                    for k in range(2):
                        T = pair * NT + i * 2 + k
                        pe.wait_ge(in_xn, after(T))
                        pe.wait_ge(in_cp, reuse(T))
                        pe.matmul(PSUM[:, k, :], WIN[:, :], i_xn[:, k, :], start=True, stop=True).then_inc(in_mm, 1)
                pe.wait_ge(in_cp, (pair + 1) * NT + CREDIT)
                settle(pe)
                with pe.Fori(0, NT // 2) as i:
                    for k in range(2):
                        t = i * 2 + k
                        pe.wait_ge(d1_act, reuse(pair * NT + t))
                        conv(k, WDW1, t).then_inc(d1_mm, 1)
                pe.wait_ge(border, pair * 2 + 2)
                settle(pe)
                with pe.Fori(0, NT // 2) as i:
                    T = [pair * NT + i * 2 + k for k in range(2)]
                    for k in range(2):
                        pe.wait_ge(d2_xb, reuse(T[k]))
                        conv(k, WDW2, i * 2 + k, XBASE).then_inc(d2_mm, 1)
                    for k in range(2):
                        pe.wait_ge(d2_xb, after(T[k]))
                        pe.wait_ge(d2_y, reuse(T[k]))
                        pe.matmul(PSUM[:, 2 + k, :], cs("center"), d_xb[:, k, :], start=True, stop=True).then_inc(d2_cen, 1)
                    for k in range(2):
                        pe.wait_ge(d2_sq, after(T[k]))
                        pe.wait_ge(d2_ln, reuse(T[k]))
                        pe.matmul(PSUM[:, 4 + k, :], cs("mean"), d_sq[:, k, :], start=True, stop=True).then_inc(d2_var, 1)
                    for k in range(2):
                        pe.wait_ge(d2_g, after(T[k]))
                        pe.wait_ge(d2_o, reuse(T[k]))
                        for y in range(ROWS):
                            ins = pe.matmul(PSUM[:, 6 + k, y * 16:(y + 1) * 16], d_y[:, k, y * W:(y + 1) * W],
                                            WOFF[:, :, :, :].rearrange("p a s g -> p (a s g)"), start=True, stop=True)
                        ins.then_inc(d2_off, 1)
                pe.wait_ge(rad_dve, pair * 5 + 1)
                pe.matmul(PSUM[0:1, 0, 0:P], SM[:, 16:17], ident, start=True, stop=True).then_inc(rad_pe, 1)
                pe.wait_ge(rad_dve, pair * 5 + 2)
                pe.matmul(PSUM[:, 0, P:P + 1], cs("one")[0:1, :], SM[0:1, 17:18], start=True, stop=True).then_inc(rad_pe, 1)
                pe.wait_ge(rad_dve, pair * 5 + 5)
                settle(pe)
                reach = pe.value_load(RI[0:1, 0:1], min_val=0, max_val=MAXR)
                pe.wait_ge(sel_in, pair * 16 + 16)
                settle(pe)
                with pe.Fori(0, NT) as t:
                    T = pair * NT + t
                    pe.wait_ge(df_w9, T + 2)
                    pe.wait_ge(sc_sq, T + 1)
                    for y in range(ROWS):
                        ins = pe.transpose(PSUM[0:9 * SG, 5, y * W:(y + 1) * W],
                                           W9[:, y, :, :].rearrange("p d g -> p (d g)"), ident)
                    ins.then_inc(df_tr, 1)
                    pe.wait_ge(df_wt, T + 2)
                    for j in range(9):
                        pe.wait_ge(df_p, T * 9 + (j if j > 1 else 1))
                        pe.matmul(PSUM[:, j % 2, :], SEL[0:9 * SG, j, :], WT[0:9 * SG, :],
                                  start=True, stop=True).then_inc(df_w, 1)
                    with pe.If(reach > 0):
                        far_pe(pe, t, reach)
                    pe.wait_ge(xs_ready, T + 2)
                    pe.wait_ge(sc_ln, T + 1)
                    pe.wait_ge(sc_hc, T + 1)
                    pe.matmul(PSUM[:, 2, :], WZ[:, :], XS, start=True, stop=True)
                    pe.matmul(PSUM[:, 3, :], WB[:, :], XS, start=True, stop=True)
                    pe.matmul(PSUM[:, 4, :], WC[:, :], XS, start=True, stop=True).then_inc(sc_zbc, 1)
                    pe.wait_ge(sc_y, T + 2)
                    pe.wait_ge(sc_t, T + 1)
                    pe.matmul(PSUM[:, 5, :], cs("center"), YY, start=True, stop=True)
                    pe.matmul(PSUM[:, 6, :], WOUT2[:, :], YY, start=True, stop=True).then_inc(sc_cen, 1)
                    pe.wait_ge(sc_sq, T + 2)
                    pe.matmul(PSUM[:, 7, :], cs("mean"), SQ2, start=True, stop=True).then_inc(sc_var, 1)
                group_norm(pair * 4 + 3)
                pe.wait_ge(l3_xn, (pair + 1) * NT + CREDIT)
                settle(pe)
                with pe.Fori(0, NT // 2) as i:
                    for k in range(2):
                        t = i * 2 + k
                        pe.wait_ge(l3_o, reuse(pair * NT + t))
                        conv(k, WL3, t).then_inc(l3_mm, 1)


def constants():
    import numpy as np
    c = np.zeros((P, NCST), np.float32)
    i = np.arange(P)

    def put(name, a):
        at, n = CST[name]
        c[:, at:at + n] = a

    same = (i[:, None] // C == i[None, :] // C).astype(np.float32)
    put("ident", np.eye(P))
    put("center", np.eye(P) - same / C)
    put("mean", same / C)
    put("pair", (i[:, None] // 2 == i[None, :] // 2) * 0.5)
    put("one", 1.0)
    put("group4", i[:, None] // 4 == i[None, :] // 4)
    put("mask3", same * ((i[:, None] - i[None, :]) % 4 == 0))
    put("headcol", i[:, None] // HD == np.arange(NH)[None, :])
    put("headrow", (np.arange(2 * P - HD)[None, :] // HD == (P - HD) // HD) * np.ones((P, 1)))
    put("shift", np.array([[-1.0, 0.0, 1.0]]))
    put("col", i[:, None])
    put("row", np.arange(H)[None, :])
    return c


def selection():
    import numpy as np
    r, t, c = np.ogrid[0:9 * SG, 0:9, 0:P]
    return ((r // SG == t) & (r % SG == c // (C // GROUP))).astype(np.float32)


def kernel(**a):
    import numpy as np
    import concourse.bacc as bacc
    from concourse.bass_utils import run_bass_kernel_spmd

    f = {n: np.asarray(v) for n, v in a.items()}
    g = {n: f[k] for n, k in (
        ("ln_w", "L0_conv_ln_w"), ("ln_b", "L0_conv_ln_b"), ("proj_b", "L0_conv_proj_b"), ("conv2d_b", "L2_conv_conv2d_b"),
        ("dw_b", "L2_conv_dw_b"), ("dw_ln_g", "L2_conv_dw_ln_g"), ("dw_ln_b", "L2_conv_dw_ln_b"), ("dt_b", "L2_conv_dt_b"),
        ("A_logs", "L2_conv_A_logs"), ("Ds", "L2_conv_Ds"), ("out_ln_g", "L2_conv_out_ln_g"),
        ("out_ln_b", "L2_conv_out_ln_b"))}
    g["fc_b"] = f["L1_conv_fc_b"].reshape(EXPERTS, C).T
    g["conv2d_w"] = f["L2_conv_conv2d_w"].reshape(C, 9)
    g["dw_w"] = f["L2_conv_dw_w"].reshape(C, 9)
    g["experts"] = f["L1_conv_w_experts"].reshape(EXPERTS, C, 36).transpose(1, 0, 2)
    g["l3_b"] = f["L3_conv_b"]
    vec = np.concatenate([g[n].reshape(C, VEC[n][1]) for n in VEC], axis=1)
    qkv = f["L0_conv_qkv_w"].reshape(3, C, C)
    m = {"q": qkv[0].T, "k": qkv[1].T, "v": qkv[2].T, "proj": f["L0_conv_proj_w"].T, "in_proj": f["L2_conv_in_proj_w"].T,
         "off": f["L2_conv_off_w"].T, "out_proj": f["L2_conv_out_proj_w"].T, "conv": f["L1_conv_conv_w"].reshape(RED, C).T,
         "x_proj": f["L2_conv_x_proj_w"].T, "w1": f["L3_conv_w1"].T,
         "w3": f["L3_conv_w3"].reshape(C, C, 9).transpose(1, 2, 0).reshape(C, 9 * C)}
    mat = np.concatenate([m[n] for n in MAT], axis=1)
    xp = f["L2_conv_x_proj_w"][:DT_RANK]
    dts = np.concatenate([xp, xp, f["L2_conv_dt_w"].T], axis=1)
    off_b = f["L2_conv_off_b"].reshape(GROUP, 2).T.reshape(2, 1, GROUP)
    off_b = np.broadcast_to(off_b, (ROWS, 2, 2, GROUP)).reshape(-1)
    rows = np.concatenate([f["L1_conv_conv_b"], f["L1_conv_conv_b"], off_b])
    rows = np.broadcast_to(rows[None, :], (P, rows.size))
    fc = f["L1_conv_fc_w"].reshape(FC, RED, 2, P).transpose(3, 1, 2, 0)
    arrays = {"x": f["x"].reshape(BATCH * C, H, W), "vec": vec, "mat": mat, "dts": dts, "rows": rows, "fc": fc, "sel": selection(),
              "cst": constants()}
    arrays = {n: np.ascontiguousarray(v) for n, v in arrays.items()}
    nc = bacc.Bacc("TRN2", target_bir_lowering=False, num_devices=1)
    aps = [nc.dram_tensor(n, v.shape, mybir.dt.from_np(v.dtype), kind="ExternalInput").ap() for n, v in arrays.items()]
    out = nc.dram_tensor("out", (BATCH * C, H, W), F32, kind="ExternalOutput").ap()
    program(nc, *aps, out)
    r = run_bass_kernel_spmd(nc, [arrays], core_ids=[0])
    return r.results[0]["out"].reshape(BATCH, C, H, W)
```

```python
from contextlib import ExitStack

import concourse.bass as bass
from concourse import mybir

F32 = mybir.dt.float32
BF16 = mybir.dt.bfloat16
I32 = mybir.dt.int32
ALU = mybir.AluOpType
ACT = mybir.ActivationFunctionType
AX = mybir.AxisListType

BATCH, C, H, W = 4, 64, 128, 128
P = 2 * C
PAIRS = BATCH // 2
PIX = H * W
ROWS = 4
CH = ROWS * W
NT = H // ROWS
NS = H // 8
TW = NS + 2
TOK = NS * NS
HEADS, HD = 8, 8
NH = 2 * HEADS
GROUP = 4
SG = 2 * GROUP
EXPERTS, RED, FC = 4, 16, 256
DT_RANK = 8
PW = W + 2
BASE = 5
XBASE = 1
PROWS = H + BASE + 1
GN_EPS, LN_EPS = 1e-5, 1e-6
MAXR = 128
TAPS = [(dy, dx) for dy in (-1, 0, 1) for dx in (-1, 0, 1)]
NTAP = len(TAPS)
HALF = 5
PARTS = 3
WROWS = PARTS * HALF * SG
DW1_VECTOR, DW2_VECTOR = 4, 5
PE_TAPS = 4

VEC = {}
_at = 0
for _name, _n in (("ln_w", 1), ("ln_b", 1), ("proj_b", 1), ("conv2d_b", 1), ("dw_b", 1), ("dw_ln_g", 1),
                  ("dw_ln_b", 1), ("dt_b", 1), ("A_logs", 1), ("Ds", 1), ("out_ln_g", 1), ("out_ln_b", 1),
                  ("fc_b", EXPERTS), ("conv2d_w", 9), ("dw_w", 9), ("experts", EXPERTS * 36), ("l3_b", C)):
    VEC[_name] = (_at, _n)
    _at += _n
NVEC = _at
MAT = {}
_at = 0
for _name, _n in (("q", C), ("k", C), ("v", C), ("proj", C), ("in_proj", C), ("off", 2 * GROUP), ("out_proj", C),
                  ("conv", RED), ("x_proj", DT_RANK + 2), ("w1", C), ("w3", 9 * C)):
    MAT[_name] = (_at, _n)
    _at += _n
NMAT = _at
CST = {}
_at = 0
for _name, _n in (("ident", P), ("center", P), ("mean", P), ("pair", P), ("one", P), ("zero", P), ("group4", P),
                  ("mask3", P), ("same", P), ("headcol", NH), ("headrow", 2 * P - HD), ("shift", 3), ("col", 1), ("row", H)):
    CST[_name] = (_at, _n)
    _at += _n
NCST = _at

NREG = 10032
CREDIT = 2


def after(t):
    return t + 1 + CREDIT


def reuse(t):
    return t - 1 + CREDIT


def program(nc, x, vec, mat, dts, rows, fc, sel, far_sel, cst, out):
    ctx = ExitStack()
    with ctx:
        def sb(name, shape, dt=F32):
            return ctx.enter_context(nc.sbuf_tensor(name, shape, dt))

        def sem(name):
            return ctx.enter_context(nc.semaphore(name))

        X = sb("X", [P, H, W])
        PAD = sb("PAD", [P, PROWS, PW])
        VECS = sb("VECS", [P, NVEC])
        DTS = sb("DTS", [DT_RANK, 3 * C])
        ROWV = sb("ROWV", [P, 2 * RED + 4 * 16])
        CSTS = sb("CSTS", [P, NCST])
        WQ, WK, WV, WPROJ, WIN, WZ, WB, WC = (sb(n, [P, P]) for n in
            ("WQ", "WK", "WV", "WPROJ", "WIN", "WZ", "WB", "WC"))
        WOUT2, GNE = sb("WOUT2", [P, P]), sb("GNE", [P, 2])
        WOFF = sb("WOFF", [P, 2, 2, GROUP])
        WCONV = sb("WCONV", [P, 2, RED])
        WDW1 = sb("WDW1", [P, NTAP - DW1_VECTOR, P])
        WDW2 = sb("WDW2", [P, NTAP - DW2_VECTOR, P])
        WL3 = sb("WL3", [P, 9, P])
        WL1 = sb("WL1", [P, 9, P])
        STATS = sb("STATS", [P, NT, 6])
        SM = sb("SM", [P, 64])
        OUTB = sb("OUTB", [P, 1])
        SELB = sb("SELB", [WROWS, NTAP, P], BF16)
        FSEL = sb("FSEL", [ROWS * SG, ROWS, P])
        IDB = sb("IDB", [P, P], BF16)
        RI = sb("RI", [P, 1], I32)
        REG = sb("REG", [P, NREG])
        MATS = REG[:, 0:NMAT]
        PLAIN, NOT3, WOUT = (REG[:, NMAT + j * P:NMAT + (j + 1) * P] for j in range(3))
        SELF = REG[0:WROWS, NMAT + 3 * P:NMAT + 3 * P + NTAP * P]

        def cs(name):
            a, n = CST[name]
            return CSTS[:, a:a + n]

        def vc(name, j=0, n=1):
            a = VEC[name][0] + j
            return VECS[:, a:a + n]

        def mt(name, lo=0, hi=P):
            a, n = MAT[name]
            return MATS[lo:hi, a:a + n]

        ident = cs("ident")
        PSUM = ctx.enter_context(nc.psum_tensor("PSUM", [P, 8, 512], F32))

        class Region:
            def __init__(self):
                self.at = 0

            def take(self, *shape):
                n = 1
                for d in shape:
                    n *= d
                a = REG[:, self.at:self.at + n]
                self.at += n
                assert self.at <= NREG, self.at
                if len(shape) == 2:
                    a = a.rearrange("p (a b) -> p a b", a=shape[0])
                if len(shape) == 3:
                    a = a.rearrange("p (a b c) -> p a b c", a=shape[0], b=shape[1])
                if len(shape) == 4:
                    a = a.rearrange("p (a b c d) -> p a b c d", a=shape[0], b=shape[1], c=shape[2])
                return a

        r = Region()
        n_xn, n_sq, n_rs, n_y = (r.take(2, CH) for _ in range(4))
        n_cen = r.take(2, 2, CH)
        r = Region()
        AFF = r.take(NS, NS, 9)
        EXPD = r.take(2, 8, 2 * C)
        SFAS = r.take(2, TW * TW)
        STB = r.take(TW, 2, TW)
        both = r.at
        STG = r.take(2, 1024)
        PIXT = r.take(2, 1024)
        LG = r.take(2, NS, 9)
        SMX = STATS.rearrange("p t n -> p (t n)")[:, 0:6 * NS].rearrange("p (k j n) -> p k j n", k=2, j=3)
        r.at = both
        SFC, QB, KB, OB = (r.take(TOK) for _ in range(4))
        VB = r.take(2, P)
        QM = r.take(2, TOK)
        PB = r.take(2, 2, TOK)
        PTB = r.take(2, 2, TOK)
        VM = r.take(2, 2, P)
        MHS = r.take(2, 6)
        r.at = both - 2 * TW * TW
        SOP = r.take(TW, TW)
        SFB = r.take(NS, 2 * C)
        STT = r.take(NS, P)
        ATB = SFB.rearrange("p a b -> p (a b)").rearrange("p (k n) -> p k n", k=2)
        WST = r.take(2, P)
        r = Region()
        FCT = r.take(RED, 2, FC)
        POOLED = r.take(TOK)
        RB = r.take(2, 2 * RED)
        FS = r.take(FC)
        RW = r.take(EXPERTS)
        CW = r.take(36)
        WE = r.take(9, P)
        r = Region()
        OFF = r.take(H, 16)
        l2at = r.at
        i_xn = r.take(2, CH)
        r.at = l2at
        d_acc, d_xb, d_sq, d_rs, d_y = (r.take(2, CH) for _ in range(5))
        r.at = l2at
        MXR = r.take(P)
        r.at = l2at
        HT = r.take(3, 64)
        W9 = r.take(ROWS, 2 * HALF, SG)
        WPART = r.take(ROWS, WROWS).bitcast(BF16).rearrange("p y (h n) -> p y h n", h=2)
        WTB = r.take(2, CH).bitcast(BF16)
        PRD = r.take(2, CH)
        FAR = r.take(3, ROWS * SG)
        CUR = r.take(4)
        FWT = r.take(W)
        XS = r.take(2, CH)
        AB, RL, DA, UU, HH, YY, RS2 = (r.take(CH) for _ in range(7))
        ACC, ZB, BB, CB, MB, OB2 = 2, 3, 4, 5, 6, 7
        TB = PSUM[0:WROWS, ACC, :].bitcast(BF16)
        r = Region()
        OBUF = r.take(2, CH)

        load = sem("load")
        const_ready = sem("const_ready")
        settled = sem("settled")
        const_pe = sem("const_pe")
        const_act = sem("const_act")
        const_dve = sem("const_dve")
        x_in = [sem(f"x_in{j}") for j in range(4)]
        stats_done = sem("stats_done")
        gn_dve, gn_pe, gn_act = sem("gn_dve"), sem("gn_pe"), sem("gn_act")
        names = {}

        def steps(*ns):
            for n in ns:
                names[n] = sem(n)
            return [names[n] for n in ns]

        ln0_xn, ln0_cen, ln0_cc, ln0_sq, ln0_var, ln0_ln, ln0_rs, ln0_y, ln0_yb = steps(
            "ln0_xn", "ln0_cen", "ln0_cc", "ln0_sq", "ln0_var", "ln0_ln", "ln0_rs", "ln0_y", "ln0_yb")
        (sp_stage, sp_lgt, sp_tr, sp_pixt, sp_log, sp_mx, sp_sub, sp_exp, sp_sum, sp_rec, sp_aff, sp_e, sp_fold,
         sp_acc) = steps("sp_stage", "sp_lgt", "sp_tr", "sp_pixt", "sp_log", "sp_mx", "sp_sub", "sp_exp", "sp_sum",
                         "sp_rec", "sp_aff", "sp_e", "sp_fold", "sp_acc")
        tok_dve, tok_zero = sem("tok_dve"), sem("tok_zero")
        sf_dve = sem("sf_dve")
        mha_pe, mha_act = sem("mha_pe"), sem("mha_act")
        mh_qm, mh_s, mh_mx, mh_nmx, mh_exp, mh_rec, mh_pn, mh_pt, mh_ptc, mh_vm, mh_pv = steps(
            "mh_qm", "mh_s", "mh_mx", "mh_nmx", "mh_exp", "mh_rec", "mh_pn", "mh_pt", "mh_ptc", "mh_vm", "mh_pv")
        so_dve, so_pe, so_act, so_zero = sem("so_dve"), sem("so_pe"), sem("so_act"), sem("so_zero")
        o_e, o_tr, o_at, o_mm, o_x = steps("o_e", "o_tr", "o_at", "o_mm", "o_x")
        fc_in = sem("fc_in")
        l1_xn, l1_mm, l1_x = steps("l1_xn", "l1_mm", "l1_x")
        l1_pool = sem("l1_pool")
        rt_pe, rt_dve, rt_act = sem("rt_pe"), sem("rt_dve"), sem("rt_act")
        in_xn, in_mm, in_cp = steps("in_xn", "in_mm", "in_cp")
        d1_mm, d1_sum, d1_act = steps("d1_mm", "d1_sum", "d1_act")
        d1_tap, d2_tap = ([sem(f"{n}{k}") for k in range(2)] for n in ("d1_tap", "d2_tap"))
        border = sem("border")
        d2_mm, d2_xb, d2_cen, d2_sq, d2_var, d2_ln, d2_rs, d2_y, d2_g, d2_off, d2_o = steps(
            "d2_mm", "d2_xb", "d2_cen", "d2_sq", "d2_var", "d2_ln", "d2_rs", "d2_y", "d2_g", "d2_off", "d2_o")
        far_step, far_w, far_tr, far_wt, far_b = (sem(n) for n in ("far_step", "far_w", "far_tr", "far_wt", "far_b"))
        rad_dve, rad_pe = sem("rad_dve"), sem("rad_pe")
        (df_zero, df_ht, df_abs, df_hat, df_w9, df_hi, df_r1, df_mid, df_lo, df_tr, df_wt, df_w, df_p, df_acc, df_xs,
         df_add) = (sem(n) for n in ("df_zero", "df_ht", "df_abs", "df_hat", "df_w9", "df_hi", "df_r1", "df_mid", "df_lo",
                                     "df_tr", "df_wt", "df_w", "df_p", "df_acc", "df_xs", "df_add"))
        far_xs = sem("far_xs")
        (sc_z, sc_bc, sc_abs, sc_exp, sc_ln, sc_delta, sc_u, sc_da, sc_bx, sc_h, sc_hc, sc_y, sc_cen, sc_sq, sc_var,
         sc_lv, sc_rs, sc_t, sc_x) = (sem(n) for n in (
            "sc_z", "sc_bc", "sc_abs", "sc_exp", "sc_ln", "sc_delta", "sc_u", "sc_da", "sc_bx", "sc_h", "sc_hc",
            "sc_y", "sc_cen", "sc_sq", "sc_var", "sc_lv", "sc_rs", "sc_t", "sc_x"))
        l3_xn, l3_mm, l3_o = steps("l3_xn", "l3_mm", "l3_o")
        out_dma = [sem(f"out_dma{k}") for k in range(2)]

        def settle(eng):
            eng.sem_inc(settled, 1)

        far_dve_step, far_dve_turn = nc.vector.alloc_register("far_dve_step"), nc.vector.alloc_register("far_dve_turn")
        far_pe_turn = nc.tensor.alloc_register("far_pe_turn")
        far_pe_done = nc.tensor.alloc_register("far_pe_done")

        def credit(eng, *sems):
            for s in sems:
                eng.sem_inc(s, CREDIT)

        block = ctx.enter_context(nc.Block())

        def xch(t):
            return X[:, bass.ds(t * ROWS, ROWS), :]

        def pch(t, base=BASE, dy=0, dx=0):
            return PAD[:, bass.ds(t * ROWS + (base + dy), ROWS), 1 + dx:1 + dx + W]

        def img(a):
            return a.rearrange("p (r w) -> p r w", r=ROWS)

        def in_turn(eng, n, ahead, behind, step):
            lo = behind + behind % 2
            hi = n - ahead - (n - ahead) % 2

            def peeled(first, last):
                for i in range(first, last):
                    step(i, i % 2, lambda d: 0 <= i + d < n)

            peeled(-ahead, lo)
            with eng.Fori(lo // 2, hi // 2) as j:
                for b in range(2):
                    step(j * 2 + b, b, lambda d: True)
            peeled(hi, n + behind)

        NM, RSTD = SM[:, 4:5], SM[:, 5:6]

        @block.sync
        def _(sp):
            for lo in (0, C):
                sp.dma_start(VECS[lo:lo + C, :], vec).then_inc(load, 16)
                sp.dma_start(MATS[lo:lo + C, :], mat).then_inc(load, 16)
            sp.dma_start(DTS[:, :], dts).then_inc(load, 16)
            sp.dma_start(ROWV[:, :], rows).then_inc(load, 16)
            sp.dma_start(CSTS[:, :], cst).then_inc(load, 16)
            sp.dma_start(SELF, sel.rearrange("r t c -> r (t c)")).then_inc(load, 16)
            sp.dma_start(FSEL[:, :, :], far_sel).then_inc(load, 16)
            for k in range(2):
                sp.sem_inc(out_dma[k], 16)
            with sp.Fori(0, PAIRS) as pair:
                sp.wait_ge(l3_o, pair * NT + CREDIT)
                for j in range(4):
                    sp.dma_start(X[:, j * H // 4:(j + 1) * H // 4, :],
                                 x[bass.ds(pair * P, P), j * H // 4:(j + 1) * H // 4, :]).then_inc(x_in[j], 16)
                sp.wait_ge(o_x, pair * NS + NS + CREDIT)
                sp.dma_start(FCT, fc).then_inc(fc_in, 16)
                with sp.Fori(0, NT // 2) as i:
                    for k in range(2):
                        t = pair * NT + i * 2 + k
                        sp.wait_ge(l3_o, after(t))
                        sp.dma_start(out[bass.ds(pair * P, P), bass.ds((i * 2 + k) * ROWS, ROWS), :],
                                     img(OBUF[:, k, :])).then_inc(out_dma[k], 16)
            for k in range(2):
                sp.wait_ge(out_dma[k], 16 * (PAIRS * NT // 2 + 1))

        def expand(dve, k, st):
            a = AFF[:, bass.ds(st, 1), :, :].rearrange("p o (j s) (r c) -> p (o j) s r c", s=2, r=3)
            for b in range(2):
                for s in range(2):
                    first = EXPD[b * 64:b * 64 + 64, k, 0, s * C + b:s * C + b + 1]
                    v = bass.AP(first.tensor, first.offset, [list(first.ap[0]), [2 * C + 2, 8], [TW, 3], [1, 3]])
                    ins = dve.tensor_scalar(v, a[b * 64:b * 64 + 64, :, s, :, :], 1.0, None, ALU.mult)
            return ins

        def far_dve(dve, t, k, reach):
            oy, ox, fy = (FAR[:, j, :].rearrange("p (y g) -> p y g", y=ROWS) for j in range(3))

            def link(ins):
                ins.then_inc(far_step, 1)
                dve.reg_add(far_dve_step, far_dve_step, 1)
                dve.wait_ge(far_step, dve.snap(far_dve_step, min_val=1))

            def hat(a):
                link(dve.scalar_tensor_tensor(out=a, in0=a, scalar=-1.0, in1=a, op0=ALU.mult, op1=ALU.min))
                link(dve.tensor_scalar(a, a, 1.0, 0.0, ALU.add, ALU.max))

            def one_row(ys, e):
                ys = nc.s_assert_within(ys, 0, H - 1, skip_runtime_bounds_check_because="both branches were taken")
                link(dve.tensor_scalar(fy, oy, CUR[:, 0:1], None, ALU.subtract))
                hat(fy)
                dve.tensor_tensor(fy, fy, ox, ALU.mult).then_inc(far_w, 1)
                dve.reg_add(far_dve_turn, far_dve_turn, 1)
                turn = dve.snap(far_dve_turn, min_val=1)
                dve.wait_ge(far_tr, turn)
                dve.tensor_scalar(FWT[0:ROWS * SG, :], PSUM[0:ROWS * SG, ACC, 0:W], 1.0, None, ALU.mult).then_inc(far_wt, 1)
                dve.wait_ge(far_b, turn)
                src = PAD[:, :, :].rearrange("p r w -> p (r w)")[:, bass.ds(ys * PW + (e - reach) + (XBASE * PW + 1), W)]
                link(dve.tensor_tensor(img(PRD[:, 0, :]), img(PSUM[:, ZB, :]),
                                       src.unsqueeze(1).broadcast_to([P, ROWS, W]), ALU.mult))
                link(dve.tensor_tensor(XS[:, k, :], XS[:, k, :], PRD[:, 0, :], ALU.add))
                settle(dve)

            off = OFF[:, bass.ds(t * ROWS, ROWS), :].rearrange("p y (a g) -> p y a g", a=2)
            row = CST["row"][0]
            link(dve.memset(XS[:, k, :], 0.0))
            link(dve.tensor_tensor(oy, off[:, :, 1, :],
                                   CSTS[:, bass.ds(t * ROWS + row, ROWS)].unsqueeze(2).broadcast_to([P, ROWS, SG]), ALU.add))
            link(dve.tensor_scalar(CUR[:, 1:2], SM[:, 19:20], 1.0, None, ALU.mult))
            settle(dve)
            with dve.Fori(0, reach * 2 + 1) as e:
                link(dve.tensor_tensor(CUR[:, 2:3], cs("col"), CUR[:, 1:2], ALU.add))
                link(dve.tensor_scalar(CUR[:, 3:4], CUR[:, 2:3], 0.0, None, ALU.is_ge))
                link(dve.tensor_scalar(CUR[:, 2:3], CUR[:, 2:3], W - 1.0, None, ALU.is_le))
                link(dve.tensor_tensor(CUR[:, 2:3], CUR[:, 2:3], CUR[:, 3:4], ALU.mult))
                link(dve.tensor_scalar(ox, off[:, :, 0, :], CUR[:, 1:2], None, ALU.subtract))
                hat(ox)
                link(dve.tensor_scalar(ox, ox, CUR[:, 2:3], None, ALU.mult))
                link(dve.tensor_tensor(CUR[:, 0:1], CSTS[:, bass.ds(t * ROWS + row, 1)], SM[:, 19:20], ALU.add))
                settle(dve)
                with dve.Fori(0, reach * 2 + ROWS) as d:
                    ys = dve.snap(t * ROWS + d - reach)
                    with dve.If(ys >= 0):
                        with dve.If(ys < H):
                            one_row(ys, e)
                    link(dve.tensor_scalar(CUR[:, 0:1], CUR[:, 0:1], 1.0, None, ALU.add))
                link(dve.tensor_scalar(CUR[:, 1:2], CUR[:, 1:2], 1.0, None, ALU.add))
            dve.sem_inc(far_xs, 1)

        def far_pe(pe, t, reach):
            with pe.Fori(0, reach * 2 + 1) as _:
                with pe.Fori(0, reach * 2 + ROWS) as d:
                    ys = pe.snap(t * ROWS + d - reach)
                    with pe.If(ys >= 0):
                        with pe.If(ys < H):
                            pe.reg_add(far_pe_turn, far_pe_turn, 1)
                            turn = pe.snap(far_pe_turn, min_val=1)
                            pe.wait_ge(far_w, turn)
                            pe.transpose(PSUM[0:ROWS * SG, ACC, 0:P], FAR[:, 2, :], ident).then_inc(far_tr, 1)
                            pe.wait_ge(far_wt, turn)
                            for y in range(ROWS):
                                ins = pe.matmul(PSUM[:, ZB, y * W:(y + 1) * W], FSEL[:, y, :],
                                                FWT[0:ROWS * SG, :], start=True, stop=True)
                            ins.then_inc(far_b, 1)
            pe.reg_add(far_pe_done, far_pe_done, 1)
            pe.wait_ge(far_xs, pe.snap(far_pe_done, min_val=1))
            settle(pe)

        def pipeline(eng, step):
            in_turn(eng, NT, 2, 3, step)

        def turn(T, q):
            return T * NTAP + (q + 1 + CREDIT)

        def summed(T, m, n):
            return T * n + (m + 1 + CREDIT)

        PE_SUMS, POOL_SUMS = PE_TAPS, NTAP - 1 - PE_TAPS

        def product_buffer(q):
            return (q if q < PE_TAPS else q - 1) % 2

        assert (NTAP - 1) % 2 == 0

        def sample_and_scan_dve(dve, pair, stats):
            dve.memset(W9, 0.0).then_inc(df_zero, 1)
            settle(dve)
            reach = dve.value_load(RI[0:1, 0:1], min_val=0, max_val=MAXR)

            def step(c, k, on):
                T = pair * NT + c

                def product(q):
                    if not on(0):
                        return
                    dy, dx = TAPS[q]
                    dve.wait_ge(df_w, turn(T, q))
                    if q == PE_TAPS:
                        dve.wait_ge(sc_y, reuse(T))
                        o = XS[:, k, :]
                    else:
                        u = q if q < PE_TAPS else q - 1
                        if u < 2:
                            dve.wait_ge(df_add, summed(T - 1, POOL_SUMS - 2 + u, POOL_SUMS))
                        elif u < PE_TAPS + 2:
                            dve.wait_ge(df_acc, summed(T, u - 2, PE_SUMS))
                        else:
                            dve.wait_ge(df_add, summed(T, u - PE_TAPS - 2, POOL_SUMS))
                        o = PRD[:, product_buffer(q), :]
                    dve.tensor_tensor(img(o), img(PSUM[:, (k + q) % 2, :]), pch(c, XBASE, dy, dx),
                                      ALU.mult).then_inc(df_p, 1)

                for q in range(PE_TAPS):
                    product(q)
                if on(-2):
                    dve.wait_ge(sc_u, after(T - 2))
                    dve.wait_ge(sc_bc, after(T - 2))
                    dve.tensor_tensor(UU, UU, PSUM[:, BB, :], ALU.mult).then_inc(sc_bx, 1)
                    dve.wait_ge(sc_bx, after(T - 2))
                    dve.wait_ge(sc_da, after(T - 2))
                    dve.tensor_tensor_scan(HH, DA, UU, SM[:, 12:13], ALU.mult, ALU.add).then_inc(sc_h, 1)
                    dve.wait_ge(sc_h, after(T - 2))
                    dve.tensor_copy(SM[:, 12:13], HH[:, CH - 1:CH])
                    dve.tensor_tensor(UU, HH, PSUM[:, CB, :], ALU.mult).then_inc(sc_hc, 1)
                    dve.wait_ge(sc_hc, after(T - 2))
                    dve.wait_ge(sc_cen, after(T - 3))
                    dve.scalar_tensor_tensor(out=YY, in0=XS[:, k, :], scalar=vc("Ds"), in1=UU,
                                             op0=ALU.mult, op1=ALU.add).then_inc(sc_y, 1)
                product(4)
                product(5)
                if on(0):
                    dve.wait_ge(df_acc, summed(T, PE_SUMS - 1, PE_SUMS))
                    dve.wait_ge(df_p, turn(T, PE_TAPS))
                    dve.tensor_tensor(XS[:, k, :], XS[:, k, :], PSUM[:, ACC, :], ALU.add).then_inc(df_xs, 1)
                product(6)
                product(7)
                if on(-3):
                    dve.wait_ge(sc_rs, after(T - 3))
                    dve.tensor_tensor(RS2, PSUM[:, OB2, :], RS2, ALU.mult).then_inc(sc_t, 1)
                product(8)
                if on(-3):
                    dve.wait_ge(sc_t, after(T - 3))
                    dve.scalar_tensor_tensor(out=xch(c - 3), in0=img(RS2), scalar=OUTB[:, :], in1=xch(c - 3),
                                             op0=ALU.add, op1=ALU.add).then_inc(sc_x, 1)
                    dve.wait_ge(sc_x, after(T - 3))
                    stats(c - 3, c - 3)
                if on(0):
                    settle(dve)
                    with dve.If(reach > 0):
                        dve.wait_ge(df_add, summed(T, POOL_SUMS - 1, POOL_SUMS))
                        far_dve(dve, c, k, reach)

            pipeline(dve, step)

        def sample_and_scan_pool(pool, pair):
            offs = OFF.rearrange("p y n -> p (y n)")
            ht = HT.rearrange("p d (y a g) -> p d y a g", y=ROWS, a=2)
            w9 = W9.rearrange("p y d g -> p y (d g)")
            w9h = w9.rearrange("p y (h n) -> p (y h) n", h=2)

            def part(j):
                return WPART.rearrange("p y h n -> p (y h) n")[:, :, j * HALF * SG:(j + 1) * HALF * SG]

            pool.wait_ge(rad_dve, pair * 5 + 5)
            pool.wait_ge(df_zero, pair + 1)

            def step(c, k, on):
                T = pair * NT + c
                if on(-2):
                    pool.wait_ge(sc_ln, after(T - 2))
                    pool.tensor_tensor(RL, RL, AB, ALU.add).then_inc(sc_delta, 1)
                    pool.wait_ge(sc_delta, after(T - 2))
                    pool.wait_ge(sc_y, after(T - 3))
                    pool.tensor_tensor(UU, RL, XS[:, k, :], ALU.mult).then_inc(sc_u, 1)
                if on(1):
                    pool.wait_ge(df_hat, after(T + 1))
                    pool.wait_ge(df_lo, after(T))
                    for j in range(3):
                        ins = pool.tensor_tensor(
                            W9[:, :, 3 * j:3 * j + 3, :].rearrange("p y d g -> p d y g"),
                            ht[:, j, :, 1, :].unsqueeze(1).broadcast_to([P, 3, ROWS, SG]), ht[:, :, :, 0, :], ALU.mult)
                    ins.then_inc(df_w9, 1)
                if on(2):
                    pool.wait_ge(df_w9, after(T + 1))
                    pool.tensor_tensor(HT, offs[:, bass.ds((c + 2) * 64, 64)].unsqueeze(1).broadcast_to([P, 3, 64]),
                                       cs("shift").unsqueeze(2).broadcast_to([P, 3, 64]), ALU.subtract).then_inc(df_ht, 1)
                if on(1):
                    pool.wait_ge(df_hi, after(T + 1))
                    pool.tensor_tensor(w9h, w9h, part(0), ALU.subtract).then_inc(df_r1, 1)
                    pool.wait_ge(df_mid, after(T + 1))
                    pool.tensor_tensor(part(2), w9h, part(1), ALU.subtract).then_inc(df_lo, 1)
                if on(0):
                    for m in range(POOL_SUMS):
                        q = PE_TAPS + 1 + m
                        pool.wait_ge(df_p, turn(T, q))
                        if m == 0:
                            pool.wait_ge(df_xs, after(T))
                        else:
                            pool.wait_ge(df_add, summed(T, m - 1, POOL_SUMS))
                        pool.tensor_tensor(XS[:, k, :], XS[:, k, :], PRD[:, product_buffer(q), :], ALU.add).then_inc(df_add, 1)

            pipeline(pool, step)

        def sample_and_scan_act(act, pair):
            w9h = W9.rearrange("p y (h d) g -> p (y h) (d g)", h=2)

            def part(j):
                return WPART.rearrange("p y h n -> p (y h) n")[:, :, j * HALF * SG:(j + 1) * HALF * SG]

            def step(c, k, on):
                T = pair * NT + c
                if on(-3):
                    act.wait_ge(sc_cen, after(T - 3))
                    act.wait_ge(sc_x, after(T - 4))
                    act.activation(RS2, PSUM[:, MB, :], ACT.Square).then_inc(sc_sq, 1)
                if on(-2):
                    act.wait_ge(sc_delta, after(T - 2))
                    act.wait_ge(sc_h, after(T - 3))
                    act.activation(DA, RL, ACT.Exp, scale=SM[:, 9:10]).then_inc(sc_da, 1)
                if on(-1):
                    act.wait_ge(sc_z, after(T - 1))
                    act.activation(AB, PSUM[:, ZB, :], ACT.Abs, bias=vc("dt_b")).then_inc(sc_abs, 1)
                    act.wait_ge(sc_u, after(T - 2))
                    act.wait_ge(sc_da, after(T - 2))
                    act.activation(RL, PSUM[:, ZB, :], ACT.Relu, bias=vc("dt_b"))
                    act.wait_ge(sc_abs, after(T - 1))
                    act.activation(AB, AB, ACT.Exp, scale=-1.0).then_inc(sc_exp, 1)
                if on(1):
                    act.wait_ge(df_w9, after(T + 1))
                    act.wait_ge(df_tr, after(T))
                    act.activation(part(0), w9h, ACT.Copy).then_inc(df_hi, 1)
                if on(2):
                    act.wait_ge(df_ht, after(T + 2))
                    act.activation(HT, HT, ACT.Abs).then_inc(df_abs, 1)
                    act.wait_ge(df_abs, after(T + 2))
                    act.activation(HT, HT, ACT.Relu, bias=1.0, scale=-1.0).then_inc(df_hat, 1)
                if on(1):
                    act.wait_ge(df_r1, after(T + 1))
                    act.activation(part(1), w9h, ACT.Copy).then_inc(df_mid, 1)
                if on(-1):
                    act.wait_ge(sc_exp, after(T - 1))
                    act.activation(AB, AB, ACT.Ln, bias=1.0).then_inc(sc_ln, 1)
                if on(-3):
                    act.wait_ge(sc_var, after(T - 3))
                    act.activation(RS2, PSUM[:, MB, :], ACT.Ln, bias=GNE[:, 1:2]).then_inc(sc_lv, 1)
                    act.wait_ge(sc_lv, after(T - 3))
                    act.activation(RS2, RS2, ACT.Exp, scale=-0.5).then_inc(sc_rs, 1)
                if on(1):
                    act.wait_ge(df_tr, after(T + 1))
                    act.activation(WTB[0:WROWS, (k + 1) % 2, :], TB, ACT.Copy).then_inc(df_wt, 1)

            pipeline(act, step)

        def sample_and_scan_pe(pe, pair):
            settle(pe)
            reach = pe.value_load(RI[0:1, 0:1], min_val=0, max_val=MAXR)

            def step(c, k, on):
                T = pair * NT + c

                def spread(q):
                    if on(0):
                        h = q // HALF
                        if q == 0:
                            pe.wait_ge(df_wt, after(T))
                        pe.wait_ge(df_p, turn(T, q - 2))
                        pe.matmul(PSUM[:, (k + q) % 2, :], SELB[:, q, :], WTB[0:WROWS, k, h * CH:(h + 1) * CH],
                                  start=True, stop=True).then_inc(df_w, 1)

                def add_up(m):
                    if on(0):
                        pe.wait_ge(df_p, turn(T, m))
                        pe.matmul(PSUM[:, ACC, :], ident, PRD[:, m % 2, :], start=(m == 0),
                                  stop=(m == PE_SUMS - 1)).then_inc(df_acc, 1)

                spread(0)
                spread(1)
                if on(-3):
                    pe.wait_ge(sc_sq, after(T - 3))
                    pe.matmul(PSUM[:, MB, :], cs("mean"), RS2, start=True, stop=True).then_inc(sc_var, 1)
                if on(-1):
                    pe.wait_ge(df_add, summed(T - 1, POOL_SUMS - 1, POOL_SUMS))
                    pe.wait_ge(sc_exp, after(T - 2))
                    settle(pe)
                    with pe.If(reach > 0):
                        far_pe(pe, c - 1, reach)
                    pe.matmul(PSUM[:, ZB, :], WZ[:, :], XS[:, (k + 1) % 2, :], start=True, stop=True).then_inc(sc_z, 1)
                spread(2)
                add_up(0)
                spread(3)
                add_up(1)
                spread(4)
                add_up(2)
                spread(5)
                add_up(3)
                if on(-1):
                    pe.wait_ge(sc_bx, after(T - 2))
                    pe.matmul(PSUM[:, BB, :], WB[:, :], XS[:, (k + 1) % 2, :], start=True, stop=True)
                    pe.wait_ge(sc_hc, after(T - 2))
                    pe.matmul(PSUM[:, CB, :], WC[:, :], XS[:, (k + 1) % 2, :], start=True, stop=True).then_inc(sc_bc, 1)
                spread(6)
                spread(7)
                if on(1):
                    pe.wait_ge(df_lo, after(T + 1))
                    pe.wait_ge(df_xs, after(T))
                    for h in range(2):
                        for y in range(ROWS):
                            ins = pe.transpose(TB[:, (h * ROWS + y) * W:(h * ROWS + y + 1) * W], WPART[:, y, h, :], IDB[:, :])
                    ins.then_inc(df_tr, 1)
                spread(8)
                if on(-2):
                    pe.wait_ge(sc_y, after(T - 2))
                    pe.wait_ge(sc_lv, after(T - 3))
                    pe.matmul(PSUM[:, MB, :], cs("center"), YY, start=True, stop=True)
                    pe.wait_ge(sc_t, after(T - 3))
                    pe.matmul(PSUM[:, OB2, :], WOUT2[:, :], YY, start=True, stop=True).then_inc(sc_cen, 1)

            pipeline(pe, step)

        def taps_done(i, j, n):
            return i * n + (j + 1 + CREDIT)

        def vector_tap(dve, i, t, j, n, acc, base, weights, done):
            dy, dx = TAPS[j]
            if j == 0:
                ins = dve.tensor_scalar(img(acc), pch(t, base, dy, dx), vc(weights, 0), None, ALU.mult)
            else:
                dve.wait_ge(done, taps_done(i, j - 1, n))
                ins = dve.scalar_tensor_tensor(out=img(acc), in0=pch(t, base, dy, dx), scalar=vc(weights, j), in1=img(acc),
                                               op0=ALU.mult, op1=ALU.add)
            ins.then_inc(done, 1)

        @block.vector
        def _(dve):
            credit(dve, ln0_xn, ln0_cc, ln0_y, *d1_tap, d1_sum, *d2_tap, d2_xb, sp_log, sp_mx, sp_sub, sp_sum, sp_rec, sp_aff, sp_e, sp_acc, mh_qm, mh_mx, mh_nmx,
                   mh_rec, mh_pn, mh_vm, o_e, o_x, l1_x, in_cp, d2_y, d2_o, l3_o)
            credit(dve, df_p, df_xs, sc_bx, sc_h, sc_hc, sc_y, sc_t, sc_x)
            dve.reg_mov(far_dve_step, 0)
            dve.reg_mov(far_dve_turn, 0)
            dve.wait_ge(load, 16 * 9)
            for w in (WQ, WK, WV, WPROJ, WIN, WOUT, WZ, WB, WC):
                dve.memset(w[:, :], 0.0)
            dve.tensor_copy(SELB[:, :, :].rearrange("p t c -> p (t c)"), SELF)
            dve.tensor_copy(IDB[:, :], ident)
            dve.memset(WOFF[:, :, :, :], 0.0)
            dve.memset(WCONV[:, :, :], 0.0)
            dve.memset(PLAIN[:, :], 0.0)
            dve.memset(SM[:, :], 0.0)
            dve.memset(GNE[:, 0:1], GN_EPS)
            dve.memset(GNE[:, 1:2], LN_EPS)
            dve.memset(WL3[:, :, :], 0.0).then_inc(const_dve, 1)
            dve.tensor_scalar(NOT3[:, :], cs("mask3"), -1.0, 1.0, ALU.mult, ALU.add).then_inc(const_dve, 1)
            dve.wait_ge(const_dve, 2)
            for s in range(2):
                p, q = s * C, s * C + C
                for w, name in ((WQ, "q"), (WK, "k"), (WV, "v"), (WPROJ, "proj"), (WIN, "in_proj"), (PLAIN, "out_proj")):
                    dve.tensor_copy(w[p:q, p:q], mt(name, p, q))
                dve.tensor_copy(WOFF[p:q, :, s, :], mt("off", p, q).rearrange("p (g a) -> p a g", a=2))
                dve.tensor_copy(WCONV[p:q, s, :], mt("conv", p, q))
                xp = MAT["x_proj"][0]
                for w, col in ((WB, DT_RANK), (WC, DT_RANK + 1)):
                    dve.tensor_copy(w[p:q, p:q], MATS[p:q, xp + col:xp + col + 1].broadcast_to([C, C]))
                dve.tensor_scalar(WOUT[p:q, p:q], mt("out_proj", p, q), vc("out_ln_g")[p:q], None, ALU.mult)
                dve.tensor_tensor(WL3[p:q, :, p:q], mt("w3", p, q).rearrange("p (t o) -> p t o", t=9),
                                  cs("mask3")[p:q, p:q].unsqueeze(1).broadcast_to([C, 9, C]), ALU.mult)
                dve.tensor_tensor(NOT3[p:q, p:q], mt("w1", p, q), NOT3[p:q, p:q], ALU.mult).then_inc(const_dve, 1)
            dve.wait_ge(const_dve, 4)
            for s in range(2):
                p, q = s * C, s * C + C
                dve.tensor_tensor(WL3[p:q, 4, p:q], WL3[p:q, 4, p:q], NOT3[p:q, p:q], ALU.add)
            for w, name, first in ((WDW1, "conv2d_w", DW1_VECTOR), (WDW2, "dw_w", DW2_VECTOR)):
                for j in range(first, NTAP):
                    dve.tensor_scalar(w[:, j - first, :], ident, vc(name, j), None, ALU.mult)
            dve.tensor_reduce(SM[:, 8:9], vc("l3_b", 0, C), AX.X, ALU.add).then_inc(const_dve, 1)
            dve.wait_ge(const_pe, 1)
            for s in range(2):
                p, q = s * C, s * C + C
                dve.tensor_copy(WZ[p:q, p:q], PSUM[p:q, 0, 0:C])
            dve.tensor_copy(OUTB[:, :], PSUM[:, 1, 0:1])
            dve.tensor_copy(WOUT2[:, :], PSUM[:, 2, 0:P])
            dve.wait_ge(const_act, 1)
            dve.tensor_scalar(SM[:, 9:10], SM[:, 10:11], -1.0, None, ALU.mult).then_inc(const_ready, 1)

            def group_norm(n):
                dve.wait_ge(stats_done, (n + 1) * NT)
                settle(dve)
                dve.bn_aggr(SM[:, 0:2], STATS[:, :, :]).then_inc(gn_dve, 1)
                dve.wait_ge(gn_pe, n * 2 + 1)
                dve.wait_ge(gn_dve, n * 5 + 1)
                dve.tensor_tensor(SM[:, 2:3], SM[:, 0:1], PSUM[:, 7, 0:1], ALU.subtract).then_inc(gn_dve, 1)
                dve.wait_ge(gn_dve, n * 5 + 2)
                dve.scalar_tensor_tensor(out=SM[:, 3:4], in0=SM[:, 2:3], scalar=SM[:, 2:3], in1=SM[:, 1:2],
                                         op0=ALU.mult, op1=ALU.add).then_inc(gn_dve, 1)
                dve.wait_ge(gn_act, n + 1)
                dve.reciprocal(SM[:, 5:6], SM[:, 6:7]).then_inc(gn_dve, 1)
                dve.wait_ge(gn_dve, n * 5 + 4)
                dve.scalar_tensor_tensor(out=SM[:, 4:5], in0=PSUM[:, 7, 0:1], scalar=-1.0, in1=SM[:, 5:6],
                                         op0=ALU.mult, op1=ALU.mult).then_inc(gn_dve, 1)

            def stats(t, s):
                dve.bn_stats(STATS[:, bass.ds(s, 1), :], xch(t)).then_inc(stats_done, 1)

            with dve.Fori(0, PAIRS) as pair:
                for j in range(4):
                    dve.wait_ge(x_in[j], pair * 16 + 16)
                    settle(dve)
                    with dve.Fori(j * NT // 4, (j + 1) * NT // 4) as t:
                        dve.bn_stats(STATS[:, bass.ds(t, 1), :], xch(t)).then_inc(stats_done, 1)
                group_norm(pair * 4)
                dve.wait_ge(gn_dve, pair * 20 + 5)
                settle(dve)

                def step(i, b, there):
                    T = [pair * NT + i * 2 + k for k in range(2)]
                    if there(0):
                        for k in range(2):
                            dve.wait_ge(ln0_cen, reuse(T[k]))
                            dve.tensor_scalar(img(n_xn[:, k, :]), xch(i * 2 + k), RSTD, NM, ALU.mult,
                                              ALU.add).then_inc(ln0_xn, 1)
                    if there(-1):
                        for k in range(2):
                            dve.wait_ge(ln0_cen, after(T[k] - 2))
                            if there(-2):
                                dve.wait_ge(ln0_y, reuse(T[k] - 4))
                            dve.tensor_scalar(n_cen[:, 1 - b, k, :], PSUM[:, k, :], 1.0, None, ALU.mult).then_inc(ln0_cc, 1)
                    if there(-2):
                        for k in range(2):
                            dve.wait_ge(ln0_rs, after(T[k] - 4))
                            dve.wait_ge(ln0_yb, reuse(T[k] - 4))
                            dve.scalar_tensor_tensor(out=n_y[:, k, :], in0=n_cen[:, b, k, :], scalar=vc("ln_w"),
                                                     in1=n_rs[:, k, :], op0=ALU.mult, op1=ALU.mult).then_inc(ln0_y, 1)

                in_turn(dve, NT // 2, 0, 2, step)
                dve.wait_ge(ln0_yb, (pair + 1) * NT + CREDIT)
                dve.memset(STB, 0.0)
                dve.memset(SFAS, 0.0)
                dve.memset(EXPD, 0.0).then_inc(tok_zero, 1)
                dve.wait_ge(tok_zero, pair + 1)
                settle(dve)
                for s in range(2):
                    with dve.Fori(0, NS) as i:
                        p, q = s * C, s * C + C
                        dve.tensor_reduce(
                            STB[p:q, bass.ds(i + 1, 1), s, 1:1 + NS],
                            PAD[p:q, bass.ds(i * 8 + BASE, 8), 1:1 + W].rearrange("p r (b q) -> p b r q", q=8),
                            AX.XY, ALU.add).then_inc(tok_dve, 1)

                def step(i, b, there):
                    S = [pair * NS + i * 2 + k for k in range(2)]
                    st = [i * 2 + k for k in range(2)]
                    if there(0):
                        for k in range(2):
                            dve.wait_ge(sp_lgt, after(S[k]))
                            v = PSUM[:, k, 0:8 * 24].rearrange("p (a r c) -> p a r c", r=3, c=4)
                            o = LG[:, k, :, :].rearrange("p a (r c) -> p a r c", r=3)
                            dve.tensor_copy(o[0:64], v[0:64, :, :, 0:3])
                            dve.tensor_copy(o[64:128], v[64:128, :, :, 1:4]).then_inc(sp_log, 1)
                        for k in range(2):
                            dve.wait_ge(sp_log, after(S[k]))
                            dve.tensor_reduce(SMX[:, k, 0, :], LG[:, k, :, :], AX.X, ALU.max).then_inc(sp_mx, 1)
                        for k in range(2):
                            dve.wait_ge(sp_mx, after(S[k]))
                            dve.tensor_tensor(LG[:, k, :, :], LG[:, k, :, :],
                                              SMX[:, k, 0, :].unsqueeze(2).broadcast_to([P, NS, 9]),
                                              ALU.subtract).then_inc(sp_sub, 1)
                        for k in range(2):
                            dve.wait_ge(sp_exp, after(S[k]))
                            dve.tensor_reduce(SMX[:, k, 1, :], LG[:, k, :, :], AX.X, ALU.add).then_inc(sp_sum, 1)
                        for k in range(2):
                            dve.wait_ge(sp_sum, after(S[k]))
                            dve.reciprocal(SMX[:, k, 2, :], SMX[:, k, 1, :]).then_inc(sp_rec, 1)
                        for k in range(2):
                            dve.wait_ge(sp_rec, after(S[k]))
                            dve.tensor_tensor(AFF[:, bass.ds(st[k], 1), :, :].rearrange("p o a b -> p (o a) b"),
                                              LG[:, k, :, :],
                                              SMX[:, k, 2, :].unsqueeze(2).broadcast_to([P, NS, 9]),
                                              ALU.mult).then_inc(sp_aff, 1)
                        for k in range(2):
                            dve.wait_ge(sp_aff, after(S[k]))
                            dve.wait_ge(sp_fold, reuse(S[k]))
                            expand(dve, k, st[k]).then_inc(sp_e, 1)
                    if there(-1):
                        for k in range(2):
                            dve.wait_ge(sp_fold, after(S[k] - 2))
                            dve.wait_ge(sp_acc, after(S[k] - 3))
                            for s in range(2):
                                p, q = s * C, s * C + C
                                v = SFAS[p:q, :, bass.ds((st[k] - 2) * TW, 3 * TW)]
                                ins = dve.tensor_tensor(
                                    v, PSUM[p:q, 6 + k, 0:2 * P].rearrange("p (a b) -> p a b", a=2)[:, :, s * C:s * C + 3 * TW],
                                    v, ALU.add)
                            ins.then_inc(sp_acc, 1)

                in_turn(dve, NS // 2, 0, 1, step)
                dve.wait_ge(sp_acc, (pair + 1) * NS + CREDIT)
                inner = SFAS.rearrange("p a (i j) -> p a i j", i=TW)[:, :, 1:1 + NS, 1:1 + NS]
                dve.tensor_scalar(inner[:, 1], inner[:, 1], 1e-12, None, ALU.add).then_inc(sf_dve, 1)
                dve.wait_ge(sf_dve, pair * 3 + 1)
                dve.reciprocal(inner[:, 1], inner[:, 1]).then_inc(sf_dve, 1)
                dve.wait_ge(sf_dve, pair * 3 + 2)
                dve.wait_ge(sp_fold, (pair + 1) * NS + CREDIT)
                dve.tensor_tensor(SFC.rearrange("p (i j) -> p i j", i=NS), inner[:, 0], inner[:, 1],
                                  ALU.mult).then_inc(sf_dve, 1)
                dve.wait_ge(mha_act, pair * 2 + 1)
                settle(dve)

                def step(i, b, there):
                    h = [i * 2 + k for k in range(2)]
                    N = [pair * NH + h[k] for k in range(2)]
                    if there(-1):
                        for k in range(2):
                            dve.wait_ge(mh_exp, after(N[k] - 2))
                            dve.reciprocal(MHS[:, k, 0:2], MHS[:, k, 4:6]).then_inc(mh_rec, 1)
                        for k in range(2):
                            dve.wait_ge(mh_rec, after(N[k] - 2))
                            dve.tensor_tensor(PB[:, k, :, :], PB[:, k, :, :],
                                              MHS[:, k, 0:2].unsqueeze(2).broadcast_to([P, 2, TOK]),
                                              ALU.mult).then_inc(mh_pn, 1)
                        for k in range(2):
                            dve.wait_ge(mh_pv, reuse(N[k] - 2))
                            a = CST["headrow"][0] + P - HD
                            dve.tensor_tensor(VM[:, k, :, :], VB,
                                              CSTS[:, bass.ds((h[k] - 2) * -HD + a, P)].unsqueeze(1).broadcast_to([P, 2, P]),
                                              ALU.mult).then_inc(mh_vm, 1)
                    if there(1):
                        for k in range(2):
                            dve.wait_ge(mh_s, reuse(N[k] + 2))
                            a = CST["headcol"][0]
                            dve.tensor_scalar(QM[:, k, :], QB, CSTS[:, bass.ds(h[k] + (a + 2), 1)], None,
                                              ALU.mult).then_inc(mh_qm, 1)
                    if there(0):
                        for k in range(2):
                            dve.wait_ge(mh_s, after(N[k]))
                            dve.wait_ge(mh_pn, reuse(N[k]))
                            dve.tensor_reduce(MHS[:, k, 0:2], PSUM[:, 2 * b + k, :].rearrange("p (a b) -> p a b", a=2),
                                              AX.X, ALU.max).then_inc(mh_mx, 1)
                        for k in range(2):
                            dve.wait_ge(mh_mx, after(N[k]))
                            dve.tensor_scalar(MHS[:, k, 2:4], MHS[:, k, 0:2], -HD ** -0.5, None,
                                              ALU.mult).then_inc(mh_nmx, 1)

                in_turn(dve, NH // 2, 1, 1, step)
                dve.wait_ge(mha_pe, pair * 3 + 3)
                dve.memset(SOP, 0.0)
                dve.memset(SFB, 0.0).then_inc(so_dve, 1)
                dve.wait_ge(so_dve, pair * 4 + 1)
                dve.tensor_scalar(SOP[:, 1:1 + NS, 1:1 + NS], PSUM[:, 6, 0:TOK].rearrange("p (i j) -> p i j", i=NS),
                                  vc("proj_b"), None, ALU.add).then_inc(so_dve, 1)
                dve.wait_ge(so_dve, pair * 4 + 2)
                for s in range(2):
                    p, q = s * C, s * C + C
                    for j in range(3):
                        ins = dve.tensor_copy(SFB[p:q, :, s * C + j * TW:s * C + (j + 1) * TW], SOP[p:q, j:j + NS, :])
                ins.then_inc(so_dve, 1)
                dve.wait_ge(so_pe, pair + 1)
                for j in range(4):
                    ins = dve.tensor_copy(STT[:, 4 * j:4 * j + 4, :],
                                          PSUM[:, j, :].rearrange("p (a b) -> p a b", a=4))
                ins.then_inc(so_dve, 1)

                def step(i, b, there):
                    S = [pair * NS + i * 2 + k for k in range(2)]
                    st = [i * 2 + k for k in range(2)]
                    if there(0):
                        for k in range(2):
                            dve.wait_ge(o_tr, reuse(S[k]))
                            expand(dve, k, st[k]).then_inc(o_e, 1)
                    if there(-1):
                        for k in range(2):
                            dve.wait_ge(o_mm, after(S[k] - 2))
                            for j in range(2):
                                v = X[:, bass.ds((st[k] - 2) * 8, 8), j * 64:(j + 1) * 64].rearrange("p r (b q) -> p b r q", q=8)
                                ins = dve.tensor_tensor(
                                    v, PSUM[:, 4 + 2 * k + j, :].rearrange("p (b r q) -> p b r q", b=8, r=8), v, ALU.add)
                            ins.then_inc(o_x, 1)
                        for k in range(2):
                            dve.wait_ge(o_x, after(S[k] - 2))
                            for j in range(2):
                                stats(st[k] * 2 + (j - 4), st[k] * 2 + (j - 4))

                in_turn(dve, NS // 2, 0, 1, step)
                group_norm(pair * 4 + 1)
                dve.wait_ge(o_at, (pair + 1) * NS + CREDIT)
                settle(dve)
                with dve.Fori(0, NS) as i:
                    dve.wait_ge(l1_xn, after(pair * NT + i * 2 + 1))
                    dve.tensor_reduce(POOLED[:, bass.ds(i * NS, NS)],
                                      PAD[:, bass.ds(i * 8 + BASE, 8), 1:1 + W].rearrange("p r (b q) -> p b r q", q=8),
                                      AX.XY, ALU.add).then_inc(l1_pool, 1)
                q0 = pair * 10
                dve.wait_ge(rt_pe, pair * 4 + 1)
                dve.scalar_tensor_tensor(out=RB, in0=PSUM[:, 0, 0:64].rearrange("p (a b) -> p a b", a=2), scalar=1.0 / 64,
                                         in1=ROWV[:, 0:2 * RED].unsqueeze(1).broadcast_to([P, 2, 2 * RED]),
                                         op0=ALU.mult, op1=ALU.add).then_inc(rt_dve, 1)
                dve.wait_ge(rt_dve, q0 + 1)
                dve.tensor_scalar(RB, RB, 0.0, None, ALU.max).then_inc(rt_dve, 1)
                dve.wait_ge(rt_pe, pair * 4 + 2)
                dve.tensor_copy(FS[0:2, :], PSUM[0:2, 1, 0:FC]).then_inc(rt_dve, 1)
                dve.wait_ge(rt_pe, pair * 4 + 3)
                dve.tensor_tensor(RW, PSUM[:, 2, 0:EXPERTS], vc("fc_b", 0, EXPERTS), ALU.add).then_inc(rt_dve, 1)
                dve.wait_ge(rt_dve, q0 + 4)
                dve.tensor_scalar(RW, RW, 0.0, None, ALU.max).then_inc(rt_dve, 1)
                dve.wait_ge(rt_act, pair + 1)
                dve.tensor_scalar(CW, vc("experts", 0, 36), RW[:, 0:1], None, ALU.mult).then_inc(rt_dve, 1)
                for e in range(1, EXPERTS):
                    dve.wait_ge(rt_dve, q0 + 5 + e)
                    dve.scalar_tensor_tensor(out=CW, in0=vc("experts", 36 * e, 36), scalar=RW[:, e:e + 1], in1=CW,
                                             op0=ALU.mult, op1=ALU.add).then_inc(rt_dve, 1)
                dve.wait_ge(rt_dve, q0 + 9)
                for j in range(9):
                    ins = dve.tensor_tensor(
                        WE[:, j, :].rearrange("p (g i) -> p g i", i=4),
                        CW.rearrange("p (i t) -> p t i", t=9)[:, j, :].unsqueeze(1).broadcast_to([P, 32, 4]),
                        cs("group4").rearrange("p (g i) -> p g i", i=4), ALU.mult)
                ins.then_inc(rt_dve, 1)
                dve.wait_ge(rt_pe, pair * 4 + 4)
                dve.tensor_copy(WL1[:, 0:4, :], PSUM[:, 3, :].rearrange("p (a b) -> p a b", a=4))
                dve.tensor_copy(WL1[:, 4:8, :], PSUM[:, 4, :].rearrange("p (a b) -> p a b", a=4))
                dve.tensor_copy(WL1[:, 8, :], PSUM[:, 5, 0:P]).then_inc(l1_pool, 1)
                with dve.Fori(0, NT // 2) as i:
                    for k in range(2):
                        t = i * 2 + k
                        T = pair * NT + t
                        dve.wait_ge(l1_mm, after(T))
                        dve.tensor_tensor(xch(t), img(PSUM[:, k, :]), xch(t), ALU.add).then_inc(l1_x, 1)
                    for k in range(2):
                        t = i * 2 + k
                        dve.wait_ge(l1_x, after(pair * NT + t))
                        stats(t, t)
                group_norm(pair * 4 + 2)
                with dve.Fori(0, NT // 2) as i:
                    for k in range(2):
                        t = i * 2 + k
                        dve.wait_ge(in_mm, after(pair * NT + t))
                        dve.tensor_scalar(pch(t), img(PSUM[:, k, :]), 1.0, None, ALU.mult).then_inc(in_cp, 1)
                dve.wait_ge(in_cp, (pair + 1) * NT + CREDIT)
                settle(dve)
                with dve.Fori(0, NT // 2) as i:
                    T = [pair * NT + i * 2 + k for k in range(2)]
                    for j in range(DW1_VECTOR):
                        for k in range(2):
                            if j == 0:
                                dve.wait_ge(d1_act, reuse(T[k]))
                            vector_tap(dve, pair * (NT // 2) + i, i * 2 + k, j, DW1_VECTOR, d_acc[:, k, :], BASE,
                                       "conv2d_w", d1_tap[k])
                    for k in range(2):
                        dve.wait_ge(d1_mm, after(T[k]))
                        dve.wait_ge(d1_tap[k], taps_done(pair * (NT // 2) + i, DW1_VECTOR - 1, DW1_VECTOR))
                        dve.tensor_tensor(d_acc[:, k, :], PSUM[:, k, :], d_acc[:, k, :], ALU.add).then_inc(d1_sum, 1)
                dve.wait_ge(border, pair * 2 + 2)
                settle(dve)

                def step(i, b, there):
                    T = [pair * NT + i * 2 + k for k in range(2)]

                    def taps(first, last):
                        if there(0):
                            for j in range(first, last):
                                for k in range(2):
                                    if j == 0:
                                        dve.wait_ge(d2_xb, reuse(T[k]))
                                    vector_tap(dve, pair * (NT // 2) + i, i * 2 + k, j, DW2_VECTOR, d_acc[:, k, :], XBASE,
                                               "dw_w", d2_tap[k])

                    taps(0, DW2_VECTOR // 2)
                    if there(-2):
                        for k in range(2):
                            dve.wait_ge(d2_rs, after(T[k] - 4))
                            dve.wait_ge(d2_off, reuse(T[k] - 4))
                            dve.scalar_tensor_tensor(out=d_y[:, k, :], in0=PSUM[:, 2 + k, :], scalar=vc("dw_ln_g"),
                                                     in1=d_rs[:, k, :], op0=ALU.mult, op1=ALU.mult).then_inc(d2_y, 1)
                    taps(DW2_VECTOR // 2, DW2_VECTOR)
                    if there(0):
                        for k in range(2):
                            dve.wait_ge(d2_mm, after(T[k]))
                            dve.wait_ge(d2_tap[k], taps_done(pair * (NT // 2) + i, DW2_VECTOR - 1, DW2_VECTOR))
                            dve.wait_ge(d2_cen, reuse(T[k]))
                            dve.scalar_tensor_tensor(out=d_xb[:, k, :], in0=PSUM[:, k, :], scalar=vc("dw_b"),
                                                     in1=d_acc[:, k, :], op0=ALU.add, op1=ALU.add).then_inc(d2_xb, 1)
                    if there(-3):
                        for k in range(2):
                            dve.wait_ge(d2_off, after(T[k] - 6))
                            dve.tensor_tensor(OFF[:, bass.ds((i * 2 + k - 6) * ROWS, ROWS), :],
                                              PSUM[:, 6 + k, 0:64].rearrange("p (a b) -> p a b", a=ROWS),
                                              ROWV[:, 2 * RED:].rearrange("p (a b) -> p a b", a=ROWS),
                                              ALU.add).then_inc(d2_o, 1)

                in_turn(dve, NT // 2, 0, 3, step)
                dve.wait_ge(d2_o, (pair + 1) * NT + CREDIT)
                dve.tensor_reduce(SM[:, 16:17], OFF, AX.XY, ALU.max, apply_absolute_value=True).then_inc(rad_dve, 1)
                dve.wait_ge(rad_pe, pair * 2 + 1)
                dve.tensor_reduce(SM[0:1, 17:18], PSUM[0:1, 0, 0:P], AX.X, ALU.max).then_inc(rad_dve, 1)
                dve.wait_ge(rad_pe, pair * 2 + 2)
                dve.tensor_scalar(SM[:, 18:19], PSUM[:, 0, P:P + 1], 1.0, None, ALU.is_gt)
                dve.tensor_scalar(SM[:, 19:20], PSUM[:, 0, P:P + 1], MAXR - 1.0, 1.0, ALU.min, ALU.add).then_inc(rad_dve, 1)
                dve.wait_ge(rad_dve, pair * 5 + 3)
                dve.tensor_tensor(RI[:, :], SM[:, 18:19], SM[:, 19:20], ALU.mult).then_inc(rad_dve, 1)
                dve.wait_ge(rad_dve, pair * 5 + 4)
                dve.tensor_scalar(SM[:, 19:20], RI[:, :], -1.0, None, ALU.mult)
                dve.memset(SM[:, 12:13], 0.0).then_inc(rad_dve, 1)
                dve.wait_ge(rad_dve, pair * 5 + 5)
                sample_and_scan_dve(dve, pair, stats)
                group_norm(pair * 4 + 3)
                with dve.Fori(0, NT // 2) as i:
                    for k in range(2):
                        t = i * 2 + k
                        T = pair * NT + t
                        dve.wait_ge(l3_mm, after(T))
                        dve.wait_ge(out_dma[k], (pair * (NT // 2) + i + 1) * 16)
                        dve.scalar_tensor_tensor(out=img(OBUF[:, k, :]), in0=img(PSUM[:, k, :]), scalar=SM[:, 8:9],
                                                 in1=xch(t), op0=ALU.add, op1=ALU.add).then_inc(l3_o, 1)

        @block.gpsimd
        def _(pool):
            credit(pool, ln0_yb, ln0_sq, df_ht, df_w9, df_r1, df_lo, df_add, sc_delta, sc_u)
            pool.memset(PAD[:, :, :], 0.0).then_inc(border, 1)
            with pool.Fori(0, PAIRS) as pair:
                def step(i, b, there):
                    T = [pair * NT + i * 2 + k for k in range(2)]
                    if there(-1):
                        for k in range(2):
                            pool.wait_ge(ln0_cc, after(T[k] - 2))
                            pool.wait_ge(ln0_var, reuse(T[k] - 2))
                            v = n_cen[:, 1 - b, k, :]
                            pool.tensor_tensor(n_sq[:, k, :], v, v, ALU.mult).then_inc(ln0_sq, 1)
                    if there(-2):
                        for k in range(2):
                            pool.wait_ge(ln0_y, after(T[k] - 4))
                            pool.tensor_tensor(pch(i * 2 + k - 4), img(n_y[:, k, :]),
                                               vc("ln_b").unsqueeze(2).broadcast_to([P, ROWS, W]), ALU.add).then_inc(ln0_yb, 1)

                pool.wait_ge(border, pair * 2 + 1)
                settle(pool)
                in_turn(pool, NT // 2, 0, 2, step)
                pool.wait_ge(d1_act, (pair + 1) * NT + CREDIT)
                settle(pool)
                pool.memset(PAD[:, XBASE + H:XBASE + H + 1, :], 0.0).then_inc(border, 1)
                sample_and_scan_pool(pool, pair)
                pool.wait_ge(sc_x, (pair + 1) * NT + CREDIT)
                settle(pool)
                pool.memset(PAD[:, BASE - 1:BASE, :], 0.0).then_inc(border, 1)

        @block.scalar
        def _(act):
            credit(act, ln0_ln, ln0_rs, sp_stage, sp_pixt, sp_exp, mh_exp, mh_ptc, o_at, l1_xn, in_xn,
                   d1_act, d2_sq, d2_ln, d2_rs, d2_g, l3_xn)
            credit(act, df_abs, df_hat, df_hi, df_mid, df_wt, sc_abs, sc_exp, sc_ln, sc_da, sc_sq, sc_lv, sc_rs)
            act.wait_ge(load, 16 * 9)
            act.wait_ge(const_dve, 5)
            act.activation(SM[:, 10:11], vc("A_logs"), ACT.Exp).then_inc(const_act, 1)

            def group_norm(n):
                act.wait_ge(gn_pe, n * 2 + 2)
                act.activation(SM[:, 6:7], PSUM[:, 7, 1:2], ACT.Sqrt, bias=GNE[:, 0:1]).then_inc(gn_act, 1)
                act.wait_ge(gn_dve, n * 5 + 5)

            def normed(t, o, s):
                act.activation(o, xch(t), ACT.Identity, bias=NM, scale=RSTD).then_inc(s, 1)

            with act.Fori(0, PAIRS) as pair:
                group_norm(pair * 4)
                with act.Fori(0, NT // 2) as i:
                    T = [pair * NT + i * 2 + k for k in range(2)]
                    for k in range(2):
                        act.wait_ge(ln0_var, after(T[k]))
                        act.wait_ge(ln0_y, reuse(T[k]))
                        act.activation(n_rs[:, k, :], PSUM[:, 4 + k, :], ACT.Ln, bias=GNE[:, 1:2]).then_inc(ln0_ln, 1)
                    for k in range(2):
                        act.wait_ge(ln0_ln, after(T[k]))
                        act.activation(n_rs[:, k, :], n_rs[:, k, :], ACT.Exp, scale=-0.5).then_inc(ln0_rs, 1)
                act.wait_ge(ln0_yb, (pair + 1) * NT + CREDIT)
                settle(act)

                def step(i, b, there):
                    S = [pair * NS + i * 2 + k for k in range(2)]
                    if there(1):
                        for k in range(2):
                            act.wait_ge(sp_tr, reuse(S[k] + 2))
                            act.activation(STG[:, k, :].rearrange("p (b r q) -> p b r q", b=NS, r=8),
                                           PAD[:, bass.ds((i * 2 + k + 2) * 8 + BASE, 8), 1:1 + W].rearrange(
                                               "p r (b q) -> p b r q", q=8), ACT.Identity).then_inc(sp_stage, 1)
                    if there(0):
                        for k in range(2):
                            act.wait_ge(sp_sub, after(S[k]))
                            act.activation(LG[:, k, :, :], LG[:, k, :, :], ACT.Exp, scale=C ** -0.5 / 64).then_inc(sp_exp, 1)
                        for k in range(2):
                            act.wait_ge(sp_tr, after(S[k]))
                            act.wait_ge(sp_fold, reuse(S[k]))
                            act.activation(PIXT[:, k, :].rearrange("p (a b) -> p a b", a=2),
                                           PSUM[:, 2 + 2 * k:4 + 2 * k, :], ACT.Copy).then_inc(sp_pixt, 1)

                in_turn(act, NS // 2, 1, 0, step)
                act.wait_ge(mha_pe, pair * 3 + 1)
                act.activation(QB, PSUM[:, 0, 0:TOK], ACT.Copy)
                act.activation(KB, PSUM[:, 0, TOK:2 * TOK], ACT.Copy)
                act.activation(VB, PSUM[:, 1, 0:2 * P].rearrange("p (a b) -> p a b", a=2), ACT.Copy).then_inc(mha_act, 1)

                def step(i, b, there):
                    N = [pair * NH + i * 2 + k for k in range(2)]
                    if there(-1):
                        for k in range(2):
                            act.wait_ge(mh_pt, after(N[k] - 2))
                            act.wait_ge(mh_pv, reuse(N[k] - 2))
                            act.activation(PTB[:, k, :, :], PSUM[:, 4 + k, :].rearrange("p (a b) -> p a b", a=2),
                                           ACT.Copy).then_inc(mh_ptc, 1)
                    if there(0):
                        for k in range(2):
                            act.wait_ge(mh_nmx, after(N[k]))
                            act.wait_ge(mh_pt, reuse(N[k]))
                            for h in range(2):
                                ins = act.activation(PB[:, k, h, :], PSUM[:, 2 * b + k, h * TOK:(h + 1) * TOK], ACT.Exp,
                                                     bias=MHS[:, k, 2 + h:3 + h], scale=HD ** -0.5,
                                                     accum_out=MHS[:, k, 4 + h:5 + h])
                            ins.then_inc(mh_exp, 1)

                in_turn(act, NH // 2, 0, 1, step)
                act.wait_ge(mha_pe, pair * 3 + 2)
                act.activation(OB, PSUM[:, 7, 0:TOK], ACT.Copy).then_inc(mha_act, 1)
                act.wait_ge(so_dve, pair * 4 + 4)
                settle(act)
                with act.Fori(0, NS // 2) as i:
                    S = [pair * NS + i * 2 + k for k in range(2)]
                    for k in range(2):
                        act.wait_ge(o_tr, after(S[k]))
                        act.wait_ge(o_mm, reuse(S[k]))
                        act.activation(WST[:, k, :].unsqueeze(1), STT[:, bass.ds(i * 2 + k, 1), :], ACT.Identity)
                        act.activation(ATB[:, k, :].rearrange("p (a b) -> p a b", a=2),
                                       PSUM[:, 2 * k:2 * k + 2, :], ACT.Copy).then_inc(o_at, 1)
                group_norm(pair * 4 + 1)
                with act.Fori(0, NT) as t:
                    normed(t, pch(t), l1_xn)
                act.wait_ge(rt_dve, pair * 10 + 5)
                act.activation(RW, RW, ACT.Sigmoid).then_inc(rt_act, 1)
                group_norm(pair * 4 + 2)
                with act.Fori(0, NT // 2) as i:
                    for k in range(2):
                        t = i * 2 + k
                        act.wait_ge(in_mm, reuse(pair * NT + t))
                        normed(t, img(i_xn[:, k, :]), in_xn)
                with act.Fori(0, NT // 2) as i:
                    for k in range(2):
                        t = i * 2 + k
                        act.wait_ge(d1_sum, after(pair * NT + t))
                        act.activation(pch(t, XBASE), img(d_acc[:, k, :]), ACT.Silu, bias=vc("conv2d_b")).then_inc(d1_act, 1)

                def step(i, b, there):
                    T = [pair * NT + i * 2 + k for k in range(2)]
                    if there(-2):
                        for k in range(2):
                            act.wait_ge(d2_var, after(T[k] - 4))
                            act.wait_ge(d2_y, reuse(T[k] - 4))
                            act.activation(d_rs[:, k, :], PSUM[:, 4 + k, :], ACT.Ln, bias=GNE[:, 1:2]).then_inc(d2_ln, 1)
                        for k in range(2):
                            act.wait_ge(d2_ln, after(T[k] - 4))
                            act.activation(d_rs[:, k, :], d_rs[:, k, :], ACT.Exp, scale=-0.5).then_inc(d2_rs, 1)
                    if there(-1):
                        for k in range(2):
                            act.wait_ge(d2_cen, after(T[k] - 2))
                            act.wait_ge(d2_var, reuse(T[k] - 2))
                            act.activation(d_sq[:, k, :], PSUM[:, 2 + k, :], ACT.Square).then_inc(d2_sq, 1)
                    if there(-2):
                        for k in range(2):
                            act.wait_ge(d2_y, after(T[k] - 4))
                            act.activation(d_y[:, k, :], d_y[:, k, :], ACT.Gelu, bias=vc("dw_ln_b")).then_inc(d2_g, 1)

                in_turn(act, NT // 2, 0, 2, step)
                sample_and_scan_act(act, pair)
                group_norm(pair * 4 + 3)
                act.wait_ge(border, pair * 2 + 3)
                settle(act)
                with act.Fori(0, NT) as t:
                    normed(t, pch(t), l3_xn)

        @block.tensor
        def _(pe):
            credit(pe, ln0_cen, ln0_var, sp_lgt, sp_tr, sp_fold, mh_s, mh_pt, mh_pv, o_tr, o_mm, l1_mm, in_mm, d1_mm,
                   d2_mm, d2_cen, d2_var, d2_off, l3_mm)
            credit(pe, df_tr, df_w, df_acc, sc_z, sc_bc, sc_cen, sc_var)
            pe.reg_mov(far_pe_turn, 0)
            pe.reg_mov(far_pe_done, 0)
            pe.wait_ge(load, 16 * 9)
            pe.wait_ge(const_dve, 5)
            pe.matmul(PSUM[:, 0, 0:C], DTS[:, 0:2 * C], DTS[:, 2 * C:3 * C], start=True, stop=True)
            pe.matmul(PSUM[:, 1, 0:1], PLAIN[:, :], vc("out_ln_b"), start=True, stop=True)
            pe.matmul(PSUM[:, 2, 0:P], cs("center"), WOUT[:, :], start=True, stop=True).then_inc(const_pe, 1)
            pe.wait_ge(const_ready, 1)

            def group_norm(n):
                pe.wait_ge(gn_dve, n * 5 + 1)
                pe.matmul(PSUM[:, 7, 0:1], cs("pair"), SM[:, 0:1], start=True, stop=True).then_inc(gn_pe, 1)
                pe.wait_ge(gn_dve, n * 5 + 3)
                pe.matmul(PSUM[:, 7, 1:2], cs("pair"), SM[:, 3:4], start=True, stop=True).then_inc(gn_pe, 1)

            def conv(k, w, t, base=BASE, first=0):
                for j in range(first, NTAP):
                    dy, dx = TAPS[j]
                    ins = pe.matmul(img(PSUM[:, k, :]), w[:, j - first, :], pch(t, base, dy, dx), start=(j == first),
                                    stop=(j == NTAP - 1))
                return ins

            with pe.Fori(0, PAIRS) as pair:
                group_norm(pair * 4)

                def step(i, b, there):
                    T = [pair * NT + i * 2 + k for k in range(2)]
                    if there(0):
                        for k in range(2):
                            pe.wait_ge(ln0_xn, after(T[k]))
                            pe.wait_ge(ln0_cc, reuse(T[k]))
                            pe.matmul(PSUM[:, k, :], cs("center"), n_xn[:, k, :], start=True,
                                      stop=True).then_inc(ln0_cen, 1)
                    if there(-1):
                        for k in range(2):
                            pe.wait_ge(ln0_sq, after(T[k] - 2))
                            pe.wait_ge(ln0_ln, reuse(T[k] - 2))
                            pe.matmul(PSUM[:, 4 + k, :], cs("mean"), n_sq[:, k, :], start=True, stop=True).then_inc(ln0_var, 1)

                in_turn(pe, NT // 2, 0, 1, step)
                pe.wait_ge(tok_dve, (pair + 1) * 2 * NS)
                settle(pe)

                def step(i, b, there):
                    S = [pair * NS + i * 2 + k for k in range(2)]
                    if there(0):
                        for k in range(2):
                            pe.wait_ge(sp_stage, after(S[k]))
                            pe.wait_ge(sp_log, reuse(S[k]))
                            for j in range(8):
                                rhs = STB[:, bass.ds(i * 2 + k, 3), :, 2 * j:2 * j + 4].rearrange("p r s c -> p s r c")
                                ins = pe.matmul(PSUM[:, k, j * 24:(j + 1) * 24].rearrange("p (s r c) -> p s r c", s=2, r=3),
                                                STG[:, k, j * P:(j + 1) * P], rhs, start=True, stop=True)
                            ins.then_inc(sp_lgt, 1)
                            pe.wait_ge(sp_pixt, reuse(S[k]))
                            for j in range(8):
                                ins = pe.transpose(PSUM[:, 2 + 2 * k + j // 4, (j % 4) * P:(j % 4 + 1) * P],
                                                   STG[:, k, j * P:(j + 1) * P], ident)
                            ins.then_inc(sp_tr, 1)
                    if there(-1):
                        for k in range(2):
                            pe.wait_ge(sp_e, after(S[k] - 2))
                            pe.wait_ge(sp_pixt, after(S[k] - 2))
                            pe.wait_ge(sp_acc, reuse(S[k] - 2))
                            for j in range(8):
                                pe.matmul(PSUM[:, 6 + k, 0:P], PIXT[:, k, j * P:(j + 1) * P], EXPD[:, k, j, :],
                                          start=(j == 0), stop=(j == 7))
                            for j in range(8):
                                ins = pe.matmul(PSUM[:, 6 + k, P:2 * P], cs("one"), EXPD[:, k, j, :],
                                                start=(j == 0), stop=(j == 7))
                            ins.then_inc(sp_fold, 1)

                in_turn(pe, NS // 2, 0, 1, step)
                pe.wait_ge(sf_dve, pair * 3 + 3)
                pe.matmul(PSUM[:, 0, 0:TOK], WQ[:, :], SFC, start=True, stop=True)
                pe.matmul(PSUM[:, 0, TOK:2 * TOK], WK[:, :], SFC, start=True, stop=True)
                for h in range(2):
                    ins = pe.matmul(PSUM[:, 1, h * P:(h + 1) * P], SFC[:, h * P:(h + 1) * P], WV[:, :],
                                    start=True, stop=True)
                ins.then_inc(mha_pe, 1)
                pe.wait_ge(mha_act, pair * 2 + 1)
                pe.matmul(PSUM[:, 7, 0:TOK], cs("zero"), SFC, start=True, stop=False, skip_group_check=True)

                def step(i, b, there):
                    N = [pair * NH + i * 2 + k for k in range(2)]
                    if there(1):
                        for k in range(2):
                            pe.wait_ge(mh_qm, after(N[k] + 2))
                            if there(-1):
                                pe.wait_ge(mh_exp, after(N[k] - 2))
                            for h in range(2):
                                ins = pe.matmul(PSUM[:, 2 * (1 - b) + k, h * TOK:(h + 1) * TOK], QM[:, k, h * P:(h + 1) * P], KB,
                                                start=True, stop=True)
                            ins.then_inc(mh_s, 1)
                    if there(-1):
                        for k in range(2):
                            pe.wait_ge(mh_pn, after(N[k] - 2))
                            pe.wait_ge(mh_ptc, reuse(N[k] - 2))
                            for kh in range(2):
                                for qh in range(2):
                                    ins = pe.transpose(PSUM[:, 4 + k, (kh * 2 + qh) * P:(kh * 2 + qh + 1) * P],
                                                       PB[:, k, qh, kh * P:(kh + 1) * P], ident)
                            ins.then_inc(mh_pt, 1)
                        for k in range(2):
                            pe.wait_ge(mh_ptc, after(N[k] - 2))
                            pe.wait_ge(mh_vm, after(N[k] - 2))
                            for kh in range(2):
                                ins = pe.matmul(PSUM[:, 7, 0:TOK], VM[:, k, kh, :], PTB[:, k, kh, :],
                                                start=False, stop=False, skip_group_check=True)
                            ins.then_inc(mh_pv, 1)

                in_turn(pe, NH // 2, 1, 1, step)
                pe.matmul(PSUM[:, 7, 0:TOK], cs("zero"), KB, start=False, stop=True,
                          skip_group_check=True).then_inc(mha_pe, 1)
                pe.wait_ge(mha_act, pair * 2 + 2)
                pe.matmul(PSUM[:, 6, 0:TOK], WPROJ[:, :], OB, start=True, stop=True).then_inc(mha_pe, 1)
                pe.wait_ge(so_dve, pair * 4 + 3)
                for j in range(NS):
                    ins = pe.transpose(PSUM[:, j // 4, (j % 4) * P:(j % 4 + 1) * P], SFB[:, j, :], ident)
                ins.then_inc(so_pe, 1)

                def step(i, b, there):
                    S = [pair * NS + i * 2 + k for k in range(2)]
                    if there(-1):
                        for k in range(2):
                            pe.wait_ge(o_at, after(S[k] - 2))
                            pe.wait_ge(o_x, reuse(S[k] - 2))
                            for j in range(2):
                                ins = pe.matmul(PSUM[:, 4 + 2 * k + j, :], WST[:, k, :], ATB[:, k, j * CH:(j + 1) * CH],
                                                start=True, stop=True)
                            ins.then_inc(o_mm, 1)
                    if there(0):
                        for k in range(2):
                            pe.wait_ge(o_e, after(S[k]))
                            pe.wait_ge(o_at, reuse(S[k]))
                            for j in range(8):
                                ins = pe.transpose(PSUM[:, 2 * k + j // 4, (j % 4) * P:(j % 4 + 1) * P], EXPD[:, k, j, :], ident)
                            ins.then_inc(o_tr, 1)

                in_turn(pe, NS // 2, 0, 1, step)
                group_norm(pair * 4 + 1)
                pe.wait_ge(l1_pool, pair * (NS + 1) + NS)
                for h in range(2):
                    ins = pe.matmul(PSUM[:, 0, h * 32:(h + 1) * 32], POOLED[:, h * P:(h + 1) * P],
                                    WCONV[:, :, :].rearrange("p a b -> p (a b)"), start=True, stop=True)
                ins.then_inc(rt_pe, 1)
                pe.wait_ge(rt_dve, pair * 10 + 2)
                pe.wait_ge(fc_in, pair * 16 + 16)
                for o in range(RED):
                    for h in range(2):
                        ins = pe.matmul(PSUM[0:2, 1, 0:FC], RB[:, h, :].rearrange("p (s o) -> p o s", s=2)[:, o, :],
                                        FCT[:, o, h, :], start=(o + h == 0), stop=(o == RED - 1 and h == 1))
                ins.then_inc(rt_pe, 1)
                pe.wait_ge(rt_dve, pair * 10 + 3)
                for s in range(2):
                    for e in range(EXPERTS):
                        ins = pe.matmul(PSUM[s * C:(s + 1) * C, 2, e:e + 1], FS[0:2, e * C:(e + 1) * C],
                                        ident[0:2, s:s + 1], start=True, stop=True)
                ins.then_inc(rt_pe, 1)
                pe.wait_ge(rt_dve, pair * 10 + 10)
                for j in range(9):
                    ins = pe.transpose(PSUM[:, 3 + j // 4, (j % 4) * P:(j % 4 + 1) * P], WE[:, j, :], ident)
                ins.then_inc(rt_pe, 1)
                pe.wait_ge(l1_pool, (pair + 1) * (NS + 1))
                settle(pe)
                with pe.Fori(0, NT // 2) as i:
                    for k in range(2):
                        t = i * 2 + k
                        pe.wait_ge(l1_x, reuse(pair * NT + t))
                        conv(k, WL1, t).then_inc(l1_mm, 1)
                group_norm(pair * 4 + 2)
                with pe.Fori(0, NT // 2) as i:
                    for k in range(2):
                        T = pair * NT + i * 2 + k
                        pe.wait_ge(in_xn, after(T))
                        pe.wait_ge(in_cp, reuse(T))
                        pe.matmul(PSUM[:, k, :], WIN[:, :], i_xn[:, k, :], start=True, stop=True).then_inc(in_mm, 1)
                pe.wait_ge(in_cp, (pair + 1) * NT + CREDIT)
                settle(pe)
                with pe.Fori(0, NT // 2) as i:
                    for k in range(2):
                        t = i * 2 + k
                        pe.wait_ge(d1_sum, reuse(pair * NT + t))
                        conv(k, WDW1, t, first=DW1_VECTOR).then_inc(d1_mm, 1)
                pe.wait_ge(border, pair * 2 + 2)
                settle(pe)

                def step(i, b, there):
                    T = [pair * NT + i * 2 + k for k in range(2)]

                    def taps(k):
                        if there(0):
                            pe.wait_ge(d2_xb, reuse(T[k]))
                            conv(k, WDW2, i * 2 + k, XBASE, first=DW2_VECTOR).then_inc(d2_mm, 1)

                    taps(0)
                    if there(-1):
                        for k in range(2):
                            pe.wait_ge(d2_xb, after(T[k] - 2))
                            pe.wait_ge(d2_y, reuse(T[k] - 2))
                            pe.matmul(PSUM[:, 2 + k, :], cs("center"), d_xb[:, k, :], start=True, stop=True).then_inc(d2_cen, 1)
                    taps(1)
                    if there(-1):
                        for k in range(2):
                            pe.wait_ge(d2_sq, after(T[k] - 2))
                            pe.wait_ge(d2_ln, reuse(T[k] - 2))
                            pe.matmul(PSUM[:, 4 + k, :], cs("mean"), d_sq[:, k, :], start=True, stop=True).then_inc(d2_var, 1)
                    if there(-2):
                        for k in range(2):
                            pe.wait_ge(d2_g, after(T[k] - 4))
                            pe.wait_ge(d2_o, reuse(T[k] - 4))
                            for y in range(ROWS):
                                ins = pe.matmul(PSUM[:, 6 + k, y * 16:(y + 1) * 16], d_y[:, k, y * W:(y + 1) * W],
                                                WOFF[:, :, :, :].rearrange("p a s g -> p (a s g)"), start=True, stop=True)
                            ins.then_inc(d2_off, 1)

                in_turn(pe, NT // 2, 0, 2, step)
                pe.wait_ge(rad_dve, pair * 5 + 1)
                pe.matmul(PSUM[0:1, 0, 0:P], SM[:, 16:17], ident, start=True, stop=True).then_inc(rad_pe, 1)
                pe.wait_ge(rad_dve, pair * 5 + 2)
                pe.matmul(PSUM[:, 0, P:P + 1], cs("one")[0:1, :], SM[0:1, 17:18], start=True, stop=True).then_inc(rad_pe, 1)
                pe.wait_ge(rad_dve, pair * 5 + 5)
                sample_and_scan_pe(pe, pair)
                group_norm(pair * 4 + 3)
                pe.wait_ge(l3_xn, (pair + 1) * NT + CREDIT)
                settle(pe)
                with pe.Fori(0, NT // 2) as i:
                    for k in range(2):
                        t = i * 2 + k
                        pe.wait_ge(l3_o, reuse(pair * NT + t))
                        conv(k, WL3, t).then_inc(l3_mm, 1)


def constants():
    import numpy as np
    c = np.zeros((P, NCST), np.float32)
    i = np.arange(P)

    def put(name, a):
        at, n = CST[name]
        c[:, at:at + n] = a

    same = (i[:, None] // C == i[None, :] // C).astype(np.float32)
    put("ident", np.eye(P))
    put("center", np.eye(P) - same / C)
    put("mean", same / C)
    put("pair", (i[:, None] // 2 == i[None, :] // 2) * 0.5)
    put("one", 1.0)
    put("group4", i[:, None] // 4 == i[None, :] // 4)
    put("mask3", same * ((i[:, None] - i[None, :]) % 4 == 0))
    put("headcol", i[:, None] // HD == np.arange(NH)[None, :])
    put("headrow", (np.arange(2 * P - HD)[None, :] // HD == (P - HD) // HD) * np.ones((P, 1)))
    put("shift", np.array([[-1.0, 0.0, 1.0]]))
    put("col", i[:, None])
    put("row", np.arange(H)[None, :])
    return c


def selections():
    import numpy as np
    r, t, c = np.ogrid[0:WROWS, 0:NTAP, 0:P]
    group = c // (C // GROUP)
    near = ((r // SG) % HALF == t % HALF) & (r % SG == group)
    r, t = r[0:ROWS * SG], t[:, 0:ROWS]
    far = (r // SG == t) & (r % SG == group)
    return near.astype(np.float32), far.astype(np.float32)


def kernel(**a):
    import numpy as np
    import concourse.bacc as bacc
    from concourse.bass_utils import run_bass_kernel_spmd

    f = {n: np.asarray(v) for n, v in a.items()}
    g = {n: f[k] for n, k in (
        ("ln_w", "L0_conv_ln_w"), ("ln_b", "L0_conv_ln_b"), ("proj_b", "L0_conv_proj_b"), ("conv2d_b", "L2_conv_conv2d_b"),
        ("dw_b", "L2_conv_dw_b"), ("dw_ln_g", "L2_conv_dw_ln_g"), ("dw_ln_b", "L2_conv_dw_ln_b"), ("dt_b", "L2_conv_dt_b"),
        ("A_logs", "L2_conv_A_logs"), ("Ds", "L2_conv_Ds"), ("out_ln_g", "L2_conv_out_ln_g"),
        ("out_ln_b", "L2_conv_out_ln_b"))}
    g["fc_b"] = f["L1_conv_fc_b"].reshape(EXPERTS, C).T
    g["conv2d_w"] = f["L2_conv_conv2d_w"].reshape(C, 9)
    g["dw_w"] = f["L2_conv_dw_w"].reshape(C, 9)
    g["experts"] = f["L1_conv_w_experts"].reshape(EXPERTS, C, 36).transpose(1, 0, 2)
    g["l3_b"] = f["L3_conv_b"]
    vec = np.concatenate([g[n].reshape(C, VEC[n][1]) for n in VEC], axis=1)
    qkv = f["L0_conv_qkv_w"].reshape(3, C, C)
    m = {"q": qkv[0].T, "k": qkv[1].T, "v": qkv[2].T, "proj": f["L0_conv_proj_w"].T, "in_proj": f["L2_conv_in_proj_w"].T,
         "off": f["L2_conv_off_w"].T, "out_proj": f["L2_conv_out_proj_w"].T, "conv": f["L1_conv_conv_w"].reshape(RED, C).T,
         "x_proj": f["L2_conv_x_proj_w"].T, "w1": f["L3_conv_w1"].T,
         "w3": f["L3_conv_w3"].reshape(C, C, 9).transpose(1, 2, 0).reshape(C, 9 * C)}
    mat = np.concatenate([m[n] for n in MAT], axis=1)
    xp = f["L2_conv_x_proj_w"][:DT_RANK]
    dts = np.concatenate([xp, xp, f["L2_conv_dt_w"].T], axis=1)
    off_b = f["L2_conv_off_b"].reshape(GROUP, 2).T.reshape(2, 1, GROUP)
    off_b = np.broadcast_to(off_b, (ROWS, 2, 2, GROUP)).reshape(-1)
    rows = np.concatenate([f["L1_conv_conv_b"], f["L1_conv_conv_b"], off_b])
    rows = np.broadcast_to(rows[None, :], (P, rows.size))
    fc = f["L1_conv_fc_w"].reshape(FC, RED, 2, P).transpose(3, 1, 2, 0)
    near, far = selections()
    arrays = {"x": f["x"].reshape(BATCH * C, H, W), "vec": vec, "mat": mat, "dts": dts, "rows": rows, "fc": fc, "sel": near, "far_sel": far,
              "cst": constants()}
    arrays = {n: np.ascontiguousarray(v) for n, v in arrays.items()}
    nc = bacc.Bacc("TRN2", target_bir_lowering=False, num_devices=1)
    aps = [nc.dram_tensor(n, v.shape, mybir.dt.from_np(v.dtype), kind="ExternalInput").ap() for n, v in arrays.items()]
    out = nc.dram_tensor("out", (BATCH * C, H, W), F32, kind="ExternalOutput").ap()
    program(nc, *aps, out)
    r = run_bass_kernel_spmd(nc, [arrays], core_ids=[0])
    return r.results[0]["out"].reshape(BATCH, C, H, W)
```

```python
from contextlib import ExitStack

import concourse.bass as bass
from concourse import mybir

F32 = mybir.dt.float32
BF16 = mybir.dt.bfloat16
I32 = mybir.dt.int32
ALU = mybir.AluOpType
ACT = mybir.ActivationFunctionType
AX = mybir.AxisListType

BATCH, C, H, W = 4, 64, 128, 128
P = 2 * C
PAIRS = BATCH // 2
PIX = H * W
ROWS = 4
CH = ROWS * W
NT = H // ROWS
NS = H // 8
TW = NS + 2
TOK = NS * NS
HEADS, HD = 8, 8
NH = 2 * HEADS
GROUP = 4
SG = 2 * GROUP
EXPERTS, RED, FC = 4, 16, 256
DT_RANK = 8
PW = W + 2
BASE = 5
XBASE = 1
PROWS = H + BASE + 1
GN_EPS, LN_EPS = 1e-5, 1e-6
MAXR = 128
TAPS = [(dy, dx) for dy in (-1, 0, 1) for dx in (-1, 0, 1)]
NTAP = len(TAPS)
HALF = 5
PARTS = 3
WROWS = PARTS * HALF * SG
DW1_VECTOR, DW2_VECTOR = 4, 5
PE_TAPS = 4

VEC = {}
_at = 0
for _name, _n in (("ln_w", 1), ("ln_b", 1), ("proj_b", 1), ("conv2d_b", 1), ("dw_b", 1), ("dw_ln_g", 1),
                  ("dw_ln_b", 1), ("dt_b", 1), ("A_logs", 1), ("Ds", 1), ("out_ln_g", 1), ("out_ln_b", 1),
                  ("fc_b", EXPERTS), ("conv2d_w", 9), ("dw_w", 9), ("experts", EXPERTS * 36), ("l3_b", C)):
    VEC[_name] = (_at, _n)
    _at += _n
NVEC = _at
MAT = {}
_at = 0
for _name, _n in (("q", C), ("k", C), ("v", C), ("proj", C), ("in_proj", C), ("off", 2 * GROUP), ("out_proj", C),
                  ("conv", RED), ("x_proj", DT_RANK + 2), ("w1", C), ("w3", 9 * C)):
    MAT[_name] = (_at, _n)
    _at += _n
NMAT = _at
CST = {}
_at = 0
for _name, _n in (("ident", P), ("center", P), ("mean", P), ("pair", P), ("one", P), ("zero", P), ("group4", P),
                  ("mask3", P), ("same", P), ("headcol", NH), ("headrow", 2 * P - HD), ("shift", 3), ("col", 1), ("row", H)):
    CST[_name] = (_at, _n)
    _at += _n
NCST = _at

NREG = 10720
CREDIT = 2


def after(t):
    return t + 1 + CREDIT


def reuse(t):
    return t - 1 + CREDIT


def program(nc, x, vec, mat, dts, rows, fc, sel, far_sel, cst, out):
    ctx = ExitStack()
    with ctx:
        def sb(name, shape, dt=F32):
            return ctx.enter_context(nc.sbuf_tensor(name, shape, dt))

        def sem(name):
            return ctx.enter_context(nc.semaphore(name))

        X = sb("X", [P, H, W])
        PAD = sb("PAD", [P, PROWS, PW])
        VECS = sb("VECS", [P, NVEC])
        DTS = sb("DTS", [DT_RANK, 3 * C])
        ROWV = sb("ROWV", [P, 2 * RED + 4 * 16])
        CSTS = sb("CSTS", [P, NCST])
        WQ, WK, WV, WPROJ, WIN, WZ, WB, WC = (sb(n, [P, P]) for n in
            ("WQ", "WK", "WV", "WPROJ", "WIN", "WZ", "WB", "WC"))
        WOUT2, GNE = sb("WOUT2", [P, P]), sb("GNE", [P, 2])
        WOFF = sb("WOFF", [P, 2, 2, GROUP])
        WCONV = sb("WCONV", [P, 2, RED])
        WDW1 = sb("WDW1", [P, NTAP - DW1_VECTOR, P])
        WDW2 = sb("WDW2", [P, NTAP - DW2_VECTOR, P])
        WL3 = sb("WL3", [P, 3, 4, P])
        STATS = sb("STATS", [P, NT, 6])
        SM = sb("SM", [P, 64])
        OUTB = sb("OUTB", [P, 1])
        SELB = sb("SELB", [WROWS, NTAP, P], BF16)
        FSEL = sb("FSEL", [ROWS * SG, ROWS, P])
        IDB = sb("IDB", [P, P], BF16)
        RI = sb("RI", [P, 1], I32)
        REG = sb("REG", [P, NREG])
        MATS = REG[:, 0:NMAT]
        PLAIN, NOT3, WOUT = (REG[:, NMAT + j * P:NMAT + (j + 1) * P] for j in range(3))
        SELF = REG[0:WROWS, NMAT + 3 * P:NMAT + 3 * P + NTAP * P]
        W3 = REG[:, NMAT + 12 * P:NMAT + 21 * P].rearrange("p (y x o) -> p y x o", y=3, x=3)
        W3H = REG[:, NMAT + 21 * P:NMAT + 24 * P].rearrange("p (y o) -> p y o", y=3)

        def cs(name):
            a, n = CST[name]
            return CSTS[:, a:a + n]

        def vc(name, j=0, n=1):
            a = VEC[name][0] + j
            return VECS[:, a:a + n]

        def mt(name, lo=0, hi=P):
            a, n = MAT[name]
            return MATS[lo:hi, a:a + n]

        ident = cs("ident")
        PSUM = ctx.enter_context(nc.psum_tensor("PSUM", [P, 8, 512], F32))

        class Region:
            def __init__(self):
                self.at = 0

            def take(self, *shape):
                n = 1
                for d in shape:
                    n *= d
                a = REG[:, self.at:self.at + n]
                self.at += n
                assert self.at <= NREG, self.at
                if len(shape) == 2:
                    a = a.rearrange("p (a b) -> p a b", a=shape[0])
                if len(shape) == 3:
                    a = a.rearrange("p (a b c) -> p a b c", a=shape[0], b=shape[1])
                if len(shape) == 4:
                    a = a.rearrange("p (a b c d) -> p a b c d", a=shape[0], b=shape[1], c=shape[2])
                return a

        r = Region()
        VC = r.take(2, 4, 10 * (W // 2)).rearrange("p k m (r j) -> p k m r j", r=10)
        cols_end = r.at
        r = Region()
        n_xn, n_sq, n_rs, n_y = (r.take(2, CH) for _ in range(4))
        n_cen = r.take(2, 2, CH)
        r = Region()
        AFF = r.take(NS, NS, 9)
        EXPD = r.take(2, 8, 2 * C)
        SFAS = r.take(2, TW * TW)
        SUMS = r.take(NS, NS)
        STB = r.take(TW, 2, TW)
        both = r.at
        STG = r.take(2, 1024)
        PIXT = r.take(2, 1024)
        LG = r.take(2, NS, 9)
        SMX = STATS.rearrange("p t n -> p (t n)")[:, 0:6 * NS].rearrange("p (k j n) -> p k j n", k=2, j=3)
        r.at = both
        SFC, QB, KB, OB = (r.take(TOK) for _ in range(4))
        VB = r.take(2, P)
        QM = r.take(2, TOK)
        PB = r.take(2, 2, TOK)
        PTB = r.take(2, 2, TOK)
        VM = r.take(2, 2, P)
        MHS = r.take(2, 6)
        r.at = both - 2 * TW * TW
        SOP = r.take(TW, TW)
        SFB = r.take(NS, 2 * C)
        STT = r.take(NS, P)
        ATB = SFB.rearrange("p a b -> p (a b)").rearrange("p (k n) -> p k n", k=2)
        WST = r.take(2, P)
        r = Region()
        FCT = r.take(RED, 2, FC)
        POOLED = r.take(TOK)
        RB = r.take(2, 2 * RED)
        FS = r.take(FC)
        RW = r.take(EXPERTS)
        CW = r.take(36)
        CU = r.take(12, 4)
        CH2 = r.take(3, 4)
        r.at = cols_end
        WE = r.take(12, P)
        WL1 = r.take(3, 4, P)
        r = Region()
        OFF = r.take(H, 16)
        l2at = r.at
        i_xn = r.take(2, CH)
        r.at = l2at
        d_acc, d_xb, d_sq, d_rs, d_y = (r.take(2, CH) for _ in range(5))
        r.at = l2at
        MXR = r.take(P)
        r.at = l2at
        HT = r.take(3, 64)
        W9 = r.take(ROWS, 2 * HALF, SG)
        WPART = r.take(ROWS, WROWS).bitcast(BF16).rearrange("p y (h n) -> p y h n", h=2)
        WTB = r.take(2, CH).bitcast(BF16)
        prd_at = r.at
        PRD = r.take(4, CH)
        l2_more = r.at
        r.at = prd_at + CH
        FAR = r.take(3, ROWS * SG)
        CUR = r.take(4)
        FWT = r.take(W)
        r.at = l2_more
        XS = r.take(2, CH)
        AB, RL, DA, UU, HH, YY, RS2 = (r.take(CH) for _ in range(7))
        ACC, ZB, BB, CB, MB, OB2 = 2, 3, 4, 5, 6, 7
        TB = PSUM[0:WROWS, ACC, :].bitcast(BF16)
        r = Region()
        r.at = cols_end
        OBUF = r.take(2, 2 * CH)

        load = sem("load")
        const_ready = sem("const_ready")
        settled = sem("settled")
        const_pe = sem("const_pe")
        const_act = sem("const_act")
        const_dve = sem("const_dve")
        x_in = [sem(f"x_in{j}") for j in range(4)]
        stats_done = sem("stats_done")
        gn_dve, gn_pe, gn_act = sem("gn_dve"), sem("gn_pe"), sem("gn_act")

        def steps(*ns):
            return [sem(n) for n in ns]

        ln0_xn, ln0_cen, ln0_cc, ln0_sq, ln0_var, ln0_ln, ln0_rs, ln0_y, ln0_yb = steps(
            "ln0_xn", "ln0_cen", "ln0_cc", "ln0_sq", "ln0_var", "ln0_ln", "ln0_rs", "ln0_y", "ln0_yb")
        (sp_stage, sp_lgt, sp_tr, sp_pixt, sp_log, sp_mx, sp_sub, sp_exp, sp_sum, sp_rec, sp_aff, sp_e, sp_fold,
         sp_acc) = steps("sp_stage", "sp_lgt", "sp_tr", "sp_pixt", "sp_log", "sp_mx", "sp_sub", "sp_exp", "sp_sum",
                         "sp_rec", "sp_aff", "sp_e", "sp_fold", "sp_acc")
        tok_dve, tok_zero = sem("tok_dve"), sem("tok_zero")
        sf_dve = sem("sf_dve")
        mha_pe, mha_act = sem("mha_pe"), sem("mha_act")
        mh_qm, mh_s, mh_mx, mh_nmx, mh_exp, mh_rec, mh_pn, mh_pt, mh_ptc, mh_vm, mh_pv = steps(
            "mh_qm", "mh_s", "mh_mx", "mh_nmx", "mh_exp", "mh_rec", "mh_pn", "mh_pt", "mh_ptc", "mh_vm", "mh_pv")
        so_dve, so_pe, so_act, so_zero = sem("so_dve"), sem("so_pe"), sem("so_act"), sem("so_zero")
        o_e, o_tr, o_at, o_mm, o_x = steps("o_e", "o_tr", "o_at", "o_mm", "o_x")
        fc_in = sem("fc_in")
        l1_xn = sem("l1_xn")
        cv_vector, cv_pool, cv_mm, cv_part, cv_done = (sem(n) for n in (
            "cv_vector", "cv_pool", "cv_mm", "cv_part", "cv_done"))
        l1_pool = sem("l1_pool")
        rt_pe, rt_dve, rt_act = sem("rt_pe"), sem("rt_dve"), sem("rt_act")
        in_xn, in_mm, in_cp = steps("in_xn", "in_mm", "in_cp")
        d1_mm, d1_sum, d1_act = steps("d1_mm", "d1_sum", "d1_act")
        d1_tap, d2_tap = ([sem(f"{n}{k}") for k in range(2)] for n in ("d1_tap", "d2_tap"))
        border = sem("border")
        d2_mm, d2_xb, d2_cen, d2_sq, d2_var, d2_ln, d2_rs, d2_y, d2_g, d2_off, d2_o = steps(
            "d2_mm", "d2_xb", "d2_cen", "d2_sq", "d2_var", "d2_ln", "d2_rs", "d2_y", "d2_g", "d2_off", "d2_o")
        far_step, far_w, far_tr, far_wt, far_b = (sem(n) for n in ("far_step", "far_w", "far_tr", "far_wt", "far_b"))
        rad_dve, rad_pe = sem("rad_dve"), sem("rad_pe")
        (df_zero, df_abs, df_hat, df_w9, df_hi, df_r1, df_mid, df_lo, df_tr, df_wt, df_w, df_p, df_acc, df_xs,
         df_add) = (sem(n) for n in ("df_zero", "df_abs", "df_hat", "df_w9", "df_hi", "df_r1", "df_mid", "df_lo",
                                     "df_tr", "df_wt", "df_w", "df_p", "df_acc", "df_xs", "df_add"))
        far_xs = sem("far_xs")
        (sc_z, sc_bc, sc_abs, sc_exp, sc_ln, sc_delta, sc_u, sc_da, sc_bx, sc_h, sc_hc, sc_y, sc_cen, sc_proj, sc_sq, sc_var,
         sc_lv, sc_rs, sc_t, sc_x) = (sem(n) for n in (
            "sc_z", "sc_bc", "sc_abs", "sc_exp", "sc_ln", "sc_delta", "sc_u", "sc_da", "sc_bx", "sc_h", "sc_hc",
            "sc_y", "sc_cen", "sc_proj", "sc_sq", "sc_var", "sc_lv", "sc_rs", "sc_t", "sc_x"))
        l3_xn = sem("l3_xn")
        out_dma = [sem(f"out_dma{k}") for k in range(2)]

        def settle(eng):
            eng.sem_inc(settled, 1)

        far_dve_step, far_dve_turn = nc.vector.alloc_register("far_dve_step"), nc.vector.alloc_register("far_dve_turn")
        far_pe_turn = nc.tensor.alloc_register("far_pe_turn")
        far_pe_done = nc.tensor.alloc_register("far_pe_done")

        def credit(eng, *sems):
            for s in sems:
                eng.sem_inc(s, CREDIT)

        block = ctx.enter_context(nc.Block())

        def xch(t):
            return X[:, bass.ds(t * ROWS, ROWS), :]

        def pch(t, base=BASE, dy=0, dx=0):
            return PAD[:, bass.ds(t * ROWS + (base + dy), ROWS), 1 + dx:1 + dx + W]

        def img(a):
            return a.rearrange("p (r w) -> p r w", r=ROWS)

        def in_turn(eng, n, ahead, behind, step):
            lo = behind + behind % 2
            hi = n - ahead - (n - ahead) % 2

            def peeled(first, last):
                for i in range(first, last):
                    step(i, i % 2, lambda d: 0 <= i + d < n)

            peeled(-ahead, lo)
            with eng.Fori(lo // 2, hi // 2) as j:
                for b in range(2):
                    step(j * 2 + b, b, lambda d: True)
            peeled(hi, n + behind)

        NM, RSTD = SM[:, 4:5], SM[:, 5:6]

        @block.sync
        def _(sp):
            for lo in (0, C):
                sp.dma_start(VECS[lo:lo + C, :], vec).then_inc(load, 16)
                sp.dma_start(MATS[lo:lo + C, :], mat).then_inc(load, 16)
            sp.dma_start(DTS[:, :], dts).then_inc(load, 16)
            sp.dma_start(ROWV[:, :], rows).then_inc(load, 16)
            sp.dma_start(CSTS[:, :], cst).then_inc(load, 16)
            sp.dma_start(SELF, sel.rearrange("r t c -> r (t c)")).then_inc(load, 16)
            sp.dma_start(FSEL[:, :, :], far_sel).then_inc(load, 16)
            for k in range(2):
                sp.sem_inc(out_dma[k], 16)

            def load_quarter(j, first_row):
                sp.dma_start(X[:, j * H // 4:(j + 1) * H // 4, :],
                             x[bass.ds(first_row, P), j * H // 4:(j + 1) * H // 4, :]).then_inc(x_in[j], 16)

            for j in range(4):
                load_quarter(j, 0)
            with sp.Fori(0, PAIRS) as pair:
                sp.wait_ge(o_x, pair * NS + NS + CREDIT)
                sp.dma_start(FCT, fc).then_inc(fc_in, 16)
                for j in range(4):
                    with sp.Fori(j * NS // 8, (j + 1) * NS // 8) as i:
                        for k in range(2):
                            sp.wait_ge(cv_done, after(pair * (2 * NS) + i * 2 + (k + NS)))
                            sp.dma_start(out[bass.ds(pair * P, P), bass.ds((i * 2 + k) * 8, 8), :],
                                         OBUF[:, k, :].rearrange("p (r w) -> p r w", r=8)).then_inc(out_dma[k], 16)
                    with sp.If(pair < PAIRS - 1):
                        load_quarter(j, nc.s_assert_within(pair * P + P, 0, (PAIRS - 1) * P,
                                                           skip_runtime_bounds_check_because="the branch was taken"))
            for k in range(2):
                sp.wait_ge(out_dma[k], 16 * (PAIRS * NS // 2 + 1))

        def expand(dve, k, st):
            a = AFF[:, bass.ds(st, 1), :, :].rearrange("p o (j s) (r c) -> p (o j) s r c", s=2, r=3)
            for b in range(2):
                for s in range(2):
                    first = EXPD[b * 64:b * 64 + 64, k, 0, s * C + b:s * C + b + 1]
                    v = bass.AP(first.tensor, first.offset, [list(first.ap[0]), [2 * C + 2, 8], [TW, 3], [1, 3]])
                    ins = dve.tensor_scalar(v, a[b * 64:b * 64 + 64, :, s, :, :], 1.0, None, ALU.mult)
            return ins

        def far_dve(dve, t, k, reach):
            oy, ox, fy = (FAR[:, j, :].rearrange("p (y g) -> p y g", y=ROWS) for j in range(3))

            def link(ins):
                ins.then_inc(far_step, 1)
                dve.reg_add(far_dve_step, far_dve_step, 1)
                dve.wait_ge(far_step, dve.snap(far_dve_step, min_val=1))

            def hat(a):
                link(dve.scalar_tensor_tensor(out=a, in0=a, scalar=-1.0, in1=a, op0=ALU.mult, op1=ALU.min))
                link(dve.tensor_scalar(a, a, 1.0, 0.0, ALU.add, ALU.max))

            def one_row(ys, e):
                ys = nc.s_assert_within(ys, 0, H - 1, skip_runtime_bounds_check_because="both branches were taken")
                link(dve.tensor_scalar(fy, oy, CUR[:, 0:1], None, ALU.subtract))
                hat(fy)
                dve.tensor_tensor(fy, fy, ox, ALU.mult).then_inc(far_w, 1)
                dve.reg_add(far_dve_turn, far_dve_turn, 1)
                turn = dve.snap(far_dve_turn, min_val=1)
                dve.wait_ge(far_tr, turn)
                dve.tensor_scalar(FWT[0:ROWS * SG, :], PSUM[0:ROWS * SG, BB, 0:W], 1.0, None, ALU.mult).then_inc(far_wt, 1)
                dve.wait_ge(far_b, turn)
                src = PAD[:, :, :].rearrange("p r w -> p (r w)")[:, bass.ds(ys * PW + (e - reach) + (XBASE * PW + 1), W)]
                link(dve.tensor_tensor(img(PRD[:, 0, :]), img(PSUM[:, ZB, :]),
                                       src.unsqueeze(1).broadcast_to([P, ROWS, W]), ALU.mult))
                link(dve.tensor_tensor(XS[:, k, :], XS[:, k, :], PRD[:, 0, :], ALU.add))
                settle(dve)

            off = OFF[:, bass.ds(t * ROWS, ROWS), :].rearrange("p y (a g) -> p y a g", a=2)
            row = CST["row"][0]
            link(dve.memset(XS[:, k, :], 0.0))
            link(dve.tensor_tensor(oy, off[:, :, 1, :],
                                   CSTS[:, bass.ds(t * ROWS + row, ROWS)].unsqueeze(2).broadcast_to([P, ROWS, SG]), ALU.add))
            link(dve.tensor_scalar(CUR[:, 1:2], SM[:, 19:20], 1.0, None, ALU.mult))
            settle(dve)
            with dve.Fori(0, reach * 2 + 1) as e:
                link(dve.tensor_tensor(CUR[:, 2:3], cs("col"), CUR[:, 1:2], ALU.add))
                link(dve.tensor_scalar(CUR[:, 3:4], CUR[:, 2:3], 0.0, None, ALU.is_ge))
                link(dve.tensor_scalar(CUR[:, 2:3], CUR[:, 2:3], W - 1.0, None, ALU.is_le))
                link(dve.tensor_tensor(CUR[:, 2:3], CUR[:, 2:3], CUR[:, 3:4], ALU.mult))
                link(dve.tensor_scalar(ox, off[:, :, 0, :], CUR[:, 1:2], None, ALU.subtract))
                hat(ox)
                link(dve.tensor_scalar(ox, ox, CUR[:, 2:3], None, ALU.mult))
                link(dve.tensor_tensor(CUR[:, 0:1], CSTS[:, bass.ds(t * ROWS + row, 1)], SM[:, 19:20], ALU.add))
                settle(dve)
                with dve.Fori(0, reach * 2 + ROWS) as d:
                    ys = dve.snap(t * ROWS + d - reach)
                    with dve.If(ys >= 0):
                        with dve.If(ys < H):
                            one_row(ys, e)
                    link(dve.tensor_scalar(CUR[:, 0:1], CUR[:, 0:1], 1.0, None, ALU.add))
                link(dve.tensor_scalar(CUR[:, 1:2], CUR[:, 1:2], 1.0, None, ALU.add))
            dve.sem_inc(far_xs, 1)

        def far_pe(pe, t, reach):
            with pe.Fori(0, reach * 2 + 1) as _:
                with pe.Fori(0, reach * 2 + ROWS) as d:
                    ys = pe.snap(t * ROWS + d - reach)
                    with pe.If(ys >= 0):
                        with pe.If(ys < H):
                            pe.reg_add(far_pe_turn, far_pe_turn, 1)
                            turn = pe.snap(far_pe_turn, min_val=1)
                            pe.wait_ge(far_w, turn)
                            pe.transpose(PSUM[0:ROWS * SG, BB, 0:P], FAR[:, 2, :], ident).then_inc(far_tr, 1)
                            pe.wait_ge(far_wt, turn)
                            for y in range(ROWS):
                                ins = pe.matmul(PSUM[:, ZB, y * W:(y + 1) * W], FSEL[:, y, :],
                                                FWT[0:ROWS * SG, :], start=True, stop=True)
                            ins.then_inc(far_b, 1)
            pe.reg_add(far_pe_done, far_pe_done, 1)
            pe.wait_ge(far_xs, pe.snap(far_pe_done, min_val=1))
            settle(pe)

        def columns(c):
            rows = bass.ds(c * 8 + (BASE - 1), 10)
            d0, d1 = (PAD[:, rows, 0:W].rearrange("p r (j e) -> p e r j", e=2)[:, e] for e in range(2))
            d2, d3 = (PAD[:, rows, 2:W + 2].rearrange("p r (j e) -> p e r j", e=2)[:, e] for e in range(2))
            return d0, d1, d2, d3

        def strip_of(pair, layer, c):
            return pair * (2 * NS) + (c + layer * NS)

        def columns_ready(eng, pair, layer, c):
            if layer:
                last = min(2 * c + 2, NT - 1) if isinstance(c, int) else c * 2 + 2
                eng.wait_ge(l3_xn, after(pair * NT + last))

        def columns_dve(dve, pair, layer, c, k):
            d0, d1, d2, d3 = columns(c)
            columns_ready(dve, pair, layer, c)
            dve.wait_ge(cv_mm, reuse(strip_of(pair, layer, c)))
            dve.tensor_tensor(VC[:, k, 1], d1, d2, ALU.add)
            dve.tensor_tensor(VC[:, k, 2], d2, d1, ALU.subtract).then_inc(cv_vector, 1)

        def columns_pool(pool, pair, layer):
            def step(c, k, there):
                d0, d1, d2, d3 = columns(c)
                columns_ready(pool, pair, layer, c)
                pool.wait_ge(cv_mm, reuse(strip_of(pair, layer, c)))
                pool.tensor_tensor(VC[:, k, 0], d0, d2, ALU.subtract)
                pool.tensor_tensor(VC[:, k, 3], d1, d3, ALU.subtract).then_inc(cv_pool, 1)

            with pool.Fori(0, NS // 2 - 1) as i:
                for k in range(2):
                    step(i * 2 + k, k, None)
            for k in range(2):
                step(NS - 2 + k, k, None)

        def columns_pe(pe, pair, layer, w):
            with pe.Fori(0, NS // 2) as i:
                for k in range(2):
                    S = strip_of(pair, layer, i * 2 + k)
                    pe.wait_ge(cv_vector, after(S))
                    pe.wait_ge(cv_pool, after(S))
                    pe.wait_ge(cv_done, reuse(S))
                    for m in range(4):
                        for dy in range(3):
                            ins = pe.matmul(PSUM[:, 4 * k + m, :].rearrange("p (r j) -> p r j", r=8), w[:, dy, m, :],
                                            VC[:, k, m, dy:dy + 8, :], start=(dy == 0), stop=(dy == 2))
                    ins.then_inc(cv_mm, 1)

        def halves(a):
            v = a.rearrange("p r (j e) -> p e r j", e=2)
            return v[:, 0], v[:, 1]

        def add_columns(dve, S, c, k, into, bias=None):
            res, to = halves(X[:, bass.ds(c * 8, 8), :]), halves(into)
            m = [PSUM[:, 4 * k + j, :].rearrange("p (r j) -> p r j", r=8) for j in range(4)]
            dve.wait_ge(cv_mm, after(S))
            for n, (e, j, op) in enumerate(((0, 0, ALU.add), (1, 1, ALU.add), (0, 1, ALU.add), (1, 2, ALU.subtract),
                                            (0, 2, ALU.add), (1, 3, ALU.subtract))):
                if n < 2:
                    if bias is None:
                        ins = dve.tensor_tensor(to[e], res[e], m[j], op)
                    else:
                        ins = dve.scalar_tensor_tensor(out=to[e], in0=m[j], scalar=bias, in1=res[e], op0=ALU.add, op1=op)
                else:
                    dve.wait_ge(cv_part, S * 5 + (n - 1 + CREDIT))
                    ins = dve.tensor_tensor(to[e], to[e], m[j], op)
                ins.then_inc(cv_part if n < 5 else cv_done, 1)

        def pipeline(eng, step):
            in_turn(eng, NT, 2, 4, step)

        def turn(T, q):
            return T * NTAP + (q + 1 + CREDIT)

        def summed(T, m, n):
            return T * n + (m + 1 + CREDIT)

        PE_SUMS, POOL_SUMS = PE_TAPS, NTAP - 1 - PE_TAPS

        def product_buffer(q):
            return q % 2 if q < PE_TAPS else 2 + (q - PE_TAPS - 1) % 2

        assert PE_SUMS % 2 == 0 and POOL_SUMS % 2 == 0

        def sample_and_scan_dve(dve, pair, stats):
            dve.memset(W9, 0.0).then_inc(df_zero, 1)
            settle(dve)
            reach = dve.value_load(RI[0:1, 0:1], min_val=0, max_val=MAXR)

            def step(c, k, on):
                T = pair * NT + c

                def product(q):
                    if not on(0):
                        return
                    dy, dx = TAPS[q]
                    dve.wait_ge(df_w, turn(T, q))
                    if q == PE_TAPS:
                        dve.wait_ge(sc_y, reuse(T))
                        o = XS[:, k, :]
                    else:
                        if q < 2:
                            dve.wait_ge(df_acc, summed(T - 1, PE_SUMS - 2 + q, PE_SUMS))
                        elif q < PE_TAPS:
                            dve.wait_ge(df_acc, summed(T, q - 2, PE_SUMS))
                        elif q < PE_TAPS + 3:
                            dve.wait_ge(df_add, summed(T - 1, POOL_SUMS - 2 + (q - PE_TAPS - 1), POOL_SUMS))
                        else:
                            dve.wait_ge(df_add, summed(T, q - PE_TAPS - 3, POOL_SUMS))
                        o = PRD[:, product_buffer(q), :]
                    dve.tensor_tensor(img(o), img(PSUM[:, (k + q) % 2, :]), pch(c, XBASE, dy, dx),
                                      ALU.mult).then_inc(df_p, 1)

                product(0)
                if on(-4):
                    dve.wait_ge(sc_rs, after(T - 4))
                    dve.wait_ge(sc_proj, after(T - 4))
                    dve.tensor_tensor(RS2, PSUM[:, OB2, :], RS2, ALU.mult).then_inc(sc_t, 1)
                product(1)
                if on(-4):
                    dve.wait_ge(sc_t, after(T - 4))
                    dve.scalar_tensor_tensor(out=xch(c - 4), in0=img(RS2), scalar=OUTB[:, :], in1=xch(c - 4),
                                             op0=ALU.add, op1=ALU.add).then_inc(sc_x, 1)
                product(2)
                if on(-2):
                    dve.wait_ge(sc_u, after(T - 2))
                    dve.wait_ge(sc_bc, after(T - 2))
                    dve.tensor_tensor(UU, UU, PSUM[:, BB, :], ALU.mult).then_inc(sc_bx, 1)
                product(3)
                if on(-2):
                    dve.wait_ge(sc_bx, after(T - 2))
                    dve.wait_ge(sc_da, after(T - 2))
                    dve.tensor_tensor_scan(HH, DA, UU, SM[:, 12:13], ALU.mult, ALU.add).then_inc(sc_h, 1)
                    dve.wait_ge(sc_h, after(T - 2))
                    dve.tensor_copy(SM[:, 12:13], HH[:, CH - 1:CH])
                    dve.tensor_tensor(UU, HH, PSUM[:, CB, :], ALU.mult).then_inc(sc_hc, 1)
                    dve.wait_ge(sc_hc, after(T - 2))
                    dve.wait_ge(sc_proj, after(T - 3))
                    dve.scalar_tensor_tensor(out=YY, in0=XS[:, k, :], scalar=vc("Ds"), in1=UU,
                                             op0=ALU.mult, op1=ALU.add).then_inc(sc_y, 1)
                if on(-1):
                    settle(dve)
                    with dve.If(reach > 0):
                        if on(0):
                            dve.wait_ge(df_acc, summed(T, PE_SUMS - 1, PE_SUMS))
                        dve.wait_ge(df_add, summed(T - 1, POOL_SUMS - 1, POOL_SUMS))
                        far_dve(dve, c - 1, (k + 1) % 2, reach)
                product(4)
                product(5)
                if on(0):
                    dve.wait_ge(df_acc, summed(T, PE_SUMS - 1, PE_SUMS))
                    dve.wait_ge(df_p, turn(T, PE_TAPS))
                    dve.tensor_tensor(XS[:, k, :], XS[:, k, :], PSUM[:, ACC, :], ALU.add).then_inc(df_xs, 1)
                product(6)
                if on(-4):
                    dve.wait_ge(sc_x, after(T - 4))
                    stats(c - 4, c - 4)
                product(7)
                if on(-1):
                    dve.wait_ge(sc_ln, after(T - 1))
                    dve.tensor_tensor(RL, RL, AB, ALU.add).then_inc(sc_delta, 1)
                product(8)

            pipeline(dve, step)

        def sample_and_scan_pool(pool, pair):
            ht = HT.rearrange("p d (y a g) -> p d y a g", y=ROWS, a=2)
            w9 = W9.rearrange("p y d g -> p y (d g)")
            w9h = w9.rearrange("p y (h n) -> p (y h) n", h=2)

            def part(j):
                return WPART.rearrange("p y h n -> p (y h) n")[:, :, j * HALF * SG:(j + 1) * HALF * SG]

            pool.wait_ge(rad_dve, pair * 5 + 5)
            pool.wait_ge(df_zero, pair + 1)

            def step(c, k, on):
                T = pair * NT + c
                if on(1):
                    pool.wait_ge(df_hat, after(T + 1))
                    pool.wait_ge(df_lo, after(T))
                    for j in range(3):
                        ins = pool.tensor_tensor(
                            W9[:, :, 3 * j:3 * j + 3, :].rearrange("p y d g -> p d y g"),
                            ht[:, j, :, 1, :].unsqueeze(1).broadcast_to([P, 3, ROWS, SG]), ht[:, :, :, 0, :], ALU.mult)
                    ins.then_inc(df_w9, 1)
                if on(1):
                    pool.wait_ge(df_hi, after(T + 1))
                    pool.tensor_tensor(w9h, w9h, part(0), ALU.subtract).then_inc(df_r1, 1)
                    pool.wait_ge(df_mid, after(T + 1))
                    pool.tensor_tensor(part(2), w9h, part(1), ALU.subtract).then_inc(df_lo, 1)

                def add(m):
                    if on(0):
                        q = PE_TAPS + 1 + m
                        pool.wait_ge(df_p, turn(T, q))
                        if m == 0:
                            pool.wait_ge(df_xs, after(T))
                        else:
                            pool.wait_ge(df_add, summed(T, m - 1, POOL_SUMS))
                        pool.tensor_tensor(XS[:, k, :], XS[:, k, :], PRD[:, product_buffer(q), :], ALU.add).then_inc(df_add, 1)

                for m in range(POOL_SUMS):
                    add(m)
                if on(-1):
                    pool.wait_ge(sc_delta, after(T - 1))
                    pool.wait_ge(sc_y, after(T - 2))
                    pool.tensor_tensor(UU, RL, XS[:, (k + 1) % 2, :], ALU.mult).then_inc(sc_u, 1)
            pipeline(pool, step)

        def sample_and_scan_act(act, pair):
            act.wait_ge(rad_dve, pair * 5 + 5)
            settle(act)
            w9h = W9.rearrange("p y (h d) g -> p (y h) (d g)", h=2)
            offs = OFF.rearrange("p y n -> p (y n)")

            def part(j):
                return WPART.rearrange("p y h n -> p (y h) n")[:, :, j * HALF * SG:(j + 1) * HALF * SG]

            def step(c, k, on):
                T = pair * NT + c
                if on(-3):
                    act.wait_ge(sc_cen, after(T - 3))
                    act.wait_ge(sc_x, after(T - 4))
                    act.activation(RS2, PSUM[:, MB, :], ACT.Square).then_inc(sc_sq, 1)
                if on(1):
                    act.wait_ge(df_w9, after(T + 1))
                    act.wait_ge(df_tr, after(T))
                    act.activation(part(0), w9h, ACT.Copy).then_inc(df_hi, 1)
                    act.wait_ge(df_r1, after(T + 1))
                    act.activation(part(1), w9h, ACT.Copy).then_inc(df_mid, 1)
                if on(2):
                    act.wait_ge(df_w9, after(T + 1))
                    for j in range(3):
                        ins = act.activation(HT[:, j, :], offs[:, bass.ds((c + 2) * 64, 64)], ACT.Abs,
                                             bias=cs("shift")[:, 2 - j:3 - j])
                    ins.then_inc(df_abs, 1)
                    act.wait_ge(df_abs, after(T + 2))
                    act.activation(HT, HT, ACT.Relu, bias=1.0, scale=-1.0).then_inc(df_hat, 1)
                if on(-1):
                    act.wait_ge(sc_z, after(T - 1))
                    act.activation(AB, PSUM[:, ZB, :], ACT.Abs, bias=vc("dt_b")).then_inc(sc_abs, 1)
                    act.wait_ge(sc_u, after(T - 2))
                    act.wait_ge(sc_da, after(T - 2))
                    act.activation(RL, PSUM[:, ZB, :], ACT.Relu, bias=vc("dt_b"))
                    act.wait_ge(sc_abs, after(T - 1))
                    act.activation(AB, AB, ACT.Exp, scale=-1.0).then_inc(sc_exp, 1)
                    act.wait_ge(sc_exp, after(T - 1))
                    act.activation(AB, AB, ACT.Ln, bias=1.0).then_inc(sc_ln, 1)
                if on(1):
                    act.wait_ge(df_tr, after(T + 1))
                    act.activation(WTB[0:WROWS, (k + 1) % 2, :], TB, ACT.Copy).then_inc(df_wt, 1)
                if on(-3):
                    act.wait_ge(sc_var, after(T - 3))
                    act.activation(RS2, PSUM[:, MB, :], ACT.Ln, bias=GNE[:, 1:2]).then_inc(sc_lv, 1)
                    act.wait_ge(sc_lv, after(T - 3))
                    act.activation(RS2, RS2, ACT.Exp, scale=-0.5).then_inc(sc_rs, 1)
                if on(-1):
                    act.wait_ge(sc_delta, after(T - 1))
                    act.wait_ge(sc_h, after(T - 2))
                    act.activation(DA, RL, ACT.Exp, scale=SM[:, 9:10]).then_inc(sc_da, 1)

            pipeline(act, step)

        def sample_and_scan_pe(pe, pair):
            settle(pe)
            reach = pe.value_load(RI[0:1, 0:1], min_val=0, max_val=MAXR)

            def step(c, k, on):
                T = pair * NT + c

                def spread(q):
                    if on(0):
                        h = q // HALF
                        if q == 0:
                            pe.wait_ge(df_wt, after(T))
                        pe.wait_ge(df_p, turn(T, q - 2))
                        pe.matmul(PSUM[:, (k + q) % 2, :], SELB[:, q, :], WTB[0:WROWS, k, h * CH:(h + 1) * CH],
                                  start=True, stop=True).then_inc(df_w, 1)

                def add_up(m):
                    if on(0):
                        pe.wait_ge(df_p, turn(T, m))
                        pe.matmul(PSUM[:, ACC, :], ident, PRD[:, m % 2, :], start=(m == 0),
                                  stop=(m == PE_SUMS - 1)).then_inc(df_acc, 1)

                spread(0)
                spread(1)
                if on(-3):
                    pe.wait_ge(sc_y, after(T - 3))
                    pe.wait_ge(sc_lv, after(T - 4))
                    pe.matmul(PSUM[:, MB, :], cs("center"), YY, start=True, stop=True).then_inc(sc_cen, 1)
                spread(2)
                add_up(0)
                if on(-3):
                    pe.wait_ge(sc_t, after(T - 4))
                    pe.matmul(PSUM[:, OB2, :], WOUT2[:, :], YY, start=True, stop=True).then_inc(sc_proj, 1)
                for m in range(1, PE_SUMS):
                    spread(2 + m)
                    add_up(m)
                if on(-1):
                    pe.wait_ge(df_add, summed(T - 1, POOL_SUMS - 1, POOL_SUMS))
                    pe.wait_ge(sc_exp, after(T - 2))
                    pe.wait_ge(sc_bx, after(T - 2))
                    settle(pe)
                    with pe.If(reach > 0):
                        far_pe(pe, c - 1, reach)
                    pe.matmul(PSUM[:, ZB, :], WZ[:, :], XS[:, (k + 1) % 2, :], start=True, stop=True).then_inc(sc_z, 1)
                    pe.matmul(PSUM[:, BB, :], WB[:, :], XS[:, (k + 1) % 2, :], start=True, stop=True)
                    pe.wait_ge(sc_hc, after(T - 2))
                    pe.matmul(PSUM[:, CB, :], WC[:, :], XS[:, (k + 1) % 2, :], start=True, stop=True).then_inc(sc_bc, 1)
                spread(6)
                spread(7)
                if on(1):
                    pe.wait_ge(df_lo, after(T + 1))
                    pe.wait_ge(df_xs, after(T))
                    for h in range(2):
                        for y in range(ROWS):
                            ins = pe.transpose(TB[:, (h * ROWS + y) * W:(h * ROWS + y + 1) * W], WPART[:, y, h, :], IDB[:, :])
                    ins.then_inc(df_tr, 1)
                if on(-3):
                    pe.wait_ge(sc_sq, after(T - 3))
                    pe.matmul(PSUM[:, MB, :], cs("mean"), RS2, start=True, stop=True).then_inc(sc_var, 1)
                spread(8)

            pipeline(pe, step)

        def taps_done(i, j, n):
            return i * n + (j + 1 + CREDIT)

        def vector_tap(dve, i, t, j, n, acc, base, weights, done):
            dy, dx = TAPS[j]
            if j == 0:
                ins = dve.tensor_scalar(img(acc), pch(t, base, dy, dx), vc(weights, 0), None, ALU.mult)
            else:
                dve.wait_ge(done, taps_done(i, j - 1, n))
                ins = dve.scalar_tensor_tensor(out=img(acc), in0=pch(t, base, dy, dx), scalar=vc(weights, j), in1=img(acc),
                                               op0=ALU.mult, op1=ALU.add)
            ins.then_inc(done, 1)

        @block.vector
        def _(dve):
            credit(dve, ln0_xn, ln0_cc, ln0_y, *d1_tap, d1_sum, *d2_tap, d2_xb, sp_log, sp_mx, sp_sub, sp_sum, sp_rec, sp_aff, sp_e, sp_acc, mh_qm, mh_mx, mh_nmx,
                   mh_rec, mh_pn, mh_vm, o_e, o_x, in_cp, d2_y, d2_o, cv_vector, cv_part, cv_done)
            credit(dve, sc_delta, df_p, df_xs, sc_bx, sc_h, sc_hc, sc_y, sc_t, sc_x)
            dve.reg_mov(far_dve_step, 0)
            dve.reg_mov(far_dve_turn, 0)
            dve.wait_ge(load, 16 * 9)
            for w in (WQ, WK, WV, WPROJ, WIN, WOUT, WZ, WB, WC):
                dve.memset(w[:, :], 0.0)
            dve.tensor_copy(SELB[:, :, :].rearrange("p t c -> p (t c)"), SELF)
            dve.tensor_copy(IDB[:, :], ident)
            dve.memset(WOFF[:, :, :, :], 0.0)
            dve.memset(WCONV[:, :, :], 0.0)
            dve.memset(PLAIN[:, :], 0.0)
            dve.memset(SM[:, :], 0.0)
            dve.memset(GNE[:, 0:1], GN_EPS)
            dve.memset(GNE[:, 1:2], LN_EPS)
            dve.memset(W3, 0.0).then_inc(const_dve, 1)
            dve.tensor_scalar(NOT3[:, :], cs("mask3"), -1.0, 1.0, ALU.mult, ALU.add).then_inc(const_dve, 1)
            dve.wait_ge(const_dve, 2)
            for s in range(2):
                p, q = s * C, s * C + C
                for w, name in ((WQ, "q"), (WK, "k"), (WV, "v"), (WPROJ, "proj"), (WIN, "in_proj"), (PLAIN, "out_proj")):
                    dve.tensor_copy(w[p:q, p:q], mt(name, p, q))
                dve.tensor_copy(WOFF[p:q, :, s, :], mt("off", p, q).rearrange("p (g a) -> p a g", a=2))
                dve.tensor_copy(WCONV[p:q, s, :], mt("conv", p, q))
                xp = MAT["x_proj"][0]
                for w, col in ((WB, DT_RANK), (WC, DT_RANK + 1)):
                    dve.tensor_copy(w[p:q, p:q], MATS[p:q, xp + col:xp + col + 1].broadcast_to([C, C]))
                dve.tensor_scalar(WOUT[p:q, p:q], mt("out_proj", p, q), vc("out_ln_g")[p:q], None, ALU.mult)
                for y in range(3):
                    dve.tensor_tensor(W3[p:q, y, :, p:q], mt("w3", p, q).rearrange("p (y x o) -> p y x o", y=3, x=3)[:, y],
                                      cs("mask3")[p:q, p:q].unsqueeze(1).broadcast_to([C, 3, C]), ALU.mult)
                dve.tensor_tensor(NOT3[p:q, p:q], mt("w1", p, q), NOT3[p:q, p:q], ALU.mult).then_inc(const_dve, 1)
            dve.wait_ge(const_dve, 4)
            for s in range(2):
                p, q = s * C, s * C + C
                dve.tensor_tensor(W3[p:q, 1, 1, p:q], W3[p:q, 1, 1, p:q], NOT3[p:q, p:q], ALU.add)
            dve.tensor_tensor(W3H, W3[:, :, 0, :], W3[:, :, 2, :], ALU.add)
            dve.tensor_copy(WL3[:, :, 0, :], W3[:, :, 0, :])
            dve.tensor_copy(WL3[:, :, 3, :], W3[:, :, 2, :]).then_inc(const_dve, 1)
            dve.wait_ge(const_dve, 5)
            dve.tensor_scalar(W3H, W3H, 0.5, None, ALU.mult).then_inc(const_dve, 1)
            dve.wait_ge(const_dve, 6)
            for m, half in ((1, 0.5), (2, -0.5)):
                dve.scalar_tensor_tensor(out=WL3[:, :, m, :], in0=W3[:, :, 1, :], scalar=half, in1=W3H,
                                         op0=ALU.mult, op1=ALU.add)
            for w, name, first in ((WDW1, "conv2d_w", DW1_VECTOR), (WDW2, "dw_w", DW2_VECTOR)):
                for j in range(first, NTAP):
                    dve.tensor_scalar(w[:, j - first, :], ident, vc(name, j), None, ALU.mult)
            dve.tensor_reduce(SM[:, 8:9], vc("l3_b", 0, C), AX.X, ALU.add).then_inc(const_dve, 1)
            dve.wait_ge(const_pe, 1)
            for s in range(2):
                p, q = s * C, s * C + C
                dve.tensor_copy(WZ[p:q, p:q], PSUM[p:q, 0, 0:C])
            dve.tensor_copy(OUTB[:, :], PSUM[:, 1, 0:1])
            dve.tensor_copy(WOUT2[:, :], PSUM[:, 2, 0:P])
            dve.wait_ge(const_act, 1)
            dve.tensor_scalar(SM[:, 9:10], SM[:, 10:11], -1.0, None, ALU.mult).then_inc(const_ready, 1)

            def group_norm(n):
                dve.wait_ge(stats_done, (n + 1) * NT)
                settle(dve)
                dve.bn_aggr(SM[:, 0:2], STATS[:, :, :]).then_inc(gn_dve, 1)
                dve.wait_ge(gn_pe, n * 2 + 1)
                dve.wait_ge(gn_dve, n * 5 + 1)
                dve.tensor_tensor(SM[:, 2:3], SM[:, 0:1], PSUM[:, 7, 0:1], ALU.subtract).then_inc(gn_dve, 1)
                dve.wait_ge(gn_dve, n * 5 + 2)
                dve.scalar_tensor_tensor(out=SM[:, 3:4], in0=SM[:, 2:3], scalar=SM[:, 2:3], in1=SM[:, 1:2],
                                         op0=ALU.mult, op1=ALU.add).then_inc(gn_dve, 1)
                dve.wait_ge(gn_act, n + 1)
                dve.reciprocal(SM[:, 5:6], SM[:, 6:7]).then_inc(gn_dve, 1)
                dve.wait_ge(gn_dve, n * 5 + 4)
                dve.scalar_tensor_tensor(out=SM[:, 4:5], in0=PSUM[:, 7, 0:1], scalar=-1.0, in1=SM[:, 5:6],
                                         op0=ALU.mult, op1=ALU.mult).then_inc(gn_dve, 1)

            def stats(t, s):
                dve.bn_stats(STATS[:, bass.ds(s, 1), :], xch(t)).then_inc(stats_done, 1)

            with dve.Fori(0, PAIRS) as pair:
                for j in range(4):
                    dve.wait_ge(x_in[j], pair * 16 + 16)
                    settle(dve)
                    with dve.Fori(j * NT // 4, (j + 1) * NT // 4) as t:
                        dve.bn_stats(STATS[:, bass.ds(t, 1), :], xch(t)).then_inc(stats_done, 1)
                group_norm(pair * 4)
                dve.wait_ge(gn_dve, pair * 20 + 5)
                for k in range(2):
                    dve.wait_ge(out_dma[k], pair * (NS * 8) + 16)
                settle(dve)

                def step(i, b, there):
                    T = [pair * NT + i * 2 + k for k in range(2)]
                    if there(0):
                        for k in range(2):
                            dve.wait_ge(ln0_cen, reuse(T[k]))
                            dve.tensor_scalar(img(n_xn[:, k, :]), xch(i * 2 + k), RSTD, NM, ALU.mult,
                                              ALU.add).then_inc(ln0_xn, 1)
                    if there(-1):
                        for k in range(2):
                            dve.wait_ge(ln0_cen, after(T[k] - 2))
                            if there(-2):
                                dve.wait_ge(ln0_y, reuse(T[k] - 4))
                            dve.tensor_scalar(n_cen[:, 1 - b, k, :], PSUM[:, k, :], 1.0, None, ALU.mult).then_inc(ln0_cc, 1)
                    if there(-2):
                        for k in range(2):
                            dve.wait_ge(ln0_rs, after(T[k] - 4))
                            dve.wait_ge(ln0_yb, reuse(T[k] - 4))
                            dve.scalar_tensor_tensor(out=n_y[:, k, :], in0=n_cen[:, b, k, :], scalar=vc("ln_w"),
                                                     in1=n_rs[:, k, :], op0=ALU.mult, op1=ALU.mult).then_inc(ln0_y, 1)

                in_turn(dve, NT // 2, 0, 2, step)
                dve.wait_ge(ln0_yb, (pair + 1) * NT + CREDIT)
                dve.memset(STB, 0.0)
                dve.memset(SFAS, 0.0)
                dve.memset(EXPD, 0.0).then_inc(tok_zero, 1)
                dve.wait_ge(tok_zero, pair + 1)
                settle(dve)
                with dve.Fori(0, NS) as i:
                    dve.tensor_reduce(SUMS[:, bass.ds(i, 1), :],
                                      PAD[:, bass.ds(i * 8 + BASE, 8), 1:1 + W].rearrange("p r (b q) -> p b r q", q=8),
                                      AX.XY, ALU.add).then_inc(tok_dve, 1)
                dve.wait_ge(tok_dve, pair * (NS + 1) + NS)
                for s in range(2):
                    p, q = s * C, s * C + C
                    ins = dve.tensor_scalar(STB[p:q, 1:1 + NS, s, 1:1 + NS], SUMS[p:q], 1.0, None, ALU.mult)
                ins.then_inc(tok_dve, 1)

                def step(i, b, there):
                    S = [pair * NS + i * 2 + k for k in range(2)]
                    st = [i * 2 + k for k in range(2)]
                    if there(0):
                        for k in range(2):
                            dve.wait_ge(sp_lgt, after(S[k]))
                            v = PSUM[:, k, 0:8 * 24].rearrange("p (a r c) -> p a r c", r=3, c=4)
                            o = LG[:, k, :, :].rearrange("p a (r c) -> p a r c", r=3)
                            dve.tensor_copy(o[0:64], v[0:64, :, :, 0:3])
                            dve.tensor_copy(o[64:128], v[64:128, :, :, 1:4]).then_inc(sp_log, 1)
                        for k in range(2):
                            dve.wait_ge(sp_log, after(S[k]))
                            dve.tensor_reduce(SMX[:, k, 0, :], LG[:, k, :, :], AX.X, ALU.max).then_inc(sp_mx, 1)
                        for k in range(2):
                            dve.wait_ge(sp_mx, after(S[k]))
                            dve.tensor_tensor(LG[:, k, :, :], LG[:, k, :, :],
                                              SMX[:, k, 0, :].unsqueeze(2).broadcast_to([P, NS, 9]),
                                              ALU.subtract).then_inc(sp_sub, 1)
                        for k in range(2):
                            dve.wait_ge(sp_exp, after(S[k]))
                            dve.tensor_reduce(SMX[:, k, 1, :], LG[:, k, :, :], AX.X, ALU.add).then_inc(sp_sum, 1)
                        for k in range(2):
                            dve.wait_ge(sp_sum, after(S[k]))
                            dve.reciprocal(SMX[:, k, 2, :], SMX[:, k, 1, :]).then_inc(sp_rec, 1)
                        for k in range(2):
                            dve.wait_ge(sp_rec, after(S[k]))
                            dve.tensor_tensor(AFF[:, bass.ds(st[k], 1), :, :].rearrange("p o a b -> p (o a) b"),
                                              LG[:, k, :, :],
                                              SMX[:, k, 2, :].unsqueeze(2).broadcast_to([P, NS, 9]),
                                              ALU.mult).then_inc(sp_aff, 1)
                        for k in range(2):
                            dve.wait_ge(sp_aff, after(S[k]))
                            dve.wait_ge(sp_fold, reuse(S[k]))
                            expand(dve, k, st[k]).then_inc(sp_e, 1)
                    if there(-1):
                        for k in range(2):
                            dve.wait_ge(sp_fold, after(S[k] - 2))
                            dve.wait_ge(sp_acc, after(S[k] - 3))
                            for s in range(2):
                                p, q = s * C, s * C + C
                                v = SFAS[p:q, :, bass.ds((st[k] - 2) * TW, 3 * TW)]
                                ins = dve.tensor_tensor(
                                    v, PSUM[p:q, 6 + k, 0:2 * P].rearrange("p (a b) -> p a b", a=2)[:, :, s * C:s * C + 3 * TW],
                                    v, ALU.add)
                            ins.then_inc(sp_acc, 1)

                in_turn(dve, NS // 2, 0, 1, step)
                dve.wait_ge(sp_acc, (pair + 1) * NS + CREDIT)
                inner = SFAS.rearrange("p a (i j) -> p a i j", i=TW)[:, :, 1:1 + NS, 1:1 + NS]
                dve.tensor_scalar(inner[:, 1], inner[:, 1], 1e-12, None, ALU.add).then_inc(sf_dve, 1)
                dve.wait_ge(sf_dve, pair * 3 + 1)
                dve.reciprocal(inner[:, 1], inner[:, 1]).then_inc(sf_dve, 1)
                dve.wait_ge(sf_dve, pair * 3 + 2)
                dve.wait_ge(sp_fold, (pair + 1) * NS + CREDIT)
                dve.tensor_tensor(SFC.rearrange("p (i j) -> p i j", i=NS), inner[:, 0], inner[:, 1],
                                  ALU.mult).then_inc(sf_dve, 1)
                dve.wait_ge(mha_act, pair * 2 + 1)
                settle(dve)

                def step(i, b, there):
                    h = [i * 2 + k for k in range(2)]
                    N = [pair * NH + h[k] for k in range(2)]
                    if there(-1):
                        for k in range(2):
                            dve.wait_ge(mh_exp, after(N[k] - 2))
                            dve.reciprocal(MHS[:, k, 0:2], MHS[:, k, 4:6]).then_inc(mh_rec, 1)
                        for k in range(2):
                            dve.wait_ge(mh_rec, after(N[k] - 2))
                            dve.tensor_tensor(PB[:, k, :, :], PB[:, k, :, :],
                                              MHS[:, k, 0:2].unsqueeze(2).broadcast_to([P, 2, TOK]),
                                              ALU.mult).then_inc(mh_pn, 1)
                        for k in range(2):
                            dve.wait_ge(mh_pv, reuse(N[k] - 2))
                            a = CST["headrow"][0] + P - HD
                            dve.tensor_tensor(VM[:, k, :, :], VB,
                                              CSTS[:, bass.ds((h[k] - 2) * -HD + a, P)].unsqueeze(1).broadcast_to([P, 2, P]),
                                              ALU.mult).then_inc(mh_vm, 1)
                    if there(1):
                        for k in range(2):
                            dve.wait_ge(mh_s, reuse(N[k] + 2))
                            a = CST["headcol"][0]
                            dve.tensor_scalar(QM[:, k, :], QB, CSTS[:, bass.ds(h[k] + (a + 2), 1)], None,
                                              ALU.mult).then_inc(mh_qm, 1)
                    if there(0):
                        for k in range(2):
                            dve.wait_ge(mh_s, after(N[k]))
                            dve.wait_ge(mh_pn, reuse(N[k]))
                            dve.tensor_reduce(MHS[:, k, 0:2], PSUM[:, 2 * b + k, :].rearrange("p (a b) -> p a b", a=2),
                                              AX.X, ALU.max).then_inc(mh_mx, 1)
                        for k in range(2):
                            dve.wait_ge(mh_mx, after(N[k]))
                            dve.tensor_scalar(MHS[:, k, 2:4], MHS[:, k, 0:2], -HD ** -0.5, None,
                                              ALU.mult).then_inc(mh_nmx, 1)

                in_turn(dve, NH // 2, 1, 1, step)
                dve.wait_ge(mha_pe, pair * 3 + 3)
                dve.memset(SOP, 0.0)
                dve.memset(SFB, 0.0).then_inc(so_dve, 1)
                dve.wait_ge(so_dve, pair * 4 + 1)
                dve.tensor_scalar(SOP[:, 1:1 + NS, 1:1 + NS], PSUM[:, 6, 0:TOK].rearrange("p (i j) -> p i j", i=NS),
                                  vc("proj_b"), None, ALU.add).then_inc(so_dve, 1)
                dve.wait_ge(so_dve, pair * 4 + 2)
                for s in range(2):
                    p, q = s * C, s * C + C
                    for j in range(3):
                        ins = dve.tensor_copy(SFB[p:q, :, s * C + j * TW:s * C + (j + 1) * TW], SOP[p:q, j:j + NS, :])
                ins.then_inc(so_dve, 1)
                dve.wait_ge(so_pe, pair + 1)
                for j in range(4):
                    ins = dve.tensor_copy(STT[:, 4 * j:4 * j + 4, :],
                                          PSUM[:, j, :].rearrange("p (a b) -> p a b", a=4))
                ins.then_inc(so_dve, 1)

                def step(i, b, there):
                    S = [pair * NS + i * 2 + k for k in range(2)]
                    st = [i * 2 + k for k in range(2)]
                    if there(0):
                        for k in range(2):
                            dve.wait_ge(o_tr, reuse(S[k]))
                            expand(dve, k, st[k]).then_inc(o_e, 1)
                    if there(-1):
                        for k in range(2):
                            dve.wait_ge(o_mm, after(S[k] - 2))
                            for j in range(2):
                                v = X[:, bass.ds((st[k] - 2) * 8, 8), j * 64:(j + 1) * 64].rearrange("p r (b q) -> p b r q", q=8)
                                ins = dve.tensor_tensor(
                                    v, PSUM[:, 4 + 2 * k + j, :].rearrange("p (b r q) -> p b r q", b=8, r=8), v, ALU.add)
                            ins.then_inc(o_x, 1)
                        for k in range(2):
                            dve.wait_ge(o_x, after(S[k] - 2))
                            for j in range(2):
                                stats(st[k] * 2 + (j - 4), st[k] * 2 + (j - 4))

                in_turn(dve, NS // 2, 0, 1, step)
                group_norm(pair * 4 + 1)
                dve.wait_ge(o_at, (pair + 1) * NS + CREDIT)
                settle(dve)
                with dve.Fori(0, NS) as i:
                    dve.wait_ge(l1_xn, after(pair * NT + i * 2 + 1))
                    dve.tensor_reduce(POOLED[:, bass.ds(i * NS, NS)],
                                      PAD[:, bass.ds(i * 8 + BASE, 8), 1:1 + W].rearrange("p r (b q) -> p b r q", q=8),
                                      AX.XY, ALU.add).then_inc(l1_pool, 1)
                q0 = pair * 13
                dve.wait_ge(rt_pe, pair * 4 + 1)
                dve.scalar_tensor_tensor(out=RB, in0=PSUM[:, 0, 0:64].rearrange("p (a b) -> p a b", a=2), scalar=1.0 / 64,
                                         in1=ROWV[:, 0:2 * RED].unsqueeze(1).broadcast_to([P, 2, 2 * RED]),
                                         op0=ALU.mult, op1=ALU.add).then_inc(rt_dve, 1)
                dve.wait_ge(rt_dve, q0 + 1)
                dve.tensor_scalar(RB, RB, 0.0, None, ALU.max).then_inc(rt_dve, 1)
                dve.wait_ge(rt_pe, pair * 4 + 2)
                dve.tensor_copy(FS[0:2, :], PSUM[0:2, 1, 0:FC]).then_inc(rt_dve, 1)
                dve.wait_ge(rt_pe, pair * 4 + 3)
                dve.tensor_tensor(RW, PSUM[:, 2, 0:EXPERTS], vc("fc_b", 0, EXPERTS), ALU.add).then_inc(rt_dve, 1)
                dve.wait_ge(rt_dve, q0 + 4)
                dve.tensor_scalar(RW, RW, 0.0, None, ALU.max).then_inc(rt_dve, 1)
                dve.wait_ge(rt_act, pair + 1)
                dve.tensor_scalar(CW, vc("experts", 0, 36), RW[:, 0:1], None, ALU.mult).then_inc(rt_dve, 1)
                for e in range(1, EXPERTS):
                    dve.wait_ge(rt_dve, q0 + 5 + e)
                    dve.scalar_tensor_tensor(out=CW, in0=vc("experts", 36 * e, 36), scalar=RW[:, e:e + 1], in1=CW,
                                             op0=ALU.mult, op1=ALU.add).then_inc(rt_dve, 1)
                dve.wait_ge(rt_dve, q0 + 9)
                w0, w1, w2 = (CW.rearrange("p (i y x) -> p x y i", i=4, y=3)[:, x] for x in range(3))
                cu = CU.rearrange("p (y m) i -> p m y i", m=4)
                dve.tensor_tensor(CH2, w0, w2, ALU.add)
                dve.tensor_copy(cu[:, 0], w0)
                dve.tensor_copy(cu[:, 3], w2).then_inc(rt_dve, 1)
                dve.wait_ge(rt_dve, q0 + 10)
                dve.tensor_scalar(CH2, CH2, 0.5, None, ALU.mult).then_inc(rt_dve, 1)
                dve.wait_ge(rt_dve, q0 + 11)
                for m, half in ((1, 0.5), (2, -0.5)):
                    ins = dve.scalar_tensor_tensor(out=cu[:, m], in0=w1, scalar=half, in1=CH2, op0=ALU.mult, op1=ALU.add)
                ins.then_inc(rt_dve, 1)
                dve.wait_ge(rt_dve, q0 + 12)
                for j in range(12):
                    ins = dve.tensor_tensor(
                        WE[:, j, :].rearrange("p (g i) -> p g i", i=4), CU[:, j, :].unsqueeze(1).broadcast_to([P, 32, 4]),
                        cs("group4").rearrange("p (g i) -> p g i", i=4), ALU.mult)
                ins.then_inc(rt_dve, 1)
                dve.wait_ge(rt_pe, pair * 4 + 4)
                for j in range(3):
                    ins = dve.tensor_copy(WL1[:, j], PSUM[:, 3 + j, :].rearrange("p (a b) -> p a b", a=4))
                ins.then_inc(l1_pool, 1)

                def step(c, k, there):
                    if there(1):
                        columns_dve(dve, pair, 0, c + 1, (k + 1) % 2)
                    if there(-1):
                        S = strip_of(pair, 0, c - 1)
                        add_columns(dve, S, c - 1, (k + 1) % 2, X[:, bass.ds((c - 1) * 8, 8), :])
                        dve.wait_ge(cv_done, after(S))
                        for j in range(2):
                            stats(c * 2 + (j - 2), c * 2 + (j - 2))

                in_turn(dve, NS, 1, 1, step)
                group_norm(pair * 4 + 2)
                with dve.Fori(0, NT // 2) as i:
                    for k in range(2):
                        t = i * 2 + k
                        dve.wait_ge(in_mm, after(pair * NT + t))
                        dve.tensor_scalar(pch(t), img(PSUM[:, k, :]), 1.0, None, ALU.mult).then_inc(in_cp, 1)
                dve.wait_ge(in_cp, (pair + 1) * NT + CREDIT)
                settle(dve)
                with dve.Fori(0, NT // 2) as i:
                    T = [pair * NT + i * 2 + k for k in range(2)]
                    for j in range(DW1_VECTOR):
                        for k in range(2):
                            if j == 0:
                                dve.wait_ge(d1_act, reuse(T[k]))
                            vector_tap(dve, pair * (NT // 2) + i, i * 2 + k, j, DW1_VECTOR, d_acc[:, k, :], BASE,
                                       "conv2d_w", d1_tap[k])
                    for k in range(2):
                        dve.wait_ge(d1_mm, after(T[k]))
                        dve.wait_ge(d1_tap[k], taps_done(pair * (NT // 2) + i, DW1_VECTOR - 1, DW1_VECTOR))
                        dve.tensor_tensor(d_acc[:, k, :], PSUM[:, k, :], d_acc[:, k, :], ALU.add).then_inc(d1_sum, 1)
                dve.wait_ge(border, pair * 2 + 2)
                settle(dve)

                def step(i, b, there):
                    T = [pair * NT + i * 2 + k for k in range(2)]

                    def taps(first, last):
                        if there(0):
                            for j in range(first, last):
                                for k in range(2):
                                    if j == 0:
                                        dve.wait_ge(d2_xb, reuse(T[k]))
                                    vector_tap(dve, pair * (NT // 2) + i, i * 2 + k, j, DW2_VECTOR, d_acc[:, k, :], XBASE,
                                               "dw_w", d2_tap[k])

                    taps(0, DW2_VECTOR // 2)
                    if there(-2):
                        for k in range(2):
                            dve.wait_ge(d2_rs, after(T[k] - 4))
                            dve.wait_ge(d2_off, reuse(T[k] - 4))
                            dve.scalar_tensor_tensor(out=d_y[:, k, :], in0=PSUM[:, 2 + k, :], scalar=vc("dw_ln_g"),
                                                     in1=d_rs[:, k, :], op0=ALU.mult, op1=ALU.mult).then_inc(d2_y, 1)
                    taps(DW2_VECTOR // 2, DW2_VECTOR)
                    if there(0):
                        for k in range(2):
                            dve.wait_ge(d2_mm, after(T[k]))
                            dve.wait_ge(d2_tap[k], taps_done(pair * (NT // 2) + i, DW2_VECTOR - 1, DW2_VECTOR))
                            dve.wait_ge(d2_cen, reuse(T[k]))
                            dve.scalar_tensor_tensor(out=d_xb[:, k, :], in0=PSUM[:, k, :], scalar=vc("dw_b"),
                                                     in1=d_acc[:, k, :], op0=ALU.add, op1=ALU.add).then_inc(d2_xb, 1)
                    if there(-3):
                        for k in range(2):
                            dve.wait_ge(d2_off, after(T[k] - 6))
                            dve.tensor_tensor(OFF[:, bass.ds((i * 2 + k - 6) * ROWS, ROWS), :],
                                              PSUM[:, 6 + k, 0:64].rearrange("p (a b) -> p a b", a=ROWS),
                                              ROWV[:, 2 * RED:].rearrange("p (a b) -> p a b", a=ROWS),
                                              ALU.add).then_inc(d2_o, 1)

                in_turn(dve, NT // 2, 0, 3, step)
                dve.wait_ge(d2_o, (pair + 1) * NT + CREDIT)
                dve.tensor_reduce(SM[:, 16:17], OFF, AX.XY, ALU.max, apply_absolute_value=True).then_inc(rad_dve, 1)
                dve.wait_ge(rad_pe, pair * 2 + 1)
                dve.tensor_reduce(SM[0:1, 17:18], PSUM[0:1, 0, 0:P], AX.X, ALU.max).then_inc(rad_dve, 1)
                dve.wait_ge(rad_pe, pair * 2 + 2)
                dve.tensor_scalar(SM[:, 18:19], PSUM[:, 0, P:P + 1], 1.0, None, ALU.is_gt)
                dve.tensor_scalar(SM[:, 19:20], PSUM[:, 0, P:P + 1], MAXR - 1.0, 1.0, ALU.min, ALU.add).then_inc(rad_dve, 1)
                dve.wait_ge(rad_dve, pair * 5 + 3)
                dve.tensor_tensor(RI[:, :], SM[:, 18:19], SM[:, 19:20], ALU.mult).then_inc(rad_dve, 1)
                dve.wait_ge(rad_dve, pair * 5 + 4)
                dve.tensor_scalar(SM[:, 19:20], RI[:, :], -1.0, None, ALU.mult)
                dve.memset(SM[:, 12:13], 0.0).then_inc(rad_dve, 1)
                dve.wait_ge(rad_dve, pair * 5 + 5)
                sample_and_scan_dve(dve, pair, stats)
                group_norm(pair * 4 + 3)
                dve.wait_ge(border, pair * 2 + 3)
                settle(dve)

                def step(c, k, there):
                    if there(1):
                        columns_dve(dve, pair, 1, c + 1, (k + 1) % 2)
                    if there(-1):
                        S = strip_of(pair, 1, c - 1)
                        b = (k + 1) % 2
                        dve.wait_ge(out_dma[b], pair * (NS * 8) + (c - 1 - b) * 8 + 16)
                        add_columns(dve, S, c - 1, b, OBUF[:, b, :].rearrange("p (r w) -> p r w", r=8), SM[:, 8:9])

                in_turn(dve, NS, 1, 1, step)

        @block.gpsimd
        def _(pool):
            credit(pool, cv_pool, ln0_yb, ln0_sq, df_w9, df_r1, df_lo, df_add, sc_u)
            pool.memset(PAD[:, :, :], 0.0).then_inc(border, 1)
            with pool.Fori(0, PAIRS) as pair:
                def step(i, b, there):
                    T = [pair * NT + i * 2 + k for k in range(2)]
                    if there(-1):
                        for k in range(2):
                            pool.wait_ge(ln0_cc, after(T[k] - 2))
                            pool.wait_ge(ln0_var, reuse(T[k] - 2))
                            v = n_cen[:, 1 - b, k, :]
                            pool.tensor_tensor(n_sq[:, k, :], v, v, ALU.mult).then_inc(ln0_sq, 1)
                    if there(-2):
                        for k in range(2):
                            pool.wait_ge(ln0_y, after(T[k] - 4))
                            pool.tensor_tensor(pch(i * 2 + k - 4), img(n_y[:, k, :]),
                                               vc("ln_b").unsqueeze(2).broadcast_to([P, ROWS, W]), ALU.add).then_inc(ln0_yb, 1)

                pool.wait_ge(border, pair * 2 + 1)
                settle(pool)
                in_turn(pool, NT // 2, 0, 2, step)
                pool.wait_ge(l1_pool, (pair + 1) * (NS + 1))
                settle(pool)
                columns_pool(pool, pair, 0)
                pool.wait_ge(d1_act, (pair + 1) * NT + CREDIT)
                settle(pool)
                pool.memset(PAD[:, XBASE + H:XBASE + H + 1, :], 0.0).then_inc(border, 1)
                sample_and_scan_pool(pool, pair)
                pool.wait_ge(sc_x, (pair + 1) * NT + CREDIT)
                settle(pool)
                pool.memset(PAD[:, BASE - 1:BASE, :], 0.0).then_inc(border, 1)
                pool.wait_ge(border, pair * 2 + 3)
                settle(pool)
                columns_pool(pool, pair, 1)

        @block.scalar
        def _(act):
            credit(act, ln0_ln, ln0_rs, sp_stage, sp_pixt, sp_exp, mh_exp, mh_ptc, o_at, l1_xn, in_xn,
                   d1_act, d2_sq, d2_ln, d2_rs, d2_g, l3_xn)
            credit(act, df_abs, df_hat, df_hi, df_mid, df_wt, sc_abs, sc_exp, sc_ln, sc_da, sc_sq, sc_lv, sc_rs)
            act.wait_ge(load, 16 * 9)
            act.wait_ge(const_dve, 7)
            act.activation(SM[:, 10:11], vc("A_logs"), ACT.Exp).then_inc(const_act, 1)

            def group_norm(n):
                act.wait_ge(gn_pe, n * 2 + 2)
                act.activation(SM[:, 6:7], PSUM[:, 7, 1:2], ACT.Sqrt, bias=GNE[:, 0:1]).then_inc(gn_act, 1)
                act.wait_ge(gn_dve, n * 5 + 5)

            def normed(t, o, s):
                act.activation(o, xch(t), ACT.Identity, bias=NM, scale=RSTD).then_inc(s, 1)

            with act.Fori(0, PAIRS) as pair:
                group_norm(pair * 4)
                with act.Fori(0, NT // 2) as i:
                    T = [pair * NT + i * 2 + k for k in range(2)]
                    for k in range(2):
                        act.wait_ge(ln0_var, after(T[k]))
                        act.wait_ge(ln0_y, reuse(T[k]))
                        act.activation(n_rs[:, k, :], PSUM[:, 4 + k, :], ACT.Ln, bias=GNE[:, 1:2]).then_inc(ln0_ln, 1)
                    for k in range(2):
                        act.wait_ge(ln0_ln, after(T[k]))
                        act.activation(n_rs[:, k, :], n_rs[:, k, :], ACT.Exp, scale=-0.5).then_inc(ln0_rs, 1)
                act.wait_ge(ln0_yb, (pair + 1) * NT + CREDIT)
                settle(act)

                def step(i, b, there):
                    S = [pair * NS + i * 2 + k for k in range(2)]
                    if there(1):
                        for k in range(2):
                            act.wait_ge(sp_tr, reuse(S[k] + 2))
                            act.activation(STG[:, k, :].rearrange("p (b r q) -> p b r q", b=NS, r=8),
                                           PAD[:, bass.ds((i * 2 + k + 2) * 8 + BASE, 8), 1:1 + W].rearrange(
                                               "p r (b q) -> p b r q", q=8), ACT.Identity).then_inc(sp_stage, 1)
                    if there(0):
                        for k in range(2):
                            act.wait_ge(sp_sub, after(S[k]))
                            act.activation(LG[:, k, :, :], LG[:, k, :, :], ACT.Exp, scale=C ** -0.5 / 64).then_inc(sp_exp, 1)
                        for k in range(2):
                            act.wait_ge(sp_tr, after(S[k]))
                            act.wait_ge(sp_fold, reuse(S[k]))
                            act.activation(PIXT[:, k, :].rearrange("p (a b) -> p a b", a=2),
                                           PSUM[:, 2 + 2 * k:4 + 2 * k, :], ACT.Copy).then_inc(sp_pixt, 1)

                in_turn(act, NS // 2, 1, 0, step)
                act.wait_ge(mha_pe, pair * 3 + 1)
                act.activation(QB, PSUM[:, 0, 0:TOK], ACT.Copy)
                act.activation(KB, PSUM[:, 0, TOK:2 * TOK], ACT.Copy)
                act.activation(VB, PSUM[:, 1, 0:2 * P].rearrange("p (a b) -> p a b", a=2), ACT.Copy).then_inc(mha_act, 1)

                def step(i, b, there):
                    N = [pair * NH + i * 2 + k for k in range(2)]
                    if there(-1):
                        for k in range(2):
                            act.wait_ge(mh_pt, after(N[k] - 2))
                            act.wait_ge(mh_pv, reuse(N[k] - 2))
                            act.activation(PTB[:, k, :, :], PSUM[:, 4 + k, :].rearrange("p (a b) -> p a b", a=2),
                                           ACT.Copy).then_inc(mh_ptc, 1)
                    if there(0):
                        for k in range(2):
                            act.wait_ge(mh_nmx, after(N[k]))
                            act.wait_ge(mh_pt, reuse(N[k]))
                            for h in range(2):
                                ins = act.activation(PB[:, k, h, :], PSUM[:, 2 * b + k, h * TOK:(h + 1) * TOK], ACT.Exp,
                                                     bias=MHS[:, k, 2 + h:3 + h], scale=HD ** -0.5,
                                                     accum_out=MHS[:, k, 4 + h:5 + h])
                            ins.then_inc(mh_exp, 1)

                in_turn(act, NH // 2, 0, 1, step)
                act.wait_ge(mha_pe, pair * 3 + 2)
                act.activation(OB, PSUM[:, 7, 0:TOK], ACT.Copy).then_inc(mha_act, 1)
                act.wait_ge(so_dve, pair * 4 + 4)
                settle(act)
                with act.Fori(0, NS // 2) as i:
                    S = [pair * NS + i * 2 + k for k in range(2)]
                    for k in range(2):
                        act.wait_ge(o_tr, after(S[k]))
                        act.wait_ge(o_mm, reuse(S[k]))
                        act.activation(WST[:, k, :].unsqueeze(1), STT[:, bass.ds(i * 2 + k, 1), :], ACT.Identity)
                        act.activation(ATB[:, k, :].rearrange("p (a b) -> p a b", a=2),
                                       PSUM[:, 2 * k:2 * k + 2, :], ACT.Copy).then_inc(o_at, 1)
                group_norm(pair * 4 + 1)
                with act.Fori(0, NT) as t:
                    normed(t, pch(t), l1_xn)
                act.wait_ge(rt_dve, pair * 13 + 5)
                act.activation(RW, RW, ACT.Sigmoid).then_inc(rt_act, 1)
                group_norm(pair * 4 + 2)
                with act.Fori(0, NT // 2) as i:
                    for k in range(2):
                        t = i * 2 + k
                        act.wait_ge(in_mm, reuse(pair * NT + t))
                        normed(t, img(i_xn[:, k, :]), in_xn)
                with act.Fori(0, NT // 2) as i:
                    for k in range(2):
                        t = i * 2 + k
                        act.wait_ge(d1_sum, after(pair * NT + t))
                        act.activation(pch(t, XBASE), img(d_acc[:, k, :]), ACT.Silu, bias=vc("conv2d_b")).then_inc(d1_act, 1)

                def step(i, b, there):
                    T = [pair * NT + i * 2 + k for k in range(2)]
                    if there(-2):
                        for k in range(2):
                            act.wait_ge(d2_var, after(T[k] - 4))
                            act.wait_ge(d2_y, reuse(T[k] - 4))
                            act.activation(d_rs[:, k, :], PSUM[:, 4 + k, :], ACT.Ln, bias=GNE[:, 1:2]).then_inc(d2_ln, 1)
                        for k in range(2):
                            act.wait_ge(d2_ln, after(T[k] - 4))
                            act.activation(d_rs[:, k, :], d_rs[:, k, :], ACT.Exp, scale=-0.5).then_inc(d2_rs, 1)
                    if there(-1):
                        for k in range(2):
                            act.wait_ge(d2_cen, after(T[k] - 2))
                            act.wait_ge(d2_var, reuse(T[k] - 2))
                            act.activation(d_sq[:, k, :], PSUM[:, 2 + k, :], ACT.Square).then_inc(d2_sq, 1)
                    if there(-2):
                        for k in range(2):
                            act.wait_ge(d2_y, after(T[k] - 4))
                            act.activation(d_y[:, k, :], d_y[:, k, :], ACT.Gelu, bias=vc("dw_ln_b")).then_inc(d2_g, 1)

                in_turn(act, NT // 2, 0, 2, step)
                sample_and_scan_act(act, pair)
                group_norm(pair * 4 + 3)
                act.wait_ge(border, pair * 2 + 3)
                settle(act)
                with act.Fori(0, NT) as t:
                    normed(t, pch(t), l3_xn)

        @block.tensor
        def _(pe):
            credit(pe, ln0_cen, ln0_var, sp_lgt, sp_tr, sp_fold, mh_s, mh_pt, mh_pv, o_tr, o_mm, cv_mm, in_mm, d1_mm,
                   d2_mm, d2_cen, d2_var, d2_off)
            credit(pe, df_tr, df_w, df_acc, sc_z, sc_bc, sc_cen, sc_proj, sc_var)
            pe.reg_mov(far_pe_turn, 0)
            pe.reg_mov(far_pe_done, 0)
            pe.wait_ge(load, 16 * 9)
            pe.wait_ge(const_dve, 7)
            pe.matmul(PSUM[:, 0, 0:C], DTS[:, 0:2 * C], DTS[:, 2 * C:3 * C], start=True, stop=True)
            pe.matmul(PSUM[:, 1, 0:1], PLAIN[:, :], vc("out_ln_b"), start=True, stop=True)
            pe.matmul(PSUM[:, 2, 0:P], cs("center"), WOUT[:, :], start=True, stop=True).then_inc(const_pe, 1)
            pe.wait_ge(const_ready, 1)

            def group_norm(n):
                pe.wait_ge(gn_dve, n * 5 + 1)
                pe.matmul(PSUM[:, 7, 0:1], cs("pair"), SM[:, 0:1], start=True, stop=True).then_inc(gn_pe, 1)
                pe.wait_ge(gn_dve, n * 5 + 3)
                pe.matmul(PSUM[:, 7, 1:2], cs("pair"), SM[:, 3:4], start=True, stop=True).then_inc(gn_pe, 1)

            def conv(k, w, t, base=BASE, first=0):
                for j in range(first, NTAP):
                    dy, dx = TAPS[j]
                    ins = pe.matmul(img(PSUM[:, k, :]), w[:, j - first, :], pch(t, base, dy, dx), start=(j == first),
                                    stop=(j == NTAP - 1))
                return ins

            with pe.Fori(0, PAIRS) as pair:
                group_norm(pair * 4)

                def step(i, b, there):
                    T = [pair * NT + i * 2 + k for k in range(2)]
                    if there(0):
                        for k in range(2):
                            pe.wait_ge(ln0_xn, after(T[k]))
                            pe.wait_ge(ln0_cc, reuse(T[k]))
                            pe.matmul(PSUM[:, k, :], cs("center"), n_xn[:, k, :], start=True,
                                      stop=True).then_inc(ln0_cen, 1)
                    if there(-1):
                        for k in range(2):
                            pe.wait_ge(ln0_sq, after(T[k] - 2))
                            pe.wait_ge(ln0_ln, reuse(T[k] - 2))
                            pe.matmul(PSUM[:, 4 + k, :], cs("mean"), n_sq[:, k, :], start=True, stop=True).then_inc(ln0_var, 1)

                in_turn(pe, NT // 2, 0, 1, step)
                pe.wait_ge(tok_dve, (pair + 1) * (NS + 1))
                settle(pe)

                def step(i, b, there):
                    S = [pair * NS + i * 2 + k for k in range(2)]
                    if there(0):
                        for k in range(2):
                            pe.wait_ge(sp_stage, after(S[k]))
                            pe.wait_ge(sp_log, reuse(S[k]))
                            for j in range(8):
                                rhs = STB[:, bass.ds(i * 2 + k, 3), :, 2 * j:2 * j + 4].rearrange("p r s c -> p s r c")
                                ins = pe.matmul(PSUM[:, k, j * 24:(j + 1) * 24].rearrange("p (s r c) -> p s r c", s=2, r=3),
                                                STG[:, k, j * P:(j + 1) * P], rhs, start=True, stop=True)
                            ins.then_inc(sp_lgt, 1)
                            pe.wait_ge(sp_pixt, reuse(S[k]))
                            for j in range(8):
                                ins = pe.transpose(PSUM[:, 2 + 2 * k + j // 4, (j % 4) * P:(j % 4 + 1) * P],
                                                   STG[:, k, j * P:(j + 1) * P], ident)
                            ins.then_inc(sp_tr, 1)
                    if there(-1):
                        for k in range(2):
                            pe.wait_ge(sp_e, after(S[k] - 2))
                            pe.wait_ge(sp_pixt, after(S[k] - 2))
                            pe.wait_ge(sp_acc, reuse(S[k] - 2))
                            for j in range(8):
                                pe.matmul(PSUM[:, 6 + k, 0:P], PIXT[:, k, j * P:(j + 1) * P], EXPD[:, k, j, :],
                                          start=(j == 0), stop=(j == 7))
                            for j in range(8):
                                ins = pe.matmul(PSUM[:, 6 + k, P:2 * P], cs("one"), EXPD[:, k, j, :],
                                                start=(j == 0), stop=(j == 7))
                            ins.then_inc(sp_fold, 1)

                in_turn(pe, NS // 2, 0, 1, step)
                pe.wait_ge(sf_dve, pair * 3 + 3)
                pe.matmul(PSUM[:, 0, 0:TOK], WQ[:, :], SFC, start=True, stop=True)
                pe.matmul(PSUM[:, 0, TOK:2 * TOK], WK[:, :], SFC, start=True, stop=True)
                for h in range(2):
                    ins = pe.matmul(PSUM[:, 1, h * P:(h + 1) * P], SFC[:, h * P:(h + 1) * P], WV[:, :],
                                    start=True, stop=True)
                ins.then_inc(mha_pe, 1)
                pe.wait_ge(mha_act, pair * 2 + 1)
                pe.matmul(PSUM[:, 7, 0:TOK], cs("zero"), SFC, start=True, stop=False, skip_group_check=True)

                def step(i, b, there):
                    N = [pair * NH + i * 2 + k for k in range(2)]
                    if there(1):
                        for k in range(2):
                            pe.wait_ge(mh_qm, after(N[k] + 2))
                            if there(-1):
                                pe.wait_ge(mh_exp, after(N[k] - 2))
                            for h in range(2):
                                ins = pe.matmul(PSUM[:, 2 * (1 - b) + k, h * TOK:(h + 1) * TOK], QM[:, k, h * P:(h + 1) * P], KB,
                                                start=True, stop=True)
                            ins.then_inc(mh_s, 1)
                    if there(-1):
                        for k in range(2):
                            pe.wait_ge(mh_pn, after(N[k] - 2))
                            pe.wait_ge(mh_ptc, reuse(N[k] - 2))
                            for kh in range(2):
                                for qh in range(2):
                                    ins = pe.transpose(PSUM[:, 4 + k, (kh * 2 + qh) * P:(kh * 2 + qh + 1) * P],
                                                       PB[:, k, qh, kh * P:(kh + 1) * P], ident)
                            ins.then_inc(mh_pt, 1)
                        for k in range(2):
                            pe.wait_ge(mh_ptc, after(N[k] - 2))
                            pe.wait_ge(mh_vm, after(N[k] - 2))
                            for kh in range(2):
                                ins = pe.matmul(PSUM[:, 7, 0:TOK], VM[:, k, kh, :], PTB[:, k, kh, :],
                                                start=False, stop=False, skip_group_check=True)
                            ins.then_inc(mh_pv, 1)

                in_turn(pe, NH // 2, 1, 1, step)
                pe.matmul(PSUM[:, 7, 0:TOK], cs("zero"), KB, start=False, stop=True,
                          skip_group_check=True).then_inc(mha_pe, 1)
                pe.wait_ge(mha_act, pair * 2 + 2)
                pe.matmul(PSUM[:, 6, 0:TOK], WPROJ[:, :], OB, start=True, stop=True).then_inc(mha_pe, 1)
                pe.wait_ge(so_dve, pair * 4 + 3)
                for j in range(NS):
                    ins = pe.transpose(PSUM[:, j // 4, (j % 4) * P:(j % 4 + 1) * P], SFB[:, j, :], ident)
                ins.then_inc(so_pe, 1)

                def step(i, b, there):
                    S = [pair * NS + i * 2 + k for k in range(2)]
                    if there(-1):
                        for k in range(2):
                            pe.wait_ge(o_at, after(S[k] - 2))
                            pe.wait_ge(o_x, reuse(S[k] - 2))
                            for j in range(2):
                                ins = pe.matmul(PSUM[:, 4 + 2 * k + j, :], WST[:, k, :], ATB[:, k, j * CH:(j + 1) * CH],
                                                start=True, stop=True)
                            ins.then_inc(o_mm, 1)
                    if there(0):
                        for k in range(2):
                            pe.wait_ge(o_e, after(S[k]))
                            pe.wait_ge(o_at, reuse(S[k]))
                            for j in range(8):
                                ins = pe.transpose(PSUM[:, 2 * k + j // 4, (j % 4) * P:(j % 4 + 1) * P], EXPD[:, k, j, :], ident)
                            ins.then_inc(o_tr, 1)

                in_turn(pe, NS // 2, 0, 1, step)
                group_norm(pair * 4 + 1)
                pe.wait_ge(l1_pool, pair * (NS + 1) + NS)
                for h in range(2):
                    ins = pe.matmul(PSUM[:, 0, h * 32:(h + 1) * 32], POOLED[:, h * P:(h + 1) * P],
                                    WCONV[:, :, :].rearrange("p a b -> p (a b)"), start=True, stop=True)
                ins.then_inc(rt_pe, 1)
                pe.wait_ge(rt_dve, pair * 13 + 2)
                pe.wait_ge(fc_in, pair * 16 + 16)
                for o in range(RED):
                    for h in range(2):
                        ins = pe.matmul(PSUM[0:2, 1, 0:FC], RB[:, h, :].rearrange("p (s o) -> p o s", s=2)[:, o, :],
                                        FCT[:, o, h, :], start=(o + h == 0), stop=(o == RED - 1 and h == 1))
                ins.then_inc(rt_pe, 1)
                pe.wait_ge(rt_dve, pair * 13 + 3)
                for s in range(2):
                    for e in range(EXPERTS):
                        ins = pe.matmul(PSUM[s * C:(s + 1) * C, 2, e:e + 1], FS[0:2, e * C:(e + 1) * C],
                                        ident[0:2, s:s + 1], start=True, stop=True)
                ins.then_inc(rt_pe, 1)
                pe.wait_ge(rt_dve, pair * 13 + 13)
                for j in range(12):
                    ins = pe.transpose(PSUM[:, 3 + j // 4, (j % 4) * P:(j % 4 + 1) * P], WE[:, j, :], ident)
                ins.then_inc(rt_pe, 1)
                pe.wait_ge(l1_pool, (pair + 1) * (NS + 1))
                settle(pe)
                columns_pe(pe, pair, 0, WL1)
                group_norm(pair * 4 + 2)
                with pe.Fori(0, NT // 2) as i:
                    for k in range(2):
                        T = pair * NT + i * 2 + k
                        pe.wait_ge(in_xn, after(T))
                        pe.wait_ge(in_cp, reuse(T))
                        pe.matmul(PSUM[:, k, :], WIN[:, :], i_xn[:, k, :], start=True, stop=True).then_inc(in_mm, 1)
                pe.wait_ge(in_cp, (pair + 1) * NT + CREDIT)
                settle(pe)
                with pe.Fori(0, NT // 2) as i:
                    for k in range(2):
                        t = i * 2 + k
                        pe.wait_ge(d1_sum, reuse(pair * NT + t))
                        conv(k, WDW1, t, first=DW1_VECTOR).then_inc(d1_mm, 1)
                pe.wait_ge(border, pair * 2 + 2)
                settle(pe)

                def step(i, b, there):
                    T = [pair * NT + i * 2 + k for k in range(2)]

                    def taps(k):
                        if there(0):
                            pe.wait_ge(d2_xb, reuse(T[k]))
                            conv(k, WDW2, i * 2 + k, XBASE, first=DW2_VECTOR).then_inc(d2_mm, 1)

                    taps(0)
                    if there(-1):
                        for k in range(2):
                            pe.wait_ge(d2_xb, after(T[k] - 2))
                            pe.wait_ge(d2_y, reuse(T[k] - 2))
                            pe.matmul(PSUM[:, 2 + k, :], cs("center"), d_xb[:, k, :], start=True, stop=True).then_inc(d2_cen, 1)
                    taps(1)
                    if there(-1):
                        for k in range(2):
                            pe.wait_ge(d2_sq, after(T[k] - 2))
                            pe.wait_ge(d2_ln, reuse(T[k] - 2))
                            pe.matmul(PSUM[:, 4 + k, :], cs("mean"), d_sq[:, k, :], start=True, stop=True).then_inc(d2_var, 1)
                    if there(-2):
                        for k in range(2):
                            pe.wait_ge(d2_g, after(T[k] - 4))
                            pe.wait_ge(d2_o, reuse(T[k] - 4))
                            for y in range(ROWS):
                                ins = pe.matmul(PSUM[:, 6 + k, y * 16:(y + 1) * 16], d_y[:, k, y * W:(y + 1) * W],
                                                WOFF[:, :, :, :].rearrange("p a s g -> p (a s g)"), start=True, stop=True)
                            ins.then_inc(d2_off, 1)

                in_turn(pe, NT // 2, 0, 2, step)
                pe.wait_ge(rad_dve, pair * 5 + 1)
                pe.matmul(PSUM[0:1, 0, 0:P], SM[:, 16:17], ident, start=True, stop=True).then_inc(rad_pe, 1)
                pe.wait_ge(rad_dve, pair * 5 + 2)
                pe.matmul(PSUM[:, 0, P:P + 1], cs("one")[0:1, :], SM[0:1, 17:18], start=True, stop=True).then_inc(rad_pe, 1)
                pe.wait_ge(rad_dve, pair * 5 + 5)
                sample_and_scan_pe(pe, pair)
                group_norm(pair * 4 + 3)
                columns_pe(pe, pair, 1, WL3)


def constants():
    import numpy as np
    c = np.zeros((P, NCST), np.float32)
    i = np.arange(P)

    def put(name, a):
        at, n = CST[name]
        c[:, at:at + n] = a

    same = (i[:, None] // C == i[None, :] // C).astype(np.float32)
    put("ident", np.eye(P))
    put("center", np.eye(P) - same / C)
    put("mean", same / C)
    put("pair", (i[:, None] // 2 == i[None, :] // 2) * 0.5)
    put("one", 1.0)
    put("group4", i[:, None] // 4 == i[None, :] // 4)
    put("mask3", same * ((i[:, None] - i[None, :]) % 4 == 0))
    put("headcol", i[:, None] // HD == np.arange(NH)[None, :])
    put("headrow", (np.arange(2 * P - HD)[None, :] // HD == (P - HD) // HD) * np.ones((P, 1)))
    put("shift", np.array([[-1.0, 0.0, 1.0]]))
    put("col", i[:, None])
    put("row", np.arange(H)[None, :])
    return c


def selections():
    import numpy as np
    r, t, c = np.ogrid[0:WROWS, 0:NTAP, 0:P]
    group = c // (C // GROUP)
    near = ((r // SG) % HALF == t % HALF) & (r % SG == group)
    r, t = r[0:ROWS * SG], t[:, 0:ROWS]
    far = (r // SG == t) & (r % SG == group)
    return near.astype(np.float32), far.astype(np.float32)


def kernel(**a):
    import numpy as np
    import concourse.bacc as bacc
    from concourse.bass_utils import run_bass_kernel_spmd

    f = {n: np.asarray(v) for n, v in a.items()}
    g = {n: f[k] for n, k in (
        ("ln_w", "L0_conv_ln_w"), ("ln_b", "L0_conv_ln_b"), ("proj_b", "L0_conv_proj_b"), ("conv2d_b", "L2_conv_conv2d_b"),
        ("dw_b", "L2_conv_dw_b"), ("dw_ln_g", "L2_conv_dw_ln_g"), ("dw_ln_b", "L2_conv_dw_ln_b"), ("dt_b", "L2_conv_dt_b"),
        ("A_logs", "L2_conv_A_logs"), ("Ds", "L2_conv_Ds"), ("out_ln_g", "L2_conv_out_ln_g"),
        ("out_ln_b", "L2_conv_out_ln_b"))}
    g["fc_b"] = f["L1_conv_fc_b"].reshape(EXPERTS, C).T
    g["conv2d_w"] = f["L2_conv_conv2d_w"].reshape(C, 9)
    g["dw_w"] = f["L2_conv_dw_w"].reshape(C, 9)
    g["experts"] = f["L1_conv_w_experts"].reshape(EXPERTS, C, 36).transpose(1, 0, 2)
    g["l3_b"] = f["L3_conv_b"]
    vec = np.concatenate([g[n].reshape(C, VEC[n][1]) for n in VEC], axis=1)
    qkv = f["L0_conv_qkv_w"].reshape(3, C, C)
    m = {"q": qkv[0].T, "k": qkv[1].T, "v": qkv[2].T, "proj": f["L0_conv_proj_w"].T, "in_proj": f["L2_conv_in_proj_w"].T,
         "off": f["L2_conv_off_w"].T, "out_proj": f["L2_conv_out_proj_w"].T, "conv": f["L1_conv_conv_w"].reshape(RED, C).T,
         "x_proj": f["L2_conv_x_proj_w"].T, "w1": f["L3_conv_w1"].T,
         "w3": f["L3_conv_w3"].reshape(C, C, 9).transpose(1, 2, 0).reshape(C, 9 * C)}
    mat = np.concatenate([m[n] for n in MAT], axis=1)
    xp = f["L2_conv_x_proj_w"][:DT_RANK]
    dts = np.concatenate([xp, xp, f["L2_conv_dt_w"].T], axis=1)
    off_b = f["L2_conv_off_b"].reshape(GROUP, 2).T.reshape(2, 1, GROUP)
    off_b = np.broadcast_to(off_b, (ROWS, 2, 2, GROUP)).reshape(-1)
    rows = np.concatenate([f["L1_conv_conv_b"], f["L1_conv_conv_b"], off_b])
    rows = np.broadcast_to(rows[None, :], (P, rows.size))
    fc = f["L1_conv_fc_w"].reshape(FC, RED, 2, P).transpose(3, 1, 2, 0)
    near, far = selections()
    arrays = {"x": f["x"].reshape(BATCH * C, H, W), "vec": vec, "mat": mat, "dts": dts, "rows": rows, "fc": fc, "sel": near, "far_sel": far,
              "cst": constants()}
    arrays = {n: np.ascontiguousarray(v) for n, v in arrays.items()}
    nc = bacc.Bacc("TRN2", target_bir_lowering=False, num_devices=1)
    aps = [nc.dram_tensor(n, v.shape, mybir.dt.from_np(v.dtype), kind="ExternalInput").ap() for n, v in arrays.items()]
    out = nc.dram_tensor("out", (BATCH * C, H, W), F32, kind="ExternalOutput").ap()
    program(nc, *aps, out)
    r = run_bass_kernel_spmd(nc, [arrays], core_ids=[0])
    return r.results[0]["out"].reshape(BATCH, C, H, W)
```
